# Optimizing a Trainium2 kernel written in Bass

```python
import numpy as np
import jax
import jax.numpy as jnp

def _softmax(x, axis=-1):
    return jax.nn.softmax(x, axis=axis)

def _gelu(x):
    return jax.nn.gelu(x, approximate=True)

def _silu(x):
    return jax.nn.silu(x)

def _sigmoid(x):
    return jax.nn.sigmoid(x)

def _layernorm(x, axis=-1, eps=1e-05):
    m = jnp.mean(x, axis=axis, keepdims=True)
    v = jnp.var(x, axis=axis, keepdims=True)
    return (x - m) / jnp.sqrt(v + eps)

def _scatter_add(tgt, idx, src, axis=0):
    return tgt.at[idx].add(src)

def _segment_sum(src, seg, n):
    return jax.ops.segment_sum(src, seg, n)
kernel_name = 'mk_gnn_ffn_d2_gnn_r32_c02d28'

def setup_inputs(seed: int=0):
    np.random.seed(seed)
    _w = jnp.asarray

    def _rec_inputs():
        import jax
        import jax.numpy as jnp
        _gk = jax.random.key(seed)
        x = -0.0002117 + 1 * jax.random.normal(jax.random.fold_in(_gk, 1), (3125, 256), jnp.float32)
        src = jax.random.randint(jax.random.fold_in(_gk, 2), (50000,), 0, 3125, jnp.int32)
        dst = jax.random.randint(jax.random.fold_in(_gk, 3), (50000,), 0, 3125, jnp.int32)
        _o = jnp.argsort(dst, stable=True)
        src = src[_o]
        dst = dst[_o]
        edge_attr_64 = -9.77346e-05 + 0.999888 * jax.random.normal(jax.random.fold_in(_gk, 13), (50000, 64), jnp.float32)
        return (x, src, dst, edge_attr_64)
    x, src, dst, edge_attr_64 = _rec_inputs()

    def _L0_gnn_setup():
        import jax, jax.numpy as jnp
        import numpy as np
        N_NODES = 3125
        N_EDGES = 100000
        CHANNEL = 256
        REDUCTION = 2
        N_GRAPHS = 64
        key = jax.random.key(seed)
        ks = jax.random.split(key, 10)
        C, R = (CHANNEL, CHANNEL // REDUCTION)
        x = jax.random.normal(ks[0], (N_NODES, C), dtype=jnp.float32)
        batch = jnp.sort(jax.random.randint(ks[1], (N_NODES,), 0, N_GRAPHS, dtype=jnp.int32))
        edge_index = jax.random.randint(ks[2], (2, N_EDGES), 0, N_NODES, dtype=jnp.int32)
        w1 = jax.random.normal(ks[3], (C, R), dtype=jnp.float32) / np.sqrt(C)
        b1 = jnp.zeros((R,), dtype=jnp.float32)
        w2 = jax.random.normal(ks[4], (R, C), dtype=jnp.float32) / np.sqrt(R)
        b2 = jnp.zeros((C,), dtype=jnp.float32)
        gcn_w = jax.random.normal(ks[5], (C, 1), dtype=jnp.float32) / np.sqrt(C)
        gcn_b = jnp.zeros((1,), dtype=jnp.float32)
        return {'x': x, 'batch': batch, 'edge_index': edge_index, 'num_graphs': N_GRAPHS, 'w1': w1, 'b1': b1, 'w2': w2, 'b2': b2, 'gcn_w': gcn_w, 'gcn_b': gcn_b}
    _L0_gnn_all = _L0_gnn_setup()
    _L0_gnn_in = {k: v for k, v in _L0_gnn_all.items() if k in ('w1', 'b1', 'w2', 'b2', 'gcn_w', 'gcn_b')}
    del _L0_gnn_all

    def _L0_ffn_setup():
        import jax, jax.numpy as jnp
        import numpy as np
        B, N, D = (16, 128, 256)
        NUM_EXPERTS, TOP_K, HEADS = (4, 2, 4)
        N_EDGES = 32768
        LN_EPS = 1e-05

        def _layernorm(x, g, b):
            mu = x.mean(-1, keepdims=True)
            var = ((x - mu) ** 2).mean(-1, keepdims=True)
            return (x - mu) * jax.lax.rsqrt(var + LN_EPS) * g + b

        def _forward(x, edge_index, W_gat, att_src, att_dst, b_gat, ln_gamma, ln_beta, W1, b1, W2, b2):
            Bc, Nc, Dc = x.shape
            M = Bc * Nc
            x_flat = x.reshape(M, Dc)
            h = (x_flat @ W_gat).reshape(M, HEADS, NUM_EXPERTS)
            loops = jnp.arange(M, dtype=edge_index.dtype)
            src = jnp.concatenate([edge_index[0], loops])
            dst = jnp.concatenate([edge_index[1], loops])
            a_src = (h * att_src).sum(-1)
            a_dst = (h * att_dst).sum(-1)
            e = jax.nn.leaky_relu(a_src[src] + a_dst[dst], negative_slope=0.2)
            e_max = jax.ops.segment_max(e, dst, num_segments=M)
            ee = jnp.exp(e - e_max[dst])
            denom = jax.ops.segment_sum(ee, dst, num_segments=M)
            alpha = ee / (denom[dst] + 1e-16)
            msg = h[src] * alpha[:, :, None]
            agg = jax.ops.segment_sum(msg, dst, num_segments=M).reshape(M, HEADS * NUM_EXPERTS) + b_gat
            scores = _layernorm(agg, ln_gamma, ln_beta).reshape(M, HEADS, NUM_EXPERTS).mean(1)
            scores = scores.reshape(Bc, Nc, NUM_EXPERTS)
            topk_s, topk_i = jax.lax.top_k(scores, TOP_K)
            w = jax.nn.softmax(topk_s, axis=-1)
            out = jnp.zeros_like(x)
            for ei in range(NUM_EXPERTS):
                g = jnp.where(topk_i == ei, w, 0.0).sum(-1)
                hh = jax.nn.gelu(x @ W1[ei] + b1[ei], approximate=False)
                out = out + g[..., None] * (hh @ W2[ei] + b2[ei])
            return out
        key = jax.random.key(seed)
        ks = jax.random.split(key, 8)
        s = 0.05
        return {'x': jax.random.normal(ks[0], (B, N, D), jnp.float32), 'W_gat': jax.random.normal(ks[1], (D, HEADS * NUM_EXPERTS), jnp.float32) * s, 'att_src': jax.random.normal(ks[2], (HEADS, NUM_EXPERTS), jnp.float32) * s, 'att_dst': jax.random.normal(ks[3], (HEADS, NUM_EXPERTS), jnp.float32) * s, 'b_gat': jnp.zeros((HEADS * NUM_EXPERTS,), jnp.float32), 'ln_gamma': jnp.ones((HEADS * NUM_EXPERTS,), jnp.float32), 'ln_beta': jnp.zeros((HEADS * NUM_EXPERTS,), jnp.float32), 'W1': jax.random.normal(ks[4], (NUM_EXPERTS, D, 2 * D), jnp.float32) * s, 'b1': jnp.zeros((NUM_EXPERTS, 2 * D), jnp.float32), 'W2': jax.random.normal(ks[5], (NUM_EXPERTS, 2 * D, D), jnp.float32) * s, 'b2': jnp.zeros((NUM_EXPERTS, D), jnp.float32), 'edge_index': jax.random.randint(ks[6], (2, N_EDGES), 0, B * N, jnp.int32)}
    _L0_ffn_all = _L0_ffn_setup()
    _L0_ffn_in = {k: v for k, v in _L0_ffn_all.items() if k in ('W_gat', 'att_src', 'att_dst', 'b_gat', 'ln_gamma', 'ln_beta', 'W1', 'b1', 'W2', 'b2', 'edge_index')}
    del _L0_ffn_all

    def _L1_gnn_setup():
        import jax, jax.numpy as jnp
        import numpy as np
        ALPHA = 0.2
        key = jax.random.key(seed)
        ks = jax.random.split(key, 6)
        N, E, F_IN, F_OUT, E_DIM = (50000, 25000, 256, 256, 64)
        h = jax.random.normal(ks[0], (N, F_IN), dtype=jnp.float32)
        e_feat = jax.random.normal(ks[1], (E, E_DIM), dtype=jnp.float32)
        W = jax.random.normal(ks[2], (F_OUT, F_IN), dtype=jnp.float32) * (1.0 / np.sqrt(F_IN))
        A = jax.random.normal(ks[3], (1, 2 * F_OUT + E_DIM), dtype=jnp.float32) * 0.05
        src = jax.random.randint(ks[4], (E,), 0, N, dtype=jnp.int32)
        dst = jax.random.randint(ks[5], (E,), 0, N, dtype=jnp.int32)
        return {'h': h, 'e_feat': e_feat, 'W': W, 'A': A, 'src': src, 'dst': dst}
    _L1_gnn_all = _L1_gnn_setup()
    _L1_gnn_in = {k: v for k, v in _L1_gnn_all.items() if k in ('W', 'A')}
    del _L1_gnn_all

    def _L1_ffn_setup():
        import jax, jax.numpy as jnp
        import numpy as np
        E = 8
        K = 2
        D = 256
        H = 512
        DOUT = 256
        EPS = 1e-05
        key = jax.random.key(seed)
        ks = jax.random.split(key, 9)
        s = 0.02
        return {'x': jax.random.normal(ks[0], (4, 256, D), jnp.float32), 'gamma': 1.0 + 0.05 * jax.random.normal(ks[1], (D,), jnp.float32), 'beta': 0.05 * jax.random.normal(ks[2], (D,), jnp.float32), 'Wr': 0.01 * jax.random.normal(ks[3], (D, E), jnp.float32), 'br': jnp.zeros((E,), jnp.float32), 'W1': s * jax.random.normal(ks[4], (E, D, H), jnp.float32), 'b1': s * jax.random.normal(ks[5], (E, H), jnp.float32), 'W2': s * jax.random.normal(ks[6], (E, H, DOUT), jnp.float32), 'b2': s * jax.random.normal(ks[7], (E, DOUT), jnp.float32)}
    _L1_ffn_all = _L1_ffn_setup()
    _L1_ffn_in = {k: v for k, v in _L1_ffn_all.items() if k in ('gamma', 'beta', 'Wr', 'br', 'W1', 'b1', 'W2', 'b2')}
    del _L1_ffn_all
    return {'x': x, 'src': src, 'dst': dst, 'edge_attr_64': edge_attr_64, 'L0_gnn_w1': _L0_gnn_in['w1'], 'L0_gnn_b1': _L0_gnn_in['b1'], 'L0_gnn_w2': _L0_gnn_in['w2'], 'L0_gnn_b2': _L0_gnn_in['b2'], 'L0_gnn_gcn_w': _L0_gnn_in['gcn_w'], 'L0_gnn_gcn_b': _L0_gnn_in['gcn_b'], 'L0_ffn_W_gat': _L0_ffn_in['W_gat'], 'L0_ffn_att_src': _L0_ffn_in['att_src'], 'L0_ffn_att_dst': _L0_ffn_in['att_dst'], 'L0_ffn_b_gat': _L0_ffn_in['b_gat'], 'L0_ffn_ln_gamma': _L0_ffn_in['ln_gamma'], 'L0_ffn_ln_beta': _L0_ffn_in['ln_beta'], 'L0_ffn_W1': _L0_ffn_in['W1'], 'L0_ffn_b1': _L0_ffn_in['b1'], 'L0_ffn_W2': _L0_ffn_in['W2'], 'L0_ffn_b2': _L0_ffn_in['b2'], 'L0_ffn_edge_index': _L0_ffn_in['edge_index'], 'L1_gnn_W': _L1_gnn_in['W'], 'L1_gnn_A': _L1_gnn_in['A'], 'L1_ffn_gamma': _L1_ffn_in['gamma'], 'L1_ffn_beta': _L1_ffn_in['beta'], 'L1_ffn_Wr': _L1_ffn_in['Wr'], 'L1_ffn_br': _L1_ffn_in['br'], 'L1_ffn_W1': _L1_ffn_in['W1'], 'L1_ffn_b1': _L1_ffn_in['b1'], 'L1_ffn_W2': _L1_ffn_in['W2'], 'L1_ffn_b2': _L1_ffn_in['b2']}

def reference(x, src, dst, edge_attr_64, L0_gnn_w1, L0_gnn_b1, L0_gnn_w2, L0_gnn_b2, L0_gnn_gcn_w, L0_gnn_gcn_b, L0_ffn_W_gat, L0_ffn_att_src, L0_ffn_att_dst, L0_ffn_b_gat, L0_ffn_ln_gamma, L0_ffn_ln_beta, L0_ffn_W1, L0_ffn_b1, L0_ffn_W2, L0_ffn_b2, L0_ffn_edge_index, L1_gnn_W, L1_gnn_A, L1_ffn_gamma, L1_ffn_beta, L1_ffn_Wr, L1_ffn_br, L1_ffn_W1, L1_ffn_b1, L1_ffn_W2, L1_ffn_b2):
    import jax
    import jax.numpy as jnp

    def _L0_gnn_ref(x, batch, edge_index, num_graphs, w1, b1, w2, b2, gcn_w, gcn_b):
        import jax, jax.numpy as jnp
        import numpy as np
        N_NODES = 3125
        N_EDGES = 100000
        CHANNEL = 256
        REDUCTION = 2
        N_GRAPHS = 64
        N, C = x.shape
        seg_sum = jax.ops.segment_sum(x, batch, num_segments=num_graphs)
        cnt = jax.ops.segment_sum(jnp.ones((N,), x.dtype), batch, num_segments=num_graphs)
        chn_mean = seg_sum / jnp.maximum(cnt, 1.0)[:, None]
        gate = jax.nn.sigmoid(jax.nn.relu(chn_mean @ w1 + b1) @ w2 + b2)
        chn_se = x * gate[batch]
        h = x @ gcn_w
        loop = jnp.arange(N, dtype=edge_index.dtype)
        src = jnp.concatenate([edge_index[0], loop])
        dst = jnp.concatenate([edge_index[1], loop])
        deg = jax.ops.segment_sum(jnp.ones_like(src, dtype=x.dtype), dst, num_segments=N)
        dis = jnp.where(deg > 0, jax.lax.rsqrt(jnp.maximum(deg, 1e-12)), 0.0)
        msg = h[src] * (dis[src] * dis[dst])[:, None]
        spa = jax.nn.sigmoid(jax.ops.segment_sum(msg, dst, num_segments=N) + gcn_b)
        return x * spa + x + chn_se

    def _L0_ffn_ref(x, W_gat, att_src, att_dst, b_gat, ln_gamma, ln_beta, W1, b1, W2, b2, edge_index):
        import jax, jax.numpy as jnp
        import numpy as np
        B, N, D = (16, 128, 256)
        NUM_EXPERTS, TOP_K, HEADS = (4, 2, 4)
        N_EDGES = 32768
        LN_EPS = 1e-05

        def _layernorm(x, g, b):
            mu = x.mean(-1, keepdims=True)
            var = ((x - mu) ** 2).mean(-1, keepdims=True)
            return (x - mu) * jax.lax.rsqrt(var + LN_EPS) * g + b

        def _forward(x, edge_index, W_gat, att_src, att_dst, b_gat, ln_gamma, ln_beta, W1, b1, W2, b2):
            Bc, Nc, Dc = x.shape
            M = Bc * Nc
            x_flat = x.reshape(M, Dc)
            h = (x_flat @ W_gat).reshape(M, HEADS, NUM_EXPERTS)
            loops = jnp.arange(M, dtype=edge_index.dtype)
            src = jnp.concatenate([edge_index[0], loops])
            dst = jnp.concatenate([edge_index[1], loops])
            a_src = (h * att_src).sum(-1)
            a_dst = (h * att_dst).sum(-1)
            e = jax.nn.leaky_relu(a_src[src] + a_dst[dst], negative_slope=0.2)
            e_max = jax.ops.segment_max(e, dst, num_segments=M)
            ee = jnp.exp(e - e_max[dst])
            denom = jax.ops.segment_sum(ee, dst, num_segments=M)
            alpha = ee / (denom[dst] + 1e-16)
            msg = h[src] * alpha[:, :, None]
            agg = jax.ops.segment_sum(msg, dst, num_segments=M).reshape(M, HEADS * NUM_EXPERTS) + b_gat
            scores = _layernorm(agg, ln_gamma, ln_beta).reshape(M, HEADS, NUM_EXPERTS).mean(1)
            scores = scores.reshape(Bc, Nc, NUM_EXPERTS)
            topk_s, topk_i = jax.lax.top_k(scores, TOP_K)
            w = jax.nn.softmax(topk_s, axis=-1)
            out = jnp.zeros_like(x)
            for ei in range(NUM_EXPERTS):
                g = jnp.where(topk_i == ei, w, 0.0).sum(-1)
                hh = jax.nn.gelu(x @ W1[ei] + b1[ei], approximate=False)
                out = out + g[..., None] * (hh @ W2[ei] + b2[ei])
            return out
        return _forward(x, edge_index, W_gat, att_src, att_dst, b_gat, ln_gamma, ln_beta, W1, b1, W2, b2)

    def _L1_gnn_ref(h, e_feat, W, A, src, dst):
        import jax, jax.numpy as jnp
        import numpy as np
        ALPHA = 0.2
        N = h.shape[0]
        F_OUT = W.shape[0]
        z = h @ W.T
        z_src = z[src]
        z_dst = z[dst]
        a_src, a_dst, a_e = (A[0, :F_OUT], A[0, F_OUT:2 * F_OUT], A[0, 2 * F_OUT:])
        logits = z_src @ a_src + z_dst @ a_dst + e_feat @ a_e
        e = jax.nn.leaky_relu(logits, ALPHA)
        m = jax.ops.segment_max(e, dst, num_segments=N)
        ex = jnp.exp(e - m[dst])
        denom = jax.ops.segment_sum(ex, dst, num_segments=N)
        alpha = ex / denom[dst]
        h_out = jax.ops.segment_sum(alpha[:, None] * z_src, dst, num_segments=N)
        return h_out

    def _L1_ffn_ref(x, gamma, beta, Wr, br, W1, b1, W2, b2):
        import jax, jax.numpy as jnp
        import numpy as np
        E = 8
        K = 2
        D = 256
        H = 512
        DOUT = 256
        EPS = 1e-05
        mu = jnp.mean(x, axis=-1, keepdims=True)
        var = jnp.mean(jnp.square(x - mu), axis=-1, keepdims=True)
        xn = (x - mu) * jax.lax.rsqrt(var + EPS) * gamma + beta
        logits = jnp.einsum('bsd,de->bse', xn, Wr) + br
        top_vals, top_idx = jax.lax.top_k(logits, K)
        w = jax.nn.softmax(top_vals, axis=-1)
        w_full = jnp.einsum('bsk,bske->bse', w, jax.nn.one_hot(top_idx, E, dtype=w.dtype))
        y = jnp.zeros(x.shape[:-1] + (DOUT,), x.dtype)
        for e in range(E):
            h = jax.nn.gelu(jnp.einsum('bsd,dh->bsh', xn, W1[e]) + b1[e], approximate=False)
            y_e = jnp.einsum('bsh,hd->bsd', h, W2[e]) + b2[e]
            y = y + y_e * w_full[..., e, None]
        return y
    edge_index = jnp.stack([src, dst])
    batch0 = jnp.zeros((3125,), jnp.int32)
    x = x + _L0_gnn_ref(_layernorm(x, axis=-1), batch0, edge_index, 64, L0_gnn_w1, L0_gnn_b1, L0_gnn_w2, L0_gnn_b2, L0_gnn_gcn_w, L0_gnn_gcn_b)
    x = x + _L0_ffn_ref(_layernorm(x, axis=-1)[None], L0_ffn_W_gat, L0_ffn_att_src, L0_ffn_att_dst, L0_ffn_b_gat, L0_ffn_ln_gamma, L0_ffn_ln_beta, L0_ffn_W1, L0_ffn_b1, L0_ffn_W2, L0_ffn_b2, L0_ffn_edge_index)[0]
    x = x + _L1_gnn_ref(_layernorm(x, axis=-1), edge_attr_64, L1_gnn_W, L1_gnn_A, src, dst)
    x = x + _L1_ffn_ref(_layernorm(x, axis=-1)[None], L1_ffn_gamma, L1_ffn_beta, L1_ffn_Wr, L1_ffn_br, L1_ffn_W1, L1_ffn_b1, L1_ffn_W2, L1_ffn_b2)[0]
    return x

_drawn_inputs = setup_inputs


def setup_inputs(seed=0):
    import zlib

    import numpy as np

    out = dict(_drawn_inputs(seed))
    spreads = {'L0_gnn_b1': (0.0, 0.8),
     'L0_gnn_b2': (0.0, 0.59),
     'L0_ffn_b_gat': (0.0, 0.1),
     'L0_ffn_ln_gamma': (1.0, 0.2),
     'L0_ffn_ln_beta': (0.0, 0.1),
     'L0_ffn_b1': (0.0, 0.44),
     'L0_ffn_b2': (0.0, 0.335),
     'L1_ffn_br': (0.0, 0.599)}
    factors = {'L0_gnn_w1': 8.0,
     'L0_gnn_w2': 6.54,
     'L0_gnn_gcn_w': 2.675,
     'L0_ffn_att_src': 3.208,
     'L0_ffn_att_dst': 4.496,
     'L1_ffn_gamma': 8.0,
     'L1_ffn_beta': 8.0,
     'L1_ffn_Wr': 3.692,
     'L1_ffn_W1': 3.21,
     'L1_ffn_b1': 24.775,
     'L1_ffn_W2': 3.121,
     'L1_ffn_b2': 25.502}
    for name, (base, spread) in spreads.items():
        noise = np.random.default_rng([zlib.crc32(name.encode()), seed]).standard_normal(out[name].shape)
        drawn = base * np.exp(spread * noise) if base else spread * noise
        out[name] = jnp.asarray(drawn.astype(out[name].dtype))
    for name, factor in factors.items():
        out[name] = (out[name] * factor).astype(out[name].dtype)
    return out
```

```python
from contextlib import ExitStack

import concourse.bass as bass
from concourse import mybir

F32 = mybir.dt.float32
BF16 = mybir.dt.bfloat16
I32 = mybir.dt.int32
ALU = mybir.AluOpType
ACT = mybir.ActivationFunctionType
AX_X = mybir.AxisListType.X

N = 3125
P = 125
J = N // P
D = 256
K = D // 128
E1 = 50000
Q1 = 125
T1 = E1 // Q1
R1 = 100
C1 = T1 // R1
G1 = 20
B1 = T1 // G1
NE0 = 4
HEADS = 4
HX = HEADS * NE0
HF = HX + HEADS
E2 = 32768
Q2 = 128
T2 = E2 // Q2
R2 = 128
C2 = T2 // R2
G2 = 8
B2 = T2 // G2
U2 = 16
NE1 = 8
FE = 64
ZF = D + 3
UW = 8
SW = 4
ITEMS = T1 + J - 1
GW = ITEMS // UW
I4 = -(-ITEMS // 128)
IP = 2 * G1 * -(-ITEMS // (2 * G1))
QE = 25
ROUND = 12582912.0
EPS = 1e-5
BN = 6


class Link:

    def __init__(self, eng, sem):
        self.eng, self.sem, self.n = eng, sem, 0

    def __call__(self, ins, n=1):
        ins.then_inc(self.sem, 1)
        self.n += n
        self.eng.wait_ge(self.sem, self.n)

    def inside(self, ins, per, i, k):
        ins.then_inc(self.sem, 1)
        self.eng.wait_ge(self.sem, i * per + (self.n + k + 1))

    def loop_end(self, steps):
        self.n += steps


def spread(ap, axis, shape):
    return ap.unsqueeze(axis).broadcast_to(shape)


class Memory:
    def __init__(self, nc, ctx, prefix=""):
        self.nc, self.ctx, self.prefix, self.sems = nc, ctx, prefix, []
        ctx.callback(self.clear)

    def clear(self):
        if self.sems:
            self.nc.clear_and_free_semaphores(self.sems)
            self.nc.all_engine_barrier()

    def sb(self, name, shape, dt=F32):
        return self.ctx.enter_context(self.nc.sbuf_tensor(self.prefix + name, shape, dt))

    def ps(self, name, shape, dt=F32):
        return self.ctx.enter_context(self.nc.psum_tensor(self.prefix + name, shape, dt))

    def sem(self, name):
        self.sems.append(self.nc.alloc_semaphore(self.prefix + name))
        return self.sems[-1]


def layernorm_stats(v, link, x, st, small, std, var_ready, n_var, std_ready):
    with v.Fori(0, J) as j:
        v.bn_stats(st[:, bass.ds(j, 1), :].squeeze(1), x[:, bass.ds(j, 1), :].squeeze(1)).then_inc(link.sem, 1)
    link.loop_end(J)
    v.wait_ge(link.sem, link.n)
    mean, rstd, a, b, c = (small[:, i, :] for i in range(5))
    link(v.tensor_tensor(a, st[:, :, 1], st[:, :, 4], ALU.add))
    link(v.tensor_scalar(mean, a, 0.5, None, ALU.mult))
    link(v.tensor_tensor(b, st[:, :, 1], st[:, :, 4], ALU.subtract))
    link(v.tensor_tensor(b, b, b, ALU.mult))
    link(v.tensor_tensor(c, st[:, :, 2], st[:, :, 5], ALU.add))
    link(v.scalar_tensor_tensor(c, b, D / 4.0, c, ALU.mult, ALU.add))
    v.tensor_scalar(a, c, 1.0 / D, EPS, ALU.mult, ALU.add).then_inc(var_ready, 1)
    v.wait_ge(std_ready, n_var)
    link(v.reciprocal(rstd, std))


def layernorm_apply(v, link, xl, x, small):
    with v.Fori(0, J) as j:
        v.tensor_scalar(xl[:, bass.ds(j, 1), :].squeeze(1), x[:, bass.ds(j, 1), :].squeeze(1),
                        small[:, 0, bass.ds(j, 1)], small[:, 1, bass.ds(j, 1)],
                        ALU.subtract, ALU.mult).then_inc(link.sem, 1)
    link.loop_end(J)
    v.wait_ge(link.sem, link.n)


def three_parts(v, link, parts, rest, value):
    link(v.tensor_copy(parts[0], value))
    link(v.tensor_tensor(rest, value, parts[0], ALU.subtract))
    link(v.tensor_copy(parts[1], rest))
    link(v.tensor_tensor(rest, rest, parts[1], ALU.subtract))
    link(v.tensor_copy(parts[2], rest))


def constants(nc, c):
    with ExitStack() as ctx:
        m = Memory(nc, ctx, "constants_")
        row_i = m.sb("row_i", [128, N], I32)
        col_i = m.sb("col_i", [128, 1], I32)
        iotas = m.sem("iotas")
        chain = m.sem("const_chain")
        with nc.Block() as block:

            @block.gpsimd
            def _(pool):
                pool.iota(row_i[:], pattern=[[1, N]], base=0, channel_multiplier=0).then_inc(iotas, 1)
                pool.iota(col_i[:], pattern=[[0, 1]], base=0, channel_multiplier=1).then_inc(iotas, 1)

            @block.vector
            def _(v):
                link = Link(v, chain)
                v.wait_ge(iotas, 2)
                link(v.tensor_copy(c.row[:], row_i[:]))
                link(v.tensor_copy(c.col[:], col_i[:]))
                link(v.tensor_copy(c.row_b[:], c.row[:, 0:128]))
                link(v.tensor_scalar(c.ident[:], c.row[:, 0:128], c.col[:, 0:1], None, ALU.is_equal))
                link(v.memset(c.ones[:], 1.0))
                link(v.memset(c.zeros_b[:], 0.0))


def block_gcn(nc, c, io):
    with ExitStack() as ctx:
        m = Memory(nc, ctx, "gcn_")
        rows_i = m.sb("rows_i", [R1, 2, C1, Q1], I32)
        rows_f = m.sb("rows_f", [R1, 2, C1, Q1])
        rows_hi = m.sb("rows_hi", [R1, 2, C1, Q1])
        rows_lo = m.sb("rows_lo", [R1, 2, C1, Q1])
        rows_hi_b = m.sb("rows_hi_b", [R1, C1, Q1], BF16)
        dst_hi = m.sb("dst_hi", [Q1, T1], BF16)
        lo = m.sb("lo", [Q1, 2, T1], BF16)
        lo_hot = m.sb("lo_hot", [Q1, 2, T1, J], BF16)
        hi_line = m.sb("hi_line", [P, 2, G1 * Q1], BF16)
        hi_hot_t = m.sb("hi_hot_t", [P, 2, G1 * Q1], BF16)
        hi_hot = m.sb("hi_hot", [Q1, 2, G1, P], BF16)
        found = m.sb("found", [Q1, G1, J])
        val = m.sb("val", [Q1, G1])
        val_rest = m.sb("val_rest", [Q1, G1])
        val_b = m.sb("val_b", [Q1, 3, G1], BF16)
        payload = m.sb("payload", [Q1, 2, G1, 3, J], BF16)
        st = m.sb("st", [P, J, BN])
        small = m.sb("small", [P, 5, J])
        std = m.sb("std", [P, 2, J])
        gcn_w = m.sb("gcn_w", [P, D])
        gcn_b = m.sb("gcn_b", [P, 1])
        prod = m.sb("prod", [P, J, D])
        h = m.sb("h", [P, J])
        deg = m.sb("deg", [P, J])
        dis = m.sb("dis", [P, J])
        hd = m.sb("hd", [P, J])
        hd_rest = m.sb("hd_rest", [P, J])
        hd_b = m.sb("hd_b", [P, 3, J], BF16)
        sums = m.sb("sums", [P, 3, J])
        spa = m.sb("spa", [P, J])
        w1 = m.sb("w1", [128, K, 128])
        w2 = m.sb("w2", [128, D])
        b1 = m.sb("b1", [128, 1])
        b2 = m.sb("b2", [1, D])
        mean = m.sb("mean", [128, K])
        hidden = m.sb("hidden", [128, 1])
        hidden_row = m.sb("hidden_row", [128, P])
        gate1 = m.sb("gate1", [P, D])

        turned = [m.ps(f"turned{i}", [Q1, T1]) for i in range(3)]
        looked = [m.ps(f"looked{i}", [Q1, G1 * J]) for i in range(2)]
        ps_deg = m.ps("ps_deg", [P, J])
        ps_sum = m.ps("ps_sum", [P, 3 * J])
        ps_gate = m.ps("ps_gate", [128, D + 8])

        x_in, edges_in, gcn_in, gate_in = (m.sem(n) for n in ("x_in", "edges_in", "gcn_in", "gate_in"))
        hi_ready, hi_out = m.sem("hi_ready"), m.sem("hi_out")
        line_in = [m.sem(f"line_in{i}") for i in range(2)]
        ids_ready, ids_turned = m.sem("ids_ready"), m.sem("ids_turned")
        var_ready, std_ready = m.sem("var_ready"), m.sem("std_ready")
        xl_ready, mean_sum, mean_ready = m.sem("xl_ready"), m.sem("mean_sum"), m.sem("mean_ready")
        hidden_sum, hidden_ready = m.sem("hidden_sum"), m.sem("hidden_ready")
        gate_sum, gate_ready = m.sem("gate_sum"), m.sem("gate_ready")
        hot_ready, hot_free = m.sem("hot_ready"), m.sem("hot_free")
        deg_summed = m.sem("deg_summed")
        hot_t_ready, looked_up, looked_free = m.sem("hot_t_ready"), m.sem("looked_up"), m.sem("looked_free")
        payload_ready, all_summed = m.sem("payload_ready"), m.sem("all_summed")
        spa_in, spa_ready = m.sem("spa_in"), m.sem("spa_ready")
        chain = m.sem("gcn_chain")
        with nc.Block() as block:

            @block.sync
            def _(sp):
                sp.dma_start(rows_i[:, 0, :, :], io["src"].rearrange("(c r q) -> r c q", r=R1, q=Q1)).then_inc(edges_in, 16)
                sp.dma_start(rows_i[:, 1, :, :], io["dst"].rearrange("(c r q) -> r c q", r=R1, q=Q1)).then_inc(edges_in, 16)
                sp.dma_start(c.x[:], io["x"].rearrange("(p j) d -> p j d", j=J)).then_inc(x_in, 16)
                sp.dma_start(gcn_w[:], io["L0_gnn_gcn_w"].rearrange("d o -> o d").broadcast_to([P, D])).then_inc(gcn_in, 16)
                sp.dma_start(gcn_b[:], io["L0_gnn_gcn_b"].unsqueeze(0).broadcast_to([P, 1])).then_inc(gcn_in, 16)
                sp.dma_start(w1[:], io["L0_gnn_w1"].rearrange("(k p) r -> p k r", p=128)).then_inc(gate_in, 16)
                sp.dma_start(w2[:], io["L0_gnn_w2"]).then_inc(gate_in, 16)
                sp.dma_start(b1[:], io["L0_gnn_b1"].unsqueeze(1)).then_inc(gate_in, 16)
                sp.dma_start(b2[:], io["L0_gnn_b2"].unsqueeze(0)).then_inc(gate_in, 16)
                sp.wait_ge(hi_ready, 1)
                sp.dma_start(c.hi_line_dram.rearrange("(c r q) -> r c q", r=R1, q=Q1), rows_hi_b[:]).then_inc(hi_out, 16)
                sp.wait_ge(hi_out, 16)
                lines = c.hi_line_dram.rearrange("(b e) -> b e", e=G1 * Q1)
                for s in range(2):
                    sp.dma_start(hi_line[:, s, :], lines[s:s + 1, :].broadcast_to([P, G1 * Q1])).then_inc(line_in[s], 16)
                with sp.Fori(1, B1 // 2) as b:
                    for s in range(2):
                        sp.wait_ge(hot_t_ready, b * 2 + (s - 1))
                        sp.dma_start(hi_line[:, s, :], lines[bass.ds(b * 2 + s, 1), :].broadcast_to([P, G1 * Q1])).then_inc(line_in[s], 16)

            @block.scalar
            def _(act):
                act.wait_ge(var_ready, 1)
                act.activation(std[:, 0, :], small[:, 2, :], ACT.Sqrt).then_inc(std_ready, 1)
                act.wait_ge(var_ready, 2)
                act.activation(std[:, 1, :], deg[:], ACT.Sqrt).then_inc(std_ready, 1)
                act.wait_ge(gate_sum, 1)
                act.activation(gate1[:], ps_gate[0:P, 0:D], ACT.Sigmoid).then_inc(gate_ready, 1)
                act.wait_ge(spa_in, 1)
                act.activation(spa[:], hd_rest[:], ACT.Sigmoid).then_inc(spa_ready, 1)

            @block.tensor
            def _(pe):
                pe.wait_ge(ids_ready, 1)
                for i, rows in enumerate((rows_hi[:, 1, :, :], rows_lo[:, 0, :, :], rows_lo[:, 1, :, :])):
                    for b in range(C1):
                        ins = pe.transpose(turned[i][:, b * R1:(b + 1) * R1], rows[:, b, :], c.ident[0:R1, 0:R1])
                ins.then_inc(ids_turned, 1)
                pe.wait_ge(xl_ready, 1)
                for k in range(K):
                    for j in range(J):
                        ins = pe.matmul(ps_gate[:, D + k:D + k + 1], c.xl[:, j, k * 128:(k + 1) * 128],
                                        c.ones[0:P, 0:1], start=(j == 0), stop=(j == J - 1))
                ins.then_inc(mean_sum, 1)
                pe.matmul(ps_deg[:], c.zeros_b[0:Q1, 0:P], c.zeros_b[0:Q1, 0:J], start=True, stop=False, skip_group_check=True)
                with pe.Fori(0, B1 // 2) as b:
                    for s in range(2):
                        pe.wait_ge(hot_ready, b * 2 + (s + 1))
                        for g in range(G1):
                            ins = pe.matmul(ps_deg[:], hi_hot[:, s, g, :],
                                            lo_hot[:, 1, bass.ds(b * (2 * G1) + (s * G1 + g), 1), :].squeeze(1),
                                            start=False, stop=False, skip_group_check=True)
                        ins.then_inc(hot_free, 1)
                pe.matmul(ps_deg[:], c.zeros_b[0:Q1, 0:P], c.zeros_b[0:Q1, 0:J], start=False, stop=True,
                          skip_group_check=True).then_inc(deg_summed, 1)
                pe.wait_ge(mean_ready, 1)
                pe.wait_ge(gate_in, 64)
                for k in range(K):
                    ins = pe.matmul(ps_gate[:, D + 4:D + 5], w1[:, k, :], mean[:, k:k + 1], start=(k == 0), stop=(k == K - 1))
                ins.then_inc(hidden_sum, 1)
                pe.wait_ge(hidden_ready, 1)
                pe.matmul(ps_gate[0:P, 0:D], hidden_row[:], w2[:], start=True, stop=False)
                pe.matmul(ps_gate[0:P, 0:D], c.ones[0:1, 0:P], b2[:], start=False, stop=True).then_inc(gate_sum, 1)
                pe.matmul(ps_sum[:], c.zeros_b[0:Q1, 0:P], c.zeros_b[0:Q1, 0:3 * J], start=True, stop=False, skip_group_check=True)
                with pe.Fori(0, B1 // 2) as b:
                    for s in range(2):
                        pe.wait_ge(hot_t_ready, b * 2 + (s + 1))
                        pe.wait_ge(looked_free, b * 2 + (s + 1))
                        for g in range(G1):
                            for i in range(3):
                                ins = pe.matmul(looked[s][:, g * J:(g + 1) * J], hi_hot_t[:, s, g * Q1:(g + 1) * Q1],
                                                hd_b[:, i, :], start=(i == 0), stop=(i == 2))
                        ins.then_inc(looked_up, 1)
                        pe.wait_ge(payload_ready, b * 2 + (s + 1))
                        for g in range(G1):
                            ins = pe.matmul(ps_sum[:], hi_hot[:, s, g, :], payload[:, s, g, :, :],
                                            start=False, stop=False, skip_group_check=True)
                        ins.then_inc(hot_free, 1)
                pe.matmul(ps_sum[:], c.zeros_b[0:Q1, 0:P], c.zeros_b[0:Q1, 0:3 * J], start=False, stop=True,
                          skip_group_check=True).then_inc(all_summed, 1)

            @block.vector
            def _(v):
                link = Link(v, chain)
                v.sem_inc(hot_free, 2)
                v.sem_inc(looked_free, 2)
                v.wait_ge(edges_in, 32)
                link(v.tensor_copy(rows_f[:], rows_i[:]))
                link(v.tensor_scalar(rows_hi[:], rows_f[:], -float(J // 2), 1.0 / J, ALU.add, ALU.mult))
                link(v.tensor_scalar(rows_hi[:], rows_hi[:], ROUND, -ROUND, ALU.add, ALU.add))
                v.tensor_copy(rows_hi_b[:], rows_hi[:, 0, :, :]).then_inc(hi_ready, 1)
                v.scalar_tensor_tensor(rows_lo[:], rows_hi[:], -float(J), rows_f[:], ALU.mult, ALU.add).then_inc(ids_ready, 1)
                v.wait_ge(x_in, 16)
                layernorm_stats(v, link, c.x, st, small, std[:, 0, :], var_ready, 1, std_ready)
                layernorm_apply(v, link, c.xl, c.x, small)
                v.sem_inc(xl_ready, 1)
                v.wait_ge(ids_turned, 1)
                link(v.tensor_copy(dst_hi[:], turned[0][:]))
                link(v.tensor_copy(lo[:, 0, :], turned[1][:]))
                link(v.tensor_copy(lo[:, 1, :], turned[2][:]))
                for i in range(2):
                    link(v.tensor_tensor(lo_hot[:, i, :, :], spread(lo[:, i, :], 2, [Q1, T1, J]),
                                         spread(c.row_b[0:Q1, 0:J], 1, [Q1, T1, J]), ALU.is_equal))

                def hot(b, s):
                    v.tensor_tensor(hi_hot[:, s, :, :], spread(dst_hi[:, bass.ds(b * (2 * G1) + s * G1, G1)], 2, [Q1, G1, P]),
                                    spread(c.row_b[0:Q1, 0:P], 1, [Q1, G1, P]), ALU.is_equal).then_inc(hot_ready, 1)

                with v.Fori(0, B1 // 2) as b:
                    for s in range(2):
                        v.wait_ge(hot_free, b * 2 + (s + 1))
                        hot(b, s)
                v.wait_ge(gcn_in, 32)
                link(v.tensor_tensor(prod[:], c.xl[:], spread(gcn_w[:], 1, [P, J, D]), ALU.mult))
                link(v.tensor_reduce(h[:], prod[:], AX_X, ALU.add))
                v.wait_ge(mean_sum, 1)
                v.tensor_scalar(mean[:], ps_gate[:, D:D + K], 1.0 / N, None, ALU.mult).then_inc(mean_ready, 1)
                v.wait_ge(deg_summed, 1)
                link(v.tensor_copy(c.deg[:], ps_deg[:]))
                v.tensor_scalar(deg[:], ps_deg[:], 1.0, None, ALU.add).then_inc(var_ready, 1)
                v.wait_ge(std_ready, 2)
                link(v.reciprocal(dis[:], std[:, 1, :]))
                link(v.tensor_tensor(hd[:], h[:], dis[:], ALU.mult))
                three_parts(v, link, [hd_b[:, i, :] for i in range(3)], hd_rest[:], hd[:])
                v.wait_ge(hidden_sum, 1)
                link(v.tensor_scalar(hidden[:], ps_gate[:, D + 4:D + 5], b1[:], 0.0, ALU.add, ALU.max))
                v.tensor_copy(hidden_row[:], hidden[:, 0:1].broadcast_to([128, P])).then_inc(hidden_ready, 1)
                with v.Fori(0, B1 // 2) as b:
                    for s in range(2):
                        i = b * 2 + s
                        v.wait_ge(line_in[s], b * 16 + 16)
                        v.tensor_scalar(hi_hot_t[:, s, :], hi_line[:, s, :], c.col[0:P, 0:1], None,
                                        ALU.is_equal).then_inc(hot_t_ready, 1)
                        v.wait_ge(hot_free, i + (B1 + 1))
                        hot(b, s)
                        v.wait_ge(looked_up, i + 1)
                        v.tensor_tensor(found[:], looked[s].rearrange("q (g j) -> q g j", j=J),
                                        lo_hot[:, 0, bass.ds(b * (2 * G1) + s * G1, G1), :], ALU.mult).then_inc(looked_free, 1)
                        v.wait_ge(looked_free, i + 3)
                        link.inside(v.tensor_reduce(val[:], found[:], AX_X, ALU.add), 12, b, 6 * s)
                        link.inside(v.tensor_copy(val_b[:, 0, :], val[:]), 12, b, 6 * s + 1)
                        link.inside(v.tensor_tensor(val_rest[:], val[:], val_b[:, 0, :], ALU.subtract), 12, b, 6 * s + 2)
                        link.inside(v.tensor_copy(val_b[:, 1, :], val_rest[:]), 12, b, 6 * s + 3)
                        link.inside(v.tensor_tensor(val_rest[:], val_rest[:], val_b[:, 1, :], ALU.subtract), 12, b, 6 * s + 4)
                        link.inside(v.tensor_copy(val_b[:, 2, :], val_rest[:]), 12, b, 6 * s + 5)
                        for part in range(3):
                            ins = v.tensor_tensor(payload[:, s, :, part, :], lo_hot[:, 1, bass.ds(b * (2 * G1) + s * G1, G1), :],
                                                  spread(val_b[:, part, :], 2, [Q1, G1, J]), ALU.mult)
                        ins.then_inc(payload_ready, 1)
                link.loop_end(6 * B1)
                v.wait_ge(all_summed, 1)
                link(v.tensor_copy(sums[:], ps_sum.rearrange("p (i j) -> p i j", j=J)))
                link(v.tensor_tensor(sums[:, 1, :], sums[:, 1, :], sums[:, 2, :], ALU.add))
                link(v.tensor_tensor(sums[:, 0, :], sums[:, 0, :], sums[:, 1, :], ALU.add))
                link(v.tensor_tensor(sums[:, 0, :], sums[:, 0, :], hd[:], ALU.add))
                link(v.tensor_tensor(sums[:, 0, :], sums[:, 0, :], dis[:], ALU.mult))
                v.tensor_scalar(hd_rest[:], sums[:, 0, :], gcn_b[:], None, ALU.add).then_inc(spa_in, 1)
                v.wait_ge(gate_ready, 1)
                link(v.tensor_scalar(gate1[:], gate1[:], 1.0, None, ALU.add))
                v.wait_ge(spa_ready, 1)
                with v.Fori(0, J) as j:
                    v.scalar_tensor_tensor(prod[:, bass.ds(j, 1), :].squeeze(1), gate1[:], spa[:, bass.ds(j, 1)],
                                           c.xl[:, bass.ds(j, 1), :].squeeze(1), ALU.add, ALU.mult).then_inc(chain, 1)
                link.loop_end(J)
                v.wait_ge(chain, link.n)
                link(v.tensor_tensor(c.x[:], c.x[:], prod[:], ALU.add))


def transpose_nodes(pe, c, ps, xl_waited, ps_free, turned, first):
    i = 0
    for k in range(K):
        for j0 in range(0, J, 4):
            js = range(j0, min(j0 + 4, J))
            if i >= 2:
                pe.wait_ge(ps_free, first + i - 1)
            for j in js:
                ins = pe.transpose(ps[i % 2][:, (j - j0) * P:(j - j0 + 1) * P], c.xl[:, j, k * 128:(k + 1) * 128],
                                   c.ident[0:P, 0:P])
            ins.then_inc(turned, 1)
            i += 1


def copy_turned(eng, copy, c, ps, ps_free, turned, first):
    i = 0
    for k in range(K):
        for j0 in range(0, J, 4):
            n = min(4, J - j0) * P
            eng.wait_ge(turned, first + i + 1)
            copy(c.xt[:, k, j0 * P:j0 * P + n], ps[i % 2][:, 0:n]).then_inc(ps_free, 1)
            i += 1


TURNS = K * ((J + 3) // 4)


def top2_gates(v, link, s, gates, t, big, tri, exp_in, exp_out, n_exp):
    e = s.shape[2]
    s_i = spread(s, 3, [P, J, e, e])
    s_k = spread(s, 2, [P, J, e, e])
    rank, top, rsum = t[:, :, :, 0], t[:, :, 0, 1], t[:, :, 0, 2]
    link(v.tensor_tensor(big, s_k, s_i, ALU.is_equal))
    link(v.tensor_tensor(big.rearrange("p j i k -> p j (i k)"), big.rearrange("p j i k -> p j (i k)"),
                         spread(tri, 1, [P, J, e * e]), ALU.mult))
    link(v.tensor_reduce(rank, big, AX_X, ALU.add))
    link(v.tensor_tensor(big, s_k, s_i, ALU.is_gt))
    link(v.tensor_reduce(t[:, :, :, 3], big, AX_X, ALU.add))
    link(v.tensor_tensor(rank, rank, t[:, :, :, 3], ALU.add))
    link(v.tensor_scalar(rank, rank, 2.0, None, ALU.is_lt))
    link(v.tensor_reduce(top, s, AX_X, ALU.max))
    v.tensor_tensor(exp_in, s, spread(top, 2, [P, J, e]), ALU.subtract).then_inc(n_exp[0], 1)
    v.wait_ge(n_exp[1], n_exp[2])
    link(v.tensor_tensor(exp_out, exp_out, rank, ALU.mult))
    link(v.tensor_reduce(rsum, exp_out, AX_X, ALU.add))
    link(v.reciprocal(rsum, rsum))
    link(v.tensor_tensor(gates.rearrange("p e j -> p j e"), exp_out, spread(rsum, 2, [P, J, e]), ALU.mult))


def block_gat_tables(nc, c, io):
    with ExitStack() as ctx:
        m = Memory(nc, ctx, "gat_tables_")
        st = m.sb("st", [P, J, BN])
        small = m.sb("small", [P, 5, J])
        std = m.sb("std", [P, J])
        w_gat = m.sb("w_gat", [128, K, HX])
        att = m.sb("att", [P, 2, HX])
        prod = m.sb("prod", [P, J, HX])
        ps_turn = [m.ps(f"ps_turn{i}", [128, 512]) for i in range(2)]
        ps_h = m.ps("ps_h", [P, J * HX])
        w_in, var_ready, std_ready = m.sem("w_in"), m.sem("var_ready"), m.sem("std_ready")
        xl_ready, turned, turn_free = m.sem("xl_ready"), m.sem("turned"), m.sem("turn_free")
        h_summed, table_ready, table_out = m.sem("h_summed"), m.sem("table_ready"), m.sem("table_out")
        lowest, most_in, most_out = m.sem("lowest"), m.sem("most_in"), m.sem("most_out")
        chain = m.sem("tab_chain")
        with nc.Block() as block:

            @block.sync
            def _(sp):
                sp.dma_start(w_gat[:], io["L0_ffn_W_gat"].rearrange("(k p) r -> p k r", p=128)).then_inc(w_in, 16)
                for i, name in enumerate(("L0_ffn_att_src", "L0_ffn_att_dst")):
                    sp.dma_start(att[:, i, :], io[name].rearrange("h e -> (h e)").unsqueeze(0).broadcast_to([P, HX])).then_inc(w_in, 16)
                sp.wait_ge(table_ready, 1)
                sp.dma_start(c.h_table.rearrange("(p j) f -> p j f", j=J), c.h[:]).then_inc(table_out, 16)
                sp.wait_ge(table_out, 16)

            @block.gpsimd
            def _(pool):
                pool.wait_ge(most_in, 1)
                pool.partition_all_reduce(c.most[:], c.most_of[:], 128, bass.bass_isa.ReduceOp.max).then_inc(most_out, 1)

            @block.scalar
            def _(act):
                act.wait_ge(var_ready, 1)
                act.activation(std[:], small[:, 2, :], ACT.Sqrt).then_inc(std_ready, 1)
                copy_turned(act, act.copy, c, ps_turn, turn_free, turned, 0)

            @block.tensor
            def _(pe):
                pe.wait_ge(xl_ready, 1)
                transpose_nodes(pe, c, ps_turn, None, turn_free, turned, 0)
                pe.wait_ge(turn_free, TURNS)
                pe.wait_ge(w_in, 48)
                for j in range(J):
                    for k in range(K):
                        ins = pe.matmul(ps_h[:, j * HX:(j + 1) * HX], c.xt[:, k, j * P:(j + 1) * P], w_gat[:, k, :],
                                        start=(k == 0), stop=(k == K - 1))
                ins.then_inc(h_summed, 1)

            @block.vector
            def _(v):
                link = Link(v, chain)
                layernorm_stats(v, link, c.x, st, small, std[:], var_ready, 1, std_ready)
                layernorm_apply(v, link, c.xl, c.x, small)
                v.sem_inc(xl_ready, 1)
                link(v.memset(c.most_of[:], -3e38))
                v.wait_ge(h_summed, 1)
                v.wait_ge(w_in, 48)
                link(v.tensor_copy(c.h[:, :, 0:HX], ps_h.rearrange("p (j r) -> p j r", r=HX)))
                for i, out in enumerate((c.h[:, :, HX:HF], c.a_dst[:])):
                    link(v.tensor_tensor(prod[:], c.h[:, :, 0:HX], spread(att[:, i, :], 1, [P, J, HX]), ALU.mult))
                    link(v.tensor_reduce(out, prod.rearrange("p j (h e) -> p j h e", e=NE0), AX_X, ALU.add))
                v.sem_inc(table_ready, 1)
                link(v.tensor_reduce(c.most_of[0:P, :], c.h[:, :, HX:HF].rearrange("p j h -> p h j"), AX_X, ALU.max))
                v.sem_inc(most_in, 1)
                v.wait_ge(most_out, 1)


def block_gat_edges(nc, c, io):
    with ExitStack() as ctx:
        m = Memory(nc, ctx, "gat_edges_")
        rows_i = m.sb("rows_i", [R2, 2, C2, Q2], I32)
        rows_f = m.sb("rows_f", [R2, 2, C2, Q2])
        rows_hi = m.sb("rows_hi", [R2, C2, Q2])
        rows_lo = m.sb("rows_lo", [R2, C2, Q2])
        rows_hi_b = m.sb("rows_hi_b", [R2, C2, Q2], BF16)
        dst_hi = m.sb("dst_hi", [Q2, T2])
        dst_lo = m.sb("dst_lo", [Q2, T2], BF16)
        src_i = m.sb("src_i", [Q2, T2], I32)
        lo_hot = m.sb("lo_hot", [Q2, T2, J], BF16)
        hi_line = m.sb("hi_line", [P, 2, G2 * Q2], BF16)
        hi_hot_t = m.sb("hi_hot_t", [P, 2, G2 * Q2], BF16)
        hi_hot = m.sb("hi_hot", [Q2, 2, G2, P])
        payload = m.sb("payload", [Q2, 2, G2, J * HF])
        zero_i = m.sb("zero_i", [128, U2], I32)
        spare_i = m.sb("spare_i", [128, 1], I32)
        stage = m.sb("stage", [Q2, 2, U2], I32)
        spare = m.sb("spare", [Q2, 2])
        ring = m.sb("ring", [Q2, 2, U2, HF])
        rows = c.xl_all.rearrange("p j d -> p (j d)")[:, 0:T2 * HF].rearrange("q (t f) -> q t f", f=HF)
        a_dst_e = m.sb("a_dst_e", [Q2, T2, HEADS])
        ex = m.sb("ex", [Q2, T2, HEADS])
        cap = m.sb("cap", [Q2, T2, HEADS])
        found = m.sb("found", [Q2, G2, J, HEADS])
        a_rest = m.sb("a_rest", [P, J, HEADS])
        a_b = m.sb("a_b", [P, 3, J, HEADS], BF16)
        own = m.sb("own", [P, 3, J, HEADS])
        agg = m.sb("agg", [P, J, HF])
        params = m.sb("params", [P, 3, HX])
        sq = m.sb("sq", [P, J, HX])
        stat = m.sb("stat", [P, 4, J])
        score = m.sb("score", [P, J, NE0])
        t = m.sb("gate_t", [P, J, NE0, 4])
        big = m.sb("gate_big", [P, J, NE0, NE0])
        tri = m.sb("tri", [P, NE0 * NE0])
        exp_in = m.sb("exp_in", [P, J, NE0])
        exp_out = m.sb("exp_out", [P, J, NE0])
        turned = [m.ps(f"turned{i}", [Q2, T2]) for i in range(2)]
        looked = [m.ps(f"looked{i}", [Q2, 2, 512]) for i in range(2)]
        ps_sum = m.ps("ps_sum", [P, 512])
        names = ("ids_in", "par_in", "hi_ready", "hi_out", "rows_ready", "ids_turned", "src_ready", "staged", "ring_free",
                 "hot_t_ready", "looked_up", "looked_free", "rows_in", "exp_ready", "exp_done", "self_in",
                 "self_done", "payload_ready", "payload_free", "all_summed", "var_ready", "std_ready", "gate_in", "gate_out",
                 "edge_chain", "found_done")
        s_ = {n: m.sem("ge_" + n) for n in names}
        line_in = [m.sem(f"ge_line_in{i}") for i in range(2)]
        gathered = [m.sem(f"ge_gathered{i}") for i in range(2)]
        with nc.Block() as block:

            @block.sync
            def _(sp):
                for i in range(2):
                    sp.dma_start(rows_i[:, i, :, :], io["L0_ffn_edge_index"][i].rearrange("(c r q) -> r c q", r=R2, q=Q2)).then_inc(s_["ids_in"], 16)
                for i, name in enumerate(("L0_ffn_b_gat", "L0_ffn_ln_gamma", "L0_ffn_ln_beta")):
                    sp.dma_start(params[:, i, :], io[name].unsqueeze(0).broadcast_to([P, HX])).then_inc(s_["par_in"], 16)
                sp.wait_ge(s_["hi_ready"], 1)
                sp.dma_start(c.hi_line_dram2.rearrange("(c r q) -> r c q", r=R2, q=Q2), rows_hi_b[:]).then_inc(s_["hi_out"], 16)
                sp.wait_ge(s_["hi_out"], 16)
                lines = c.hi_line_dram2.rearrange("(b e) -> b e", e=G2 * Q2)
                for s in range(2):
                    sp.dma_start(hi_line[:, s, :], lines[s:s + 1, :].broadcast_to([P, G2 * Q2])).then_inc(line_in[s], 16)
                with sp.Fori(1, B2 // 2) as b:
                    for s in range(2):
                        sp.wait_ge(s_["hot_t_ready"], b * 2 + (s - 1))
                        sp.dma_start(hi_line[:, s, :], lines[bass.ds(b * 2 + s, 1), :].broadcast_to([P, G2 * Q2])).then_inc(line_in[s], 16)

            @block.gpsimd
            def _(pool):
                pool.memset(zero_i[:], 0).then_inc(s_["staged"], 1)
                pool.sem_inc(s_["ring_free"], 2)
                pool.wait_ge(s_["src_ready"], 1)
                pool.wait_ge(s_["staged"], 1)
                with pool.Fori(0, T2 // (2 * U2)) as b:
                    for s in range(2):
                        ids = src_i[:, bass.ds(b * (2 * U2) + s * U2, U2)]
                        pool.wait_ge(s_["ring_free"], b * 2 + (s + 1))
                        pool.tensor_tensor(stage[:, s, :], ids, zero_i[:], ALU.add).then_inc(s_["staged"], 1)
                        pool.wait_ge(s_["staged"], b * 2 + (s + 2))
                        pool.tensor_tensor(spare_i[:], zero_i[:, 0:1], zero_i[:, 1:2], ALU.add)
                        for u in range(U2):
                            pool.indirect_dma_start(ring[:, s, u, :], None, c.h_table,
                                                    bass.IndirectOffsetOnAxis(ap=stage[:, s, u:u + 1], axis=0)).then_inc(gathered[s], 16)

            @block.scalar
            def _(act):
                with act.Fori(0, T2 // (2 * U2)) as b:
                    for s in range(2):
                        act.wait_ge(gathered[s], b * (16 * U2) + 16 * U2)
                        act.copy(spare[:, s:s + 1], ring[:, s, 0, 0:1])
                        act.copy(rows[:, bass.ds(b * (2 * U2) + s * U2, U2), :], ring[:, s, :, :]).then_inc(s_["ring_free"], 1)
                act.wait_ge(s_["ring_free"], 2 + T2 // U2)
                act.sem_inc(s_["rows_in"], 1)
                act.wait_ge(s_["self_in"], 1)
                act.activation(own[:, 2, :, :], own[:, 1, :, :], ACT.Exp).then_inc(s_["self_done"], 1)
                act.wait_ge(s_["exp_ready"], 1)
                act.activation(ex[:], cap[:], ACT.Exp).then_inc(s_["exp_done"], 1)
                act.wait_ge(s_["var_ready"], 1)
                act.activation(stat[:, 2, :], stat[:, 1, :], ACT.Sqrt).then_inc(s_["std_ready"], 1)
                act.wait_ge(s_["gate_in"], 1)
                act.activation(exp_out[:], exp_in[:], ACT.Exp).then_inc(s_["gate_out"], 1)

            @block.tensor
            def _(pe):
                pe.wait_ge(s_["rows_ready"], 1)
                for b in range(C2):
                    pe.transpose(turned[0][:, b * R2:(b + 1) * R2], rows_f[:, 0, b, :], c.ident[:])
                for b in range(C2):
                    ins = pe.transpose(turned[1][:, b * R2:(b + 1) * R2], rows_hi[:, b, :], c.ident[:])
                ins.then_inc(s_["ids_turned"], 1)
                pe.wait_ge(s_["src_ready"], 1)
                for b in range(C2):
                    ins = pe.transpose(turned[0][:, b * R2:(b + 1) * R2], rows_lo[:, b, :], c.ident[:])
                ins.then_inc(s_["ids_turned"], 1)
                with pe.Fori(0, B2 // 2) as b:
                    for s in range(2):
                        pe.wait_ge(s_["hot_t_ready"], b * 2 + (s + 1))
                        pe.wait_ge(s_["looked_free"], b * 2 + (s + 1))
                        for g in range(G2):
                            for i in range(3):
                                ins = pe.matmul(looked[s][:, g // 4, (g % 4) * J * HEADS:(g % 4 + 1) * J * HEADS],
                                                hi_hot_t[:, s, g * Q2:(g + 1) * Q2], a_b[:, i, :, :],
                                                start=(i == 0), stop=(i == 2))
                        ins.then_inc(s_["looked_up"], 1)
                pe.matmul(ps_sum[:, 0:J * HF], c.zeros_b[0:Q2, 0:P], c.zeros_b[:, 0:1].broadcast_to([Q2, J * HF]), start=True, stop=False, skip_group_check=True)
                with pe.Fori(0, B2 // 2) as b:
                    for s in range(2):
                        pe.wait_ge(s_["payload_ready"], b * 2 + (s + 1))
                        for g in range(G2):
                            ins = pe.matmul(ps_sum[:, 0:J * HF], hi_hot[:, s, g, :], payload[:, s, g, :],
                                            start=False, stop=False, skip_group_check=True)
                        ins.then_inc(s_["payload_free"], 1)
                pe.matmul(ps_sum[:, 0:J * HF], c.zeros_b[0:Q2, 0:P], c.zeros_b[:, 0:1].broadcast_to([Q2, J * HF]), start=False, stop=True,
                          skip_group_check=True).then_inc(s_["all_summed"], 1)

            @block.vector
            def _(v):
                link = Link(v, s_["edge_chain"])
                v.sem_inc(s_["looked_free"], 2)
                v.sem_inc(s_["payload_free"], 2)
                v.wait_ge(s_["ids_in"], 32)
                link(v.tensor_copy(rows_f[:], rows_i[:]))
                link(v.tensor_scalar(rows_hi[:], rows_f[:, 1, :, :], -float(J // 2), 1.0 / J, ALU.add, ALU.mult))
                link(v.tensor_scalar(rows_hi[:], rows_hi[:], ROUND, -ROUND, ALU.add, ALU.add))
                v.tensor_copy(rows_hi_b[:], rows_hi[:]).then_inc(s_["hi_ready"], 1)
                v.scalar_tensor_tensor(rows_lo[:], rows_hi[:], -float(J), rows_f[:, 1, :, :], ALU.mult, ALU.add).then_inc(s_["rows_ready"], 1)
                v.wait_ge(s_["ids_turned"], 1)
                v.tensor_copy(src_i[:], turned[0][:]).then_inc(s_["src_ready"], 1)
                link(v.tensor_copy(dst_hi[:], turned[1][:]))
                three_parts(v, link, [a_b[:, i, :, :] for i in range(3)], a_rest[:], c.a_dst[:])
                v.wait_ge(s_["ids_turned"], 2)
                link(v.tensor_copy(dst_lo[:], turned[0][:]))
                link(v.tensor_tensor(lo_hot[:], spread(dst_lo[:], 2, [Q2, T2, J]), spread(c.row_b[0:Q2, 0:J], 1, [Q2, T2, J]), ALU.is_equal))
                with v.Fori(0, B2 // 2) as b:
                    for s in range(2):
                        v.wait_ge(line_in[s], b * 16 + 16)
                        v.tensor_scalar(hi_hot_t[:, s, :], hi_line[:, s, :], c.col[0:P, 0:1], None,
                                        ALU.is_equal).then_inc(s_["hot_t_ready"], 1)
                        v.wait_ge(s_["looked_up"], b * 2 + (s + 1))
                        for half in range(2):
                            ins = v.tensor_tensor(found[:, half * 4:half * 4 + 4, :, :],
                                                  looked[s][:, half, 0:4 * J * HEADS].rearrange("q (g j h) -> q g j h", g=4, j=J),
                                                  spread(lo_hot[:, bass.ds(b * (2 * G2) + s * G2 + half * 4, 4), :], 3, [Q2, 4, J, HEADS]), ALU.mult)
                        ins.then_inc(s_["looked_free"], 1)
                        v.wait_ge(s_["looked_free"], b * 2 + (s + 3))
                        v.tensor_reduce(a_dst_e[:, bass.ds(b * (2 * G2) + s * G2, G2), :],
                                        found.rearrange("q g j h -> q g h j"), AX_X, ALU.add).then_inc(s_["found_done"], 1)
                v.wait_ge(s_["found_done"], B2)

                def logits(out, cap_out, a_src, a_dst, shape):
                    most = spread(c.most[0:shape[0], :], 1, shape)
                    link(v.tensor_tensor(out, a_src, a_dst, ALU.add))
                    link(v.scalar_tensor_tensor(out, out, 0.2, out, ALU.mult, ALU.max))
                    link(v.tensor_tensor(cap_out, a_dst, most, ALU.add))
                    link(v.scalar_tensor_tensor(cap_out, cap_out, 0.2, cap_out, ALU.mult, ALU.max))
                    return v.tensor_tensor(cap_out, out, cap_out, ALU.subtract)

                logits(own[:, 0, :, :], own[:, 1, :, :], c.h[:, :, HX:HF], c.a_dst[:], [P, J, HEADS]).then_inc(s_["self_in"], 1)
                v.wait_ge(s_["rows_in"], 1)
                logits(ex[:], cap[:], rows[:, :, HX:HF], a_dst_e[:], [Q2, T2, HEADS]).then_inc(s_["exp_ready"], 1)
                v.wait_ge(s_["exp_done"], 1)
                link(v.tensor_tensor(rows[:, :, 0:HX].rearrange("q t (h e) -> q t h e", e=NE0), rows[:, :, 0:HX].rearrange("q t (h e) -> q t h e", e=NE0),
                                     spread(ex[:], 3, [Q2, T2, HEADS, NE0]), ALU.mult))
                link(v.tensor_copy(rows[:, :, HX:HF], ex[:]))
                with v.Fori(0, B2 // 2) as b:
                    for s in range(2):
                        v.wait_ge(s_["payload_free"], b * 2 + (s + 1))
                        t0 = b * (2 * G2) + s * G2
                        v.tensor_tensor(hi_hot[:, s, :, :], spread(dst_hi[:, bass.ds(t0, G2)], 2, [Q2, G2, P]),
                                        spread(c.row[0:Q2, 0:P], 1, [Q2, G2, P]), ALU.is_equal)
                        v.tensor_tensor(payload[:, s, :, :].rearrange("q g (j f) -> q g j f", f=HF),
                                        spread(lo_hot[:, bass.ds(t0, G2), :], 3, [Q2, G2, J, HF]),
                                        spread(rows[:, bass.ds(t0, G2), :], 2, [Q2, G2, J, HF]), ALU.mult).then_inc(s_["payload_ready"], 1)
                v.wait_ge(s_["par_in"], 48)
                v.wait_ge(s_["all_summed"], 1)
                v.wait_ge(s_["self_done"], 1)
                link(v.tensor_copy(agg[:], ps_sum[:, 0:J * HF].rearrange("p (j f) -> p j f", f=HF)))
                by_head = lambda ap: ap.rearrange("p j (h e) -> p j h e", e=NE0)
                link(v.tensor_tensor(by_head(sq[:]), by_head(c.h[:, :, 0:HX]), spread(own[:, 2, :, :], 3, [P, J, HEADS, NE0]), ALU.mult))
                link(v.tensor_tensor(agg[:, :, 0:HX], agg[:, :, 0:HX], sq[:], ALU.add))
                link(v.tensor_tensor(agg[:, :, HX:HF], agg[:, :, HX:HF], own[:, 2, :, :], ALU.add))
                link(v.reciprocal(own[:, 0, :, :], agg[:, :, HX:HF]))
                link(v.tensor_tensor(by_head(sq[:]), by_head(agg[:, :, 0:HX]), spread(own[:, 0, :, :], 3, [P, J, HEADS, NE0]), ALU.mult))
                link(v.tensor_tensor(agg[:, :, 0:HX], sq[:], spread(params[:, 0, :], 1, [P, J, HX]), ALU.add))
                a16, mu, var, sd, rs = agg[:, :, 0:HX], stat[:, 0, :], stat[:, 1, :], stat[:, 2, :], stat[:, 3, :]
                link(v.tensor_reduce(mu, a16, AX_X, ALU.add))
                link(v.tensor_scalar(mu, mu, 1.0 / HX, None, ALU.mult))
                link(v.tensor_tensor(a16, a16, spread(mu, 2, [P, J, HX]), ALU.subtract))
                link(v.tensor_tensor(sq[:], a16, a16, ALU.mult))
                link(v.tensor_reduce(var, sq[:], AX_X, ALU.add))
                v.tensor_scalar(var, var, 1.0 / HX, EPS, ALU.mult, ALU.add).then_inc(s_["var_ready"], 1)
                v.wait_ge(s_["std_ready"], 1)
                link(v.reciprocal(rs, sd))
                link(v.tensor_tensor(a16, a16, spread(rs, 2, [P, J, HX]), ALU.mult))
                link(v.tensor_tensor(a16, a16, spread(params[:, 1, :], 1, [P, J, HX]), ALU.mult))
                link(v.tensor_tensor(a16, a16, spread(params[:, 2, :], 1, [P, J, HX]), ALU.add))
                link(v.tensor_reduce(score[:], a16.rearrange("p j (h e) -> p j e h", e=NE0), AX_X, ALU.add))
                link(v.tensor_scalar(score[:], score[:], 1.0 / HEADS, None, ALU.mult))
                lower_triangle(v, link, c, tri, NE0)
                top2_gates(v, link, score[:], c.gates[:, 0:NE0, :], t[:], big[:], tri[:], exp_in[:], exp_out[:],
                           (s_["gate_in"], s_["gate_out"], 1))


def lower_triangle(v, link, c, tri, e):
    for i in range(e):
        ins = v.tensor_scalar(tri[:, i * e:(i + 1) * e], c.row[0:P, 0:e], float(i), None, ALU.is_lt)
    link(ins)


def block_experts(nc, c, io, pre, experts, edge_table):
    steps = 5
    cols = steps * P
    subs = ((0, 3 * P), (3 * P, cols))
    hc = 4
    body = 2 * steps
    with ExitStack() as ctx:
        m = Memory(nc, ctx, pre + "_")
        w1 = m.sb("w1s", [128, 2, K, hc * 128])
        w2 = m.sb("w2s", [128, 2, hc, D])
        b1 = m.sb("b1s", [128, experts, hc])
        bias = m.sb("bias", [128, 2, hc])
        b1_rows = m.sb("b1_rows", [experts * hc, 128])
        b2 = m.sb("b2s", [experts, D])
        gates_t = m.sb("gates_t", [experts, J, P])
        hidden = m.sb("hidden_s", [128, 2, hc, cols])
        ps_h = [[m.ps(f"ps_h{s}{i}", [128, 512]) for i in range(2)] for s in range(2)]
        ps_y = [m.ps(f"ps_y{s}", [P, 512]) for s in range(2)]
        ps_g = m.ps("ps_g", [experts, 512])
        if edge_table is not None:
            attr = m.sb("attr", [R1, 2, QE, FE])
            attr_w = m.sb("attr_w", [R1, FE])
            attr_out = m.sb("attr_out", [R1, C1, Q1])
            attr_in = [m.sem(f"attr_in{i}") for i in range(2)]
            attr_done, attr_w_in, attr_mul, attr_stored = (m.sem(n) for n in ("attr_done", "attr_w_in", "attr_mul", "attr_stored"))
        w_in = [m.sem(f"ex_w_in{i}") for i in range(2)]
        bias_ready = m.sem("bias_ready")
        b_in, b1_turned, b1_ready = m.sem("ex_b_in"), m.sem("b1_turned"), m.sem("b1_ready")
        up_done, up_free = m.sem("up_done"), m.sem("up_free")
        down_done, hidden_free, y_free = m.sem("down_done"), m.sem("hidden_free"), m.sem("y_free")
        g_turned, g_ready, bias_done, bias_added = (m.sem(n) for n in ("g_turned", "g_ready", "bias_done", "bias_added"))
        with nc.Block() as block:

            @block.sync
            def _(sp):
                def load(e, s):
                    one = bass.ds(e, 1)
                    sp.dma_start(w1[:, s, :, :], io[pre + "_W1"][one].rearrange("e (k p) h -> p (e k) h", p=128)).then_inc(w_in[s], 16)
                    sp.dma_start(w2[:, s, :, :], io[pre + "_W2"][one].rearrange("e (k p) h -> p (e k) h", p=128)).then_inc(w_in[s], 16)

                for s in range(2):
                    load(s, s)
                sp.dma_start(b1_rows[:], io[pre + "_b1"].rearrange("e (k p) -> (e k) p", p=128)).then_inc(b_in, 16)
                sp.dma_start(b2[:], io[pre + "_b2"]).then_inc(b_in, 16)
                if edge_table is not None:
                    sp.dma_start(attr_w[:], io["L1_gnn_A"][:, 2 * D:2 * D + FE].broadcast_to([R1, FE])).then_inc(attr_w_in, 16)
                    chunks = io["edge_attr_64"].rearrange("(c r b q) f -> c b r (q f)", r=R1, b=Q1 // QE, q=QE)
                    for n in range(2 * body):
                        if n >= 2:
                            sp.wait_ge(attr_done, n - 1)
                        sp.dma_start(attr[:, n % 2, :, :].rearrange("r q f -> r (q f)"), chunks[n // (Q1 // QE), n % (Q1 // QE)]).then_inc(attr_in[n % 2], 16)
                        if n == body:
                            for s in range(2):
                                sp.wait_ge(down_done, J * (s + 1))
                                load(2 + s, s)
                    sp.wait_ge(attr_done, 2 * body)
                    sp.dma_start(edge_table.rearrange("(c r q) -> r c q", r=R1, q=Q1), attr_out[:]).then_inc(attr_stored, 16)
                    sp.wait_ge(attr_stored, 16)
                    return
                with sp.Fori(1, experts // 2) as b:
                    for s in range(2):
                        sp.wait_ge(down_done, b * (2 * J) + (s - 1) * J)
                        load(b * 2 + s, s)

            @block.tensor
            def _(pe):
                def up(b, k):
                    s, g = (k // steps) % 2, k % steps
                    if k % steps == 0:
                        pe.wait_ge(w_in[s], b * 32 + 32 * (1 + k // body))
                    for h in range(hc):
                        i = (k * hc + h) % 2
                        pe.wait_ge(up_free, b * (body * hc) + (k * hc + h + 1))
                        for n, (lo, hi) in enumerate(subs):
                            for kk in range(K):
                                ins = pe.matmul(ps_h[i][n][:, 0:hi - lo], w1[:, s, kk, h * 128:(h + 1) * 128],
                                                c.xt[:, kk, g * cols + lo:g * cols + hi], start=(kk == 0), stop=(kk == K - 1))
                        ins.then_inc(up_done, 1)

                def down(b, k):
                    s = (k // steps) % 2
                    pe.wait_ge(up_free, b * (body * hc) + ((k + 1) * hc + 2))
                    for i in range(steps):
                        n = k * steps + i
                        pe.wait_ge(y_free, b * (body * steps) + (n + J - 1))
                        for h in range(hc):
                            ins = pe.matmul(ps_y[n % 2][:, 0:D], hidden[:, k % 2, h, i * P:(i + 1) * P], w2[:, s, h, :],
                                            start=(h == 0), stop=(h == hc - 1))
                        ins.then_inc(down_done, 1)

                pe.wait_ge(b_in, 32)
                pe.transpose(ps_h[0][0][:, 0:experts * hc], b1_rows[:], c.ident[0:experts * hc, 0:experts * hc]).then_inc(b1_turned, 1)
                for j in range(J):
                    if j:
                        pe.wait_ge(g_ready, j)
                    pe.transpose(ps_g[:, 0:P], c.gates[:, 0:experts, j], c.ident[0:P, 0:P]).then_inc(g_turned, 1)
                for j in range(J):
                    pe.wait_ge(g_ready, J)
                    if j >= 2:
                        pe.wait_ge(bias_added, j - 1)
                    pe.matmul(ps_y[j % 2][:, 0:D], gates_t[:, j, :], b2[:], start=True, stop=True).then_inc(bias_done, 1)
                pe.wait_ge(bias_added, J)
                pe.wait_ge(b1_ready, 1)
                up(0, 0)
                with pe.Fori(0, experts // 2 - 1) as b:
                    for k in range(body):
                        up(b, k + 1)
                        down(b, k)
                b = experts // 2 - 1
                for k in range(body):
                    if k < body - 1:
                        up(b, k + 1)
                    down(b, k)

            @block.scalar
            def _(act):
                act.sem_inc(up_free, 2)
                act.wait_ge(b1_turned, 1)
                act.copy(b1.rearrange("p e k -> p (e k)"), ps_h[0][0][:, 0:experts * hc]).then_inc(b1_ready, 1)
                act.wait_ge(b1_ready, 1)
                with act.Fori(0, experts // 2) as b:
                    for k in range(body):
                        s = (k // steps) % 2
                        if k % steps == 0:
                            act.copy(bias[:, s, :], b1[:, bass.ds(b * 2 + s, 1), :].squeeze(1)).then_inc(bias_ready, 1)
                            act.wait_ge(bias_ready, b * 2 + (s + 1))
                        act.wait_ge(hidden_free, b * body + (k + 1))
                        for h in range(hc):
                            act.wait_ge(up_done, b * (body * hc) + (k * hc + h + 1))
                            for n, (lo, hi) in enumerate(subs):
                                ins = act.activation(hidden[:, k % 2, h, lo:hi], ps_h[(k * hc + h) % 2][n][:, 0:hi - lo], ACT.Gelu,
                                                     bias=bias[:, s, h:h + 1])
                            ins.then_inc(up_free, 1)

            @block.vector
            def _(v):
                v.sem_inc(y_free, J)
                v.sem_inc(hidden_free, 2)
                for j in range(J):
                    v.wait_ge(g_turned, j + 1)
                    v.tensor_copy(gates_t[:, j, :], ps_g[:, 0:P]).then_inc(g_ready, 1)
                for j in range(J):
                    v.wait_ge(bias_done, j + 1)
                    v.tensor_tensor(c.x[:, j, :], ps_y[j % 2][:, 0:D], c.x[:, j, :], ALU.add).then_inc(bias_added, 1)
                v.wait_ge(bias_added, J)
                if edge_table is not None:
                    v.wait_ge(attr_w_in, 16)
                with v.Fori(0, experts // 2) as b:
                    for k in range(body):
                        s, g = (k // steps) % 2, k % steps
                        for i in range(steps):
                            n, j = k * steps + i, g * steps + i
                            v.wait_ge(down_done, b * (body * steps) + (n + 1))
                            v.wait_ge(y_free, b * (body * steps) + (n + 1))
                            v.scalar_tensor_tensor(c.x[:, j, :], ps_y[n % 2][:, 0:D], c.gates[:, bass.ds(b * 2 + s, 1), j],
                                                   c.x[:, j, :], ALU.mult, ALU.add).then_inc(y_free, 1)
                        v.sem_inc(hidden_free, 1)
                        if edge_table is not None:
                            v.wait_ge(attr_in[k % 2], b * (8 * body) + 16 * (k // 2 + 1))
                            v.tensor_tensor(attr[:, k % 2, :, :], attr[:, k % 2, :, :], spread(attr_w[:], 1, [R1, QE, FE]),
                                            ALU.mult).then_inc(attr_mul, 1)
                            v.wait_ge(attr_mul, b * body + (k + 1))
                            v.tensor_reduce(attr_out.rearrange("r c (b q) -> r (c b) q", q=QE)[:, bass.ds(b * body + k, 1), :].squeeze(1),
                                            attr[:, k % 2, :, :], AX_X, ALU.add).then_inc(attr_done, 1)


def block_z(nc, c, io):
    with ExitStack() as ctx:
        m = Memory(nc, ctx, "z_")
        st = m.sb("st", [P, J, BN])
        small = m.sb("small", [P, 5, J])
        std = m.sb("std", [P, J])
        w = m.sb("w", [128, K, D])
        wt = m.sb("wt", [128, K, ZF])
        a_rows = m.sb("a_rows", [2 * K, 128])
        a_cols = m.sb("a_cols", [128, 2, K])
        z = m.sb("z", [P, J, ZF])
        ps_turn = [m.ps(f"ps_turn{i}", [128, 512]) for i in range(2)]
        ps_w = m.ps("ps_w", [128, 512])
        ps_wa = m.ps("ps_wa", [128, 2 * K + 4])
        ps_z = [m.ps(f"ps_z{i}", [P, 512]) for i in range(2)]
        w_in, var_ready, std_ready, xl_ready = (m.sem(n) for n in ("w_in", "var_ready", "std_ready", "xl_ready"))
        turned, turn_free, a_turned, a_ready = (m.sem(n) for n in ("turned", "turn_free", "a_turned", "a_ready"))
        w_turned, w_ready, wa_summed, wt_ready = (m.sem(n) for n in ("w_turned", "w_ready", "wa_summed", "wt_ready"))
        z_summed, z_copied, ones_set = (m.sem(n) for n in ("z_summed", "z_copied", "ones_set"))
        x_out, z_out, a_set, line_out, chain = (m.sem(n) for n in ("x_out", "z_out", "a_set", "line_out", "chain"))
        with nc.Block() as block:

            @block.sync
            def _(sp):
                sp.dma_start(w[:], io["L1_gnn_W"].rearrange("(k p) c -> p k c", p=128)).then_inc(w_in, 16)
                sp.dma_start(a_rows[:], io["L1_gnn_A"][0, 0:2 * D].rearrange("(k p) -> k p", p=128)).then_inc(w_in, 16)
                sp.dma_start(c.x_table.rearrange("(p j) d -> p j d", j=J), c.x[:]).then_inc(x_out, 16)
                for j in range(0, J, 5):
                    sp.wait_ge(ones_set, j // 5 + 1)
                    sp.dma_start(c.z_table.rearrange("(p j) f -> p j f", j=J)[:, j:j + 5, :], z[:, j:j + 5, :]).then_inc(z_out, 16)
                sp.wait_ge(z_out, 16 * 5)
                sp.wait_ge(x_out, 16)

            @block.tensor
            def _(pe):
                pe.wait_ge(w_in, 32)
                pe.transpose(ps_wa[:, 2 * K:2 * K + 4], a_rows[:], c.ident[0:4, 0:4]).then_inc(a_turned, 1)
                for k in range(K):
                    for f in range(K):
                        ins = pe.transpose(ps_w[:, (k * K + f) * 128:(k * K + f + 1) * 128], w[:, f, k * 128:(k + 1) * 128], c.ident[:])
                ins.then_inc(w_turned, 1)
                pe.wait_ge(a_ready, 1)
                for k in range(K):
                    for f in range(K):
                        ins = pe.matmul(ps_wa[:, 2 * k:2 * k + 2], w[:, f, k * 128:(k + 1) * 128], a_cols[:, :, f],
                                        start=(f == 0), stop=(f == K - 1))
                ins.then_inc(wa_summed, 1)
                pe.wait_ge(xl_ready, 1)
                transpose_nodes(pe, c, ps_turn, None, turn_free, turned, 0)
                pe.wait_ge(turn_free, TURNS)
                pe.wait_ge(wt_ready, 2)
                for j in range(J):
                    if j >= 2:
                        pe.wait_ge(z_copied, j - 1)
                    for k in range(K):
                        ins = pe.matmul(ps_z[j % 2][:, 0:ZF], c.xt[:, k, j * P:(j + 1) * P], wt[:, k, :],
                                        start=(k == 0), stop=(k == K - 1))
                    ins.then_inc(z_summed, 1)

            @block.scalar
            def _(act):
                act.wait_ge(w_turned, 1)
                act.copy(wt[:, :, 0:D], ps_w.rearrange("p (k f) -> p k f", k=K)).then_inc(wt_ready, 1)
                act.wait_ge(var_ready, 1)
                act.activation(std[:], small[:, 2, :], ACT.Sqrt).then_inc(std_ready, 1)
                copy_turned(act, act.copy, c, ps_turn, turn_free, turned, 0)
                for j in range(J):
                    act.wait_ge(z_summed, j + 1)
                    act.copy(z[:, j, :], ps_z[j % 2][:, 0:ZF]).then_inc(z_copied, 1)

            @block.vector
            def _(v):
                link = Link(v, chain)
                v.wait_ge(a_turned, 1)
                v.tensor_copy(a_cols.rearrange("p s k -> p (s k)"), ps_wa[:, 2 * K:2 * K + 4]).then_inc(a_ready, 1)
                link(v.memset(wt[:, :, D:D + 1], 0.0))
                layernorm_stats(v, link, c.x, st, small, std[:], var_ready, 1, std_ready)
                layernorm_apply(v, link, c.xl, c.x, small)
                v.sem_inc(xl_ready, 1)
                v.wait_ge(wa_summed, 1)
                v.tensor_copy(wt[:, :, D + 1:D + 3], ps_wa[:, 0:2 * K].rearrange("p (k s) -> p k s", k=K)).then_inc(wt_ready, 1)
                for j in range(0, J, 5):
                    v.wait_ge(z_copied, j + 5)
                    v.memset(z[:, j:j + 5, D:D + 1], 1.0).then_inc(ones_set, 1)
                link(v.tensor_copy(c.ad_nodes[:], z[:, :, D + 2]))
                link(v.memset(c.most_of[:], -3e38))
                link(v.tensor_reduce(c.most_of[0:P, 0:1], z[:, :, D + 1], AX_X, ALU.max))


def block_windows(nc, c, io):
    with ExitStack() as ctx:
        m = Memory(nc, ctx, "windows_")
        acc = m.sb("acc", [P, J, D + 1])
        first = m.sb("first", [128, J])
        item_w = m.sb("item_w", [128, I4])
        item_t = m.sb("item_t", [128, I4])
        item_n = m.sb("item_n", [128, I4])
        item_t_i = m.sb("item_t_i", [128, I4], I32)
        w_rows = m.sb("w_rows", [I4, 128], I32)
        w_line = m.sb("w_line", [1, I4 * 128], I32)
        less = m.sb("less", [128, J])
        five = m.sb("five", [P, J])
        count = m.sb("count", [P, 1])
        count_row = m.sb("count_row", [P, 128])
        src_rows_i = m.sb("src_rows_i", [128, I4, Q1], I32)
        dst_rows_i = m.sb("dst_rows_i", [128, I4, Q1], I32)
        src_rows = m.sb("src_rows", [128, I4, Q1])
        dst_rows = m.sb("dst_rows", [128, I4, Q1])
        hi_rows = m.sb("hi_rows", [128, I4, Q1])
        hi_rows_b = m.sb("hi_rows_b", [128, I4, Q1], BF16)
        edge_rows = m.sb("edge_rows", [128, I4, Q1])
        src_i = m.sb("src_i", [Q1, I4 * 128], I32)
        dst = m.sb("dst", [Q1, I4 * 128])
        dst_lo = m.sb("dst_lo", [Q1, I4 * 128], BF16)
        lo_hot = m.sb("lo_hot", [Q1, IP, J], BF16)
        edge = m.sb("edge", [Q1, I4 * 128])
        ad = m.sb("ad", [Q1, IP])
        cap = m.sb("cap", [Q1, IP])
        most = m.sb("most", [128, 4])
        hi_line = m.sb("hi_line", [P, 2, G1 * Q1], BF16)
        hi_hot_t = m.sb("hi_hot_t", [P, 2, G1 * Q1], BF16)
        found = m.sb("found", [Q1, G1, J])
        ad_rest = m.sb("ad_rest", [P, J])
        ad_b = m.sb("ad_b", [P, 3, J], BF16)
        zero_i = m.sb("zero_i", [128, UW], I32)
        spare_i = m.sb("spare_i", [128, 1], I32)
        stage = m.sb("stage", [Q1, SW, UW], I32)
        ring = m.sb("ring", [Q1, SW, UW, ZF])
        logit = m.sb("logit", [Q1, 2, UW])
        lrelu = m.sb("lrelu", [Q1, 2, UW])
        below = m.sb("below", [Q1, 2, UW])
        ex = m.sb("ex", [Q1, 2, UW])
        prob = m.sb("prob", [Q1, 2, UW, P])
        rden = m.sb("rden", [P, J])
        ps_a = m.ps("ps_a", [128, 512])
        ps_b = m.ps("ps_b", [128, 512])
        looked = [m.ps(f"looked{i}", [Q1, 512]) for i in range(2)]
        part = [m.ps(f"part{i}", [P, 512]) for i in range(4)]
        names = ("count_ready", "count_summed", "items_ready", "w_turned", "w_ready", "w_out", "rows_in", "hi_ready",
                 "hi_out", "rows_ready", "turned", "turn_free", "src_ready", "most_in", "most_out", "hot_t_ready",
                 "looked_up", "looked_free", "found_done", "x_in", "staged", "used", "below_ready", "ex_ready",
                 "prob_ready", "part_ready", "part_free", "small_chain", "chain", "z_line")
        s_ = {n: m.sem(n) for n in names}
        line_in = [m.sem(f"line_in{i}") for i in range(2)]
        gathered = [m.sem(f"gathered{i}") for i in range(SW)]
        table = lambda ap: ap.rearrange("(t q) -> t q", q=Q1)
        with nc.Block() as block:

            @block.sync
            def _(sp):
                sp.dma_start(c.x[:], c.x_table.rearrange("(w d) f -> d w f", d=P)).then_inc(s_["x_in"], 16)
                sp.wait_ge(s_["w_ready"], 1)
                sp.dma_start(c.w_dram.rearrange("(k p) -> k p", p=128), w_rows[:]).then_inc(s_["w_out"], 16)
                sp.wait_ge(s_["w_out"], 16)
                sp.dma_start(w_line[:], c.w_dram.unsqueeze(0)).then_inc(s_["z_line"], 16)
                sp.wait_ge(s_["hi_ready"], 1)
                sp.dma_start(c.hi_line_dram3.rearrange("(k p q) -> p k q", p=128, q=Q1), hi_rows_b[:]).then_inc(s_["hi_out"], 16)
                sp.wait_ge(s_["hi_out"], 16)
                lines = c.hi_line_dram3[0:IP * Q1].rearrange("(b e) -> b e", e=G1 * Q1)
                for s in range(2):
                    sp.dma_start(hi_line[:, s, :], lines[s:s + 1, :].broadcast_to([P, G1 * Q1])).then_inc(line_in[s], 16)
                with sp.Fori(1, IP // G1 // 2) as b:
                    for s in range(2):
                        sp.wait_ge(s_["hot_t_ready"], b * 2 + (s - 1))
                        sp.dma_start(hi_line[:, s, :], lines[bass.ds(b * 2 + s, 1), :].broadcast_to([P, G1 * Q1])).then_inc(line_in[s], 16)

            @block.gpsimd
            def _(pool):
                pool.memset(zero_i[:], 0).then_inc(s_["staged"], 1)
                pool.wait_ge(s_["items_ready"], 1)
                for k in range(I4):
                    at = bass.IndirectOffsetOnAxis(ap=item_t_i[:, k:k + 1], axis=0)
                    pool.indirect_dma_start(src_rows_i[:, k, :], None, table(io["src"]), at).then_inc(s_["rows_in"], 16)
                    pool.indirect_dma_start(dst_rows_i[:, k, :], None, table(io["dst"]), at).then_inc(s_["rows_in"], 16)
                    pool.indirect_dma_start(edge_rows[:, k, :], None, table(c.edge_table), at).then_inc(s_["rows_in"], 16)
                pool.wait_ge(s_["src_ready"], 1)
                pool.wait_ge(s_["staged"], 1)

                def gather(g, s):
                    pool.wait_ge(s_["used"], g + 1)
                    pool.tensor_tensor(stage[:, s, :], src_i[:, bass.ds(g * UW, UW)], zero_i[0:Q1, :], ALU.add).then_inc(s_["staged"], 1)
                    pool.wait_ge(s_["staged"], g + 2)
                    pool.tensor_tensor(spare_i[:], zero_i[:, 0:1], zero_i[:, 1:2], ALU.add)
                    for u in range(UW):
                        pool.indirect_dma_start(ring[:, s, u, :], None, c.z_table,
                                                bass.IndirectOffsetOnAxis(ap=stage[:, s, u:u + 1], axis=0)).then_inc(gathered[s], 16)

                gather(0, 0)
                pool.wait_ge(s_["most_in"], 1)
                pool.partition_all_reduce(most[:, 0:2], c.most_of[:, 0:2], 128, bass.bass_isa.ReduceOp.max).then_inc(s_["most_out"], 1)
                with pool.Fori(0, GW // SW) as b:
                    for s in range(SW):
                        gather(b * SW + (s + 1), (s + 1) % SW)

            @block.tensor
            def _(pe):
                pe.wait_ge(s_["count_ready"], 1)
                pe.matmul(ps_a[:, 0:J], count_row[:], five[:], start=True, stop=True).then_inc(s_["count_summed"], 1)
                pe.wait_ge(s_["items_ready"], 1)
                pe.transpose(ps_b[0:I4, 0:128], item_w[:], c.ident[:]).then_inc(s_["w_turned"], 1)
                pe.wait_ge(s_["w_ready"], 1)
                pe.wait_ge(s_["rows_ready"], 1)
                for i, rows in enumerate((src_rows, dst_rows, hi_rows, edge_rows)):
                    if i >= 2:
                        pe.wait_ge(s_["turn_free"], i - 1)
                    for k in range(I4):
                        ins = pe.transpose((ps_a, ps_b)[i % 2][0:Q1, k * 128:(k + 1) * 128], rows[:, k, :], c.ident[:])
                    ins.then_inc(s_["turned"], 1)
                with pe.Fori(0, IP // G1 // 2) as b:
                    for s in range(2):
                        pe.wait_ge(s_["hot_t_ready"], b * 2 + (s + 1))
                        pe.wait_ge(s_["looked_free"], b * 2 + (s + 1))
                        for g in range(G1):
                            for i in range(3):
                                ins = pe.matmul(looked[s][:, g * J:(g + 1) * J], hi_hot_t[:, s, g * Q1:(g + 1) * Q1],
                                                ad_b[:, i, :], start=(i == 0), stop=(i == 2))
                        ins.then_inc(s_["looked_up"], 1)

                def group(g, s, half):
                    for u in range(UW):
                        pe.wait_ge(s_["prob_ready"], g * UW + (u + 1))
                        pe.wait_ge(s_["part_free"], g * UW + (u + 1))
                        ins = pe.matmul(part[u % 4][:, 0:D + 1], prob[:, half, u, :], ring[:, s, u, 0:D + 1], start=True, stop=True)
                        ins.then_inc(s_["part_ready"], 1)

                with pe.Fori(0, GW // SW) as b:
                    for s in range(SW):
                        group(b * SW + s, s, s % 2)
                group(GW - 1, (GW - 1) % SW, (GW - 1) % 2)

            @block.scalar
            def _(act):
                def exps(g, half):
                    act.wait_ge(s_["below_ready"], g + 1)
                    act.activation(ex[:, half, :], below[:, half, :], ACT.Exp).then_inc(s_["ex_ready"], 1)

                with act.Fori(0, (GW - 1) // 2) as b:
                    for s in range(2):
                        exps(b * 2 + s, s)
                exps(GW - 1, (GW - 1) % 2)

            @block.vector
            def _(v):
                link = Link(v, s_["chain"])
                v.sem_inc(s_["looked_free"], 2)
                v.sem_inc(s_["part_free"], 4)
                v.sem_inc(s_["used"], SW)
                link(v.tensor_scalar(five[:], c.row[0:P, 0:J], float(P // J), None, ALU.mult))
                link(v.tensor_scalar(five[:], five[:], c.col[0:P, :], None, ALU.is_gt))
                link(v.tensor_reduce(count[:], c.deg[:], AX_X, ALU.add))
                v.tensor_copy(count_row[:], count[:, 0:1].broadcast_to([P, 128])).then_inc(s_["count_ready"], 1)
                link(v.memset(acc[:], 0.0))
                v.wait_ge(s_["count_summed"], 1)
                link(v.tensor_scalar(first[:], ps_a[:, 0:J], -float(Q1 // 2), 1.0 / Q1, ALU.add, ALU.mult))
                link(v.tensor_scalar(first[:], first[:], ROUND, -ROUND, ALU.add, ALU.add))
                link(v.tensor_scalar(first[:], first[:], float(T1 - 1), None, ALU.min))
                link(v.tensor_tensor(first[:], first[:], c.row[:, 0:J], ALU.add))
                for k in range(I4):
                    link(v.tensor_scalar(item_n[:, k:k + 1], c.col[:], 128.0 * k, None, ALU.add))
                    link(v.tensor_scalar(less[:, 0:J - 1], first[:, 1:J], item_n[:, k:k + 1], None, ALU.is_le))
                    link(v.tensor_reduce(item_w[:, k:k + 1], less[:, 0:J - 1], AX_X, ALU.add))
                link(v.tensor_tensor(item_t[:], item_n[:], item_w[:], ALU.subtract))
                link(v.tensor_scalar(item_t[:], item_t[:], float(T1 - 1), None, ALU.min))
                v.tensor_copy(item_t_i[:], item_t[:]).then_inc(s_["items_ready"], 1)
                v.wait_ge(s_["w_turned"], 1)
                v.tensor_copy(w_rows[:], ps_b[0:I4, 0:128]).then_inc(s_["w_ready"], 1)
                link(v.tensor_scalar(item_w[:], item_w[:], float(P), None, ALU.mult))
                three_parts(v, link, [ad_b[:, i, :] for i in range(3)], ad_rest[:], c.ad_nodes[:])
                v.wait_ge(s_["rows_in"], 16 * 3 * I4)
                link(v.tensor_copy(src_rows[:], src_rows_i[:]))
                link(v.tensor_copy(dst_rows[:], dst_rows_i[:]))
                link(v.tensor_scalar(hi_rows[:], dst_rows[:], -float(J // 2), 1.0 / J, ALU.add, ALU.mult))
                link(v.tensor_scalar(hi_rows[:], hi_rows[:], ROUND, -ROUND, ALU.add, ALU.add))
                link(v.tensor_copy(hi_rows_b[:], hi_rows[:]))
                v.sem_inc(s_["hi_ready"], 1)
                link(v.scalar_tensor_tensor(hi_rows[:], hi_rows[:], -float(J), dst_rows[:], ALU.mult, ALU.add))
                for k in range(I4):
                    link(v.tensor_scalar(dst_rows[:, k, :], dst_rows[:, k, :], item_w[:, k:k + 1], None, ALU.subtract))
                v.sem_inc(s_["rows_ready"], 1)
                link(v.tensor_reduce(c.most_of[:, 1:2], edge_rows.rearrange("p k q -> p (k q)"), AX_X, ALU.max))
                v.sem_inc(s_["most_in"], 1)
                for i, to in enumerate((src_i, dst, dst_lo, edge)):
                    v.wait_ge(s_["turned"], i + 1)
                    ins = v.tensor_copy(to[:], (ps_a, ps_b)[i % 2][0:Q1, :])
                    link(ins)
                    v.sem_inc(s_["turn_free"], 1)
                    if i == 0:
                        v.sem_inc(s_["src_ready"], 1)
                link(v.tensor_tensor(lo_hot[:], spread(dst_lo[:, 0:IP], 2, [Q1, IP, J]), spread(c.row_b[0:Q1, 0:J], 1, [Q1, IP, J]), ALU.is_equal))
                with v.Fori(0, IP // G1 // 2) as b:
                    for s in range(2):
                        v.wait_ge(line_in[s], b * 16 + 16)
                        v.tensor_scalar(hi_hot_t[:, s, :], hi_line[:, s, :], c.col[0:P, 0:1], None,
                                        ALU.is_equal).then_inc(s_["hot_t_ready"], 1)
                        v.wait_ge(s_["looked_up"], b * 2 + (s + 1))
                        t0 = b * (2 * G1) + s * G1
                        v.tensor_tensor(found[:], looked[s][:, 0:G1 * J].rearrange("q (g j) -> q g j", j=J),
                                        lo_hot[:, bass.ds(t0, G1), :], ALU.mult).then_inc(s_["looked_free"], 1)
                        v.wait_ge(s_["looked_free"], b * 2 + (s + 3))
                        v.tensor_reduce(ad[:, bass.ds(t0, G1)], found[:], AX_X, ALU.add).then_inc(s_["found_done"], 1)
                v.wait_ge(s_["found_done"], IP // G1)
                v.wait_ge(s_["most_out"], 1)
                link(v.tensor_tensor(most[:, 2:3], most[:, 0:1], most[:, 1:2], ALU.add))
                link(v.tensor_scalar(cap[:], ad[:], most[0:Q1, 2:3], None, ALU.add))
                link(v.scalar_tensor_tensor(cap[:], cap[:], 0.2, cap[:], ALU.mult, ALU.max))
                link(v.tensor_tensor(ad[:], ad[:], edge[:, 0:IP], ALU.add))

                def logits(g, s, half, seen):
                    now = bass.ds(g * UW, UW) if not isinstance(g, int) else slice(g * UW, (g + 1) * UW)
                    v.wait_ge(gathered[s], seen)
                    v.tensor_tensor(logit[:, half, :], ring[:, s, :, D + 1], ad[:, now], ALU.add).then_inc(s_["small_chain"], 1)
                    v.wait_ge(s_["small_chain"], g * 2 + 1)
                    v.scalar_tensor_tensor(lrelu[:, half, :], logit[:, half, :], 0.2, logit[:, half, :], ALU.mult, ALU.max).then_inc(s_["small_chain"], 1)
                    v.wait_ge(s_["small_chain"], g * 2 + 2)
                    v.tensor_tensor(below[:, half, :], lrelu[:, half, :], cap[:, now], ALU.subtract).then_inc(s_["below_ready"], 1)

                def one_hot(g, u, half):
                    i = g * UW + u
                    at = bass.ds(i, 1) if not isinstance(g, int) else slice(i, i + 1)
                    v.tensor_scalar(prob[:, half, u, :], c.row[0:Q1, 0:P], dst[:, at], ex[:, half, u:u + 1],
                                    ALU.is_equal, ALU.mult).then_inc(s_["prob_ready"], 1)

                def add(g, u):
                    i = g * UW + u
                    at = bass.ds(i, 1) if not isinstance(g, int) else slice(i, i + 1)
                    w = v.value_load(w_line[0:1, at], min_val=0, max_val=J - 1)
                    v.wait_ge(s_["part_ready"], i + 1)
                    v.wait_ge(s_["part_free"], i + 4)
                    row = acc[:, bass.ds(w, 1), :].squeeze(1)
                    v.tensor_tensor(row, part[u % 4][:, 0:D + 1], row, ALU.add).then_inc(s_["part_free"], 1)
                    if u == UW - 1:
                        v.sem_inc(s_["used"], 1)

                v.wait_ge(s_["z_line"], 16)
                logits(0, 0, 0, 16 * UW)
                v.wait_ge(s_["ex_ready"], 1)
                for u in range(UW):
                    one_hot(0, u, 0)
                with v.Fori(0, (GW - 1) // SW) as b:
                    for k in range(SW):
                        g, s, half = b * SW + (k + 1), (k + 1) % SW, (k + 1) % 2
                        logits(g, s, half, b * (16 * UW) + 16 * UW * (1 + (k + 1) // SW))
                        for u in range(UW):
                            add(b * SW + k, u)
                            if u == 0:
                                v.wait_ge(s_["ex_ready"], g + 1)
                            one_hot(g, u, half)
                for u in range(UW):
                    add(GW - 1, u)
                v.wait_ge(s_["part_free"], GW * UW + 4)
                link(v.tensor_scalar(rden[:], acc[:, :, D], 1e-37, None, ALU.max))
                link(v.reciprocal(rden[:], rden[:]))
                v.wait_ge(s_["x_in"], 16)
                with v.Fori(0, J) as j:
                    v.scalar_tensor_tensor(c.x[:, bass.ds(j, 1), :].squeeze(1), acc[:, bass.ds(j, 1), 0:D].squeeze(1), rden[:, bass.ds(j, 1)],
                                           c.x[:, bass.ds(j, 1), :].squeeze(1), ALU.mult, ALU.add).then_inc(link.sem, 1)
                link.loop_end(J)
                v.wait_ge(link.sem, link.n)


def block_router(nc, c, io):
    with ExitStack() as ctx:
        m = Memory(nc, ctx, "router_")
        st = m.sb("st", [P, J, BN])
        small = m.sb("small", [P, 5, J])
        std = m.sb("std", [P, 2, J])
        scale = m.sb("scale", [P, 2, D])
        wr = m.sb("wr", [128, K, NE1])
        br = m.sb("br", [P, NE1])
        score = m.sb("score", [P, J, NE1])
        t = m.sb("t", [P, J, NE1, 4])
        big = m.sb("big", [P, J, NE1, NE1])
        tri = m.sb("tri", [P, NE1 * NE1])
        exp_in = m.sb("exp_in", [P, J, NE1])
        exp_out = m.sb("exp_out", [P, J, NE1])
        ps_turn = [m.ps(f"ps_turn{i}", [128, 512]) for i in range(2)]
        ps_r = m.ps("ps_r", [P, J * NE1])
        w_in, var_ready, std_ready, xl_ready = (m.sem(n) for n in ("w_in", "var_ready", "std_ready", "xl_ready"))
        turned, turn_free, summed, gate_in, gate_out, chain = (
            m.sem(n) for n in ("turned", "turn_free", "summed", "gate_in", "gate_out", "chain"))
        with nc.Block() as block:

            @block.sync
            def _(sp):
                sp.dma_start(wr[:], io["L1_ffn_Wr"].rearrange("(k p) e -> p k e", p=128)).then_inc(w_in, 16)
                sp.dma_start(br[:], io["L1_ffn_br"].unsqueeze(0).broadcast_to([P, NE1])).then_inc(w_in, 16)
                sp.dma_start(scale[:, 0, :], io["L1_ffn_gamma"].unsqueeze(0).broadcast_to([P, D])).then_inc(w_in, 16)
                sp.dma_start(scale[:, 1, :], io["L1_ffn_beta"].unsqueeze(0).broadcast_to([P, D])).then_inc(w_in, 16)

            @block.scalar
            def _(act):
                for i in range(2):
                    act.wait_ge(var_ready, i + 1)
                    act.activation(std[:, i, :], small[:, 2, :], ACT.Sqrt).then_inc(std_ready, 1)
                copy_turned(act, act.copy, c, ps_turn, turn_free, turned, 0)
                act.wait_ge(gate_in, 1)
                act.activation(exp_out[:], exp_in[:], ACT.Exp).then_inc(gate_out, 1)

            @block.tensor
            def _(pe):
                pe.wait_ge(xl_ready, 1)
                transpose_nodes(pe, c, ps_turn, None, turn_free, turned, 0)
                pe.wait_ge(turn_free, TURNS)
                pe.wait_ge(w_in, 64)
                for j in range(J):
                    for k in range(K):
                        ins = pe.matmul(ps_r[:, j * NE1:(j + 1) * NE1], c.xt[:, k, j * P:(j + 1) * P], wr[:, k, :],
                                        start=(k == 0), stop=(k == K - 1))
                ins.then_inc(summed, 1)

            @block.vector
            def _(v):
                link = Link(v, chain)
                layernorm_stats(v, link, c.x, st, small, std[:, 0, :], var_ready, 1, std_ready)
                layernorm_apply(v, link, c.xl, c.x, small)
                layernorm_stats(v, link, c.xl, st, small, std[:, 1, :], var_ready, 2, std_ready)
                layernorm_apply(v, link, c.xl, c.xl, small)
                v.wait_ge(w_in, 64)
                link(v.tensor_tensor(c.xl[:], c.xl[:], spread(scale[:, 0, :], 1, [P, J, D]), ALU.mult))
                link(v.tensor_tensor(c.xl[:], c.xl[:], spread(scale[:, 1, :], 1, [P, J, D]), ALU.add))
                v.sem_inc(xl_ready, 1)
                lower_triangle(v, link, c, tri, NE1)
                v.wait_ge(summed, 1)
                link(v.tensor_tensor(score[:], ps_r.rearrange("p (j e) -> p j e", e=NE1), spread(br[:], 1, [P, J, NE1]), ALU.add))
                top2_gates(v, link, score[:], c.gates[:, 0:NE1, :], t[:], big[:], tri[:], exp_in[:], exp_out[:],
                           (gate_in, gate_out, 1))


def store_x(nc, c, io):
    with ExitStack() as ctx:
        m = Memory(nc, ctx, "store_x_")
        stored = m.sem("stored")
        with nc.Block() as block:

            @block.sync
            def _(sp):
                sp.dma_start(io["out"].rearrange("(w d) f -> d w f", d=P), c.x[:]).then_inc(stored, 16)
                sp.wait_ge(stored, 16)


class Common:
    pass


def program(nc, io, stages=4):
    with ExitStack() as ctx:
        m = Memory(nc, ctx)
        c = Common()
        c.x = m.sb("x_nodes", [P, J, D])
        c.xl_all = m.sb("xl_nodes", [128, J, D])
        c.xl = c.xl_all[0:P, :, :]
        c.row = m.sb("row", [128, N])
        c.row_b = m.sb("row_b", [128, 128], BF16)
        c.col = m.sb("col", [128, 1])
        c.ident = m.sb("ident", [128, 128])
        c.ones = m.sb("ones", [128, 128])
        c.zeros_b = m.sb("zeros_b", [128, 128], BF16)
        c.hi_line_dram = nc.dram_tensor("hi_line_dram", [E1], BF16, kind="Internal").ap()
        c.hi_line_dram2 = nc.dram_tensor("hi_line_dram2", [E2], BF16, kind="Internal").ap()
        c.hi_line_dram3 = nc.dram_tensor("hi_line_dram3", [I4 * 128 * Q1], BF16, kind="Internal").ap()
        c.w_dram = nc.dram_tensor("w_dram", [I4 * 128], I32, kind="Internal").ap()
        c.edge_table = nc.dram_tensor("edge_table", [E1], F32, kind="Internal").ap()
        c.x_table = nc.dram_tensor("x_table", [N, D], F32, kind="Internal").ap()
        c.z_table = nc.dram_tensor("z_table", [N, ZF], F32, kind="Internal").ap()
        c.deg = m.sb("deg_nodes", [P, J])
        c.ad_nodes = m.sb("ad_nodes", [P, J])
        c.h_table = nc.dram_tensor("h_table", [N, HF], F32, kind="Internal").ap()
        c.h = m.sb("h_nodes", [P, J, HF])
        c.a_dst = m.sb("a_dst", [P, J, HEADS])
        c.most_of = m.sb("most_of", [128, HEADS])
        c.most = m.sb("most", [128, HEADS])
        c.gates = m.sb("gates", [P, 8, J])
        constants(nc, c)
        block_gcn(nc, c, io)
        with ExitStack() as inner:
            c.xt = Memory(nc, inner).sb("xt_nodes", [128, K, N])
            block_gat_tables(nc, c, io)
            block_gat_edges(nc, c, io)
            block_experts(nc, c, io, "L0_ffn", NE0, c.edge_table)
            block_z(nc, c, io)
        block_windows(nc, c, io)
        with ExitStack() as inner:
            c.xt = Memory(nc, inner).sb("xt_windows", [128, K, N])
            block_router(nc, c, io)
            block_experts(nc, c, io, "L1_ffn", NE1, None)
        store_x(nc, c, io)


_INS = ['x', 'src', 'dst', 'edge_attr_64', 'L0_gnn_w1', 'L0_gnn_b1', 'L0_gnn_w2', 'L0_gnn_b2', 'L0_gnn_gcn_w',
        'L0_gnn_gcn_b', 'L0_ffn_W_gat', 'L0_ffn_att_src', 'L0_ffn_att_dst', 'L0_ffn_b_gat', 'L0_ffn_ln_gamma',
        'L0_ffn_ln_beta', 'L0_ffn_W1', 'L0_ffn_b1', 'L0_ffn_W2', 'L0_ffn_b2', 'L0_ffn_edge_index', 'L1_gnn_W',
        'L1_gnn_A', 'L1_ffn_gamma', 'L1_ffn_beta', 'L1_ffn_Wr', 'L1_ffn_br', 'L1_ffn_W1', 'L1_ffn_b1', 'L1_ffn_W2',
        'L1_ffn_b2']


def kernel(**inputs):
    import numpy as _np
    import concourse.bacc as _bacc
    from concourse import mybir as _mybir
    from concourse.bass_utils import run_bass_kernel_spmd as _run

    nc = _bacc.Bacc("TRN2", target_bir_lowering=False, num_devices=1)
    arrays, io = {}, {}
    for name in _INS:
        a = _np.ascontiguousarray(inputs[name])
        arrays[f"in_{name}_dram"] = a
        io[name] = nc.dram_tensor(f"in_{name}_dram", a.shape, _mybir.dt.from_np(a.dtype), kind="ExternalInput").ap()
    io["out"] = nc.dram_tensor("out_dram", (N, D), F32, kind="ExternalOutput").ap()
    program(nc, io)
    r = _run(nc, [arrays], core_ids=[0])
    return r.results[0]["out_dram"]
```

```python
from contextlib import ExitStack

import concourse.bass as bass
from concourse import mybir

F32 = mybir.dt.float32
BF16 = mybir.dt.bfloat16
I32 = mybir.dt.int32
ALU = mybir.AluOpType
ACT = mybir.ActivationFunctionType
AX_X = mybir.AxisListType.X

N = 3125
P = 125
J = N // P
D = 256
K = D // 128
E1 = 50000
Q1 = 125
T1 = E1 // Q1
R1 = 100
C1 = T1 // R1
G1 = 20
B1 = T1 // G1
NE0 = 4
HEADS = 4
HX = HEADS * NE0
HF = HX + HEADS
E2 = 32768
Q2 = 128
T2 = E2 // Q2
R2 = 128
C2 = T2 // R2
G2 = 8
B2 = T2 // G2
U2 = 16
NE1 = 8
FE = 64
ZF = D + 3
UW = 8
SW = 4
ITEMS = T1 + J - 1
GW = ITEMS // UW
I4 = -(-ITEMS // 128)
IP = 2 * G1 * -(-ITEMS // (2 * G1))
XS = 4
ROUND = 12582912.0
EPS = 1e-5
BN = 6


class Link:

    def __init__(self, eng, sem):
        self.eng, self.sem, self.n = eng, sem, 0

    def __call__(self, ins, n=1):
        ins.then_inc(self.sem, 1)
        self.n += n
        self.eng.wait_ge(self.sem, self.n)

    def at(self, ins, n):
        ins.then_inc(self.sem, 1)
        self.eng.wait_ge(self.sem, n + self.n)

    def loop_end(self, steps):
        self.n += steps


def spread(ap, axis, shape):
    return ap.unsqueeze(axis).broadcast_to(shape)


class Memory:
    def __init__(self, nc, ctx, prefix=""):
        self.nc, self.ctx, self.prefix, self.sems = nc, ctx, prefix, []
        ctx.callback(self.clear)

    def clear(self):
        if self.sems:
            self.nc.clear_and_free_semaphores(self.sems)
            self.nc.all_engine_barrier()

    def sb(self, name, shape, dt=F32):
        return self.ctx.enter_context(self.nc.sbuf_tensor(self.prefix + name, shape, dt))

    def ps(self, name, shape, dt=F32):
        return self.ctx.enter_context(self.nc.psum_tensor(self.prefix + name, shape, dt))

    def sem(self, name):
        self.sems.append(self.nc.alloc_semaphore(self.prefix + name))
        return self.sems[-1]


def layernorm_stats(v, link, x, st, small, std, var_ready, n_var, std_ready):
    with v.Fori(0, J) as j:
        v.bn_stats(st[:, bass.ds(j, 1), :].squeeze(1), x[:, bass.ds(j, 1), :].squeeze(1)).then_inc(link.sem, 1)
    link.loop_end(J)
    v.wait_ge(link.sem, link.n)
    mean, rstd, a, b, c = (small[:, i, :] for i in range(5))
    link(v.tensor_tensor(a, st[:, :, 1], st[:, :, 4], ALU.add))
    link(v.tensor_scalar(mean, a, 0.5, None, ALU.mult))
    link(v.tensor_tensor(b, st[:, :, 1], st[:, :, 4], ALU.subtract))
    link(v.tensor_tensor(b, b, b, ALU.mult))
    link(v.tensor_tensor(c, st[:, :, 2], st[:, :, 5], ALU.add))
    link(v.scalar_tensor_tensor(c, b, D / 4.0, c, ALU.mult, ALU.add))
    v.tensor_scalar(a, c, 1.0 / D, EPS, ALU.mult, ALU.add).then_inc(var_ready, 1)
    v.wait_ge(std_ready, n_var)
    link(v.reciprocal(rstd, std))


def layernorm_apply(v, link, xl, x, small):
    with v.Fori(0, J) as j:
        v.tensor_scalar(xl[:, bass.ds(j, 1), :].squeeze(1), x[:, bass.ds(j, 1), :].squeeze(1),
                        small[:, 0, bass.ds(j, 1)], small[:, 1, bass.ds(j, 1)],
                        ALU.subtract, ALU.mult).then_inc(link.sem, 1)
    link.loop_end(J)
    v.wait_ge(link.sem, link.n)


def three_parts(v, link, parts, rest, value):
    link(v.tensor_copy(parts[0], value))
    link(v.tensor_tensor(rest, value, parts[0], ALU.subtract))
    link(v.tensor_copy(parts[1], rest))
    link(v.tensor_tensor(rest, rest, parts[1], ALU.subtract))
    link(v.tensor_copy(parts[2], rest))


def constants(nc, c):
    with ExitStack() as ctx:
        m = Memory(nc, ctx, "constants_")
        row_i = m.sb("row_i", [128, N], I32)
        col_i = m.sb("col_i", [128, 1], I32)
        iotas = m.sem("iotas")
        chain = m.sem("const_chain")
        with nc.Block() as block:

            @block.gpsimd
            def _(pool):
                pool.iota(row_i[:], pattern=[[1, N]], base=0, channel_multiplier=0).then_inc(iotas, 1)
                pool.iota(col_i[:], pattern=[[0, 1]], base=0, channel_multiplier=1).then_inc(iotas, 1)

            @block.vector
            def _(v):
                link = Link(v, chain)
                v.wait_ge(iotas, 2)
                link(v.tensor_copy(c.row[:], row_i[:]))
                link(v.tensor_copy(c.col[:], col_i[:]))
                link(v.tensor_copy(c.row_b[:], c.row[:, 0:128]))
                link(v.tensor_scalar(c.ident[:], c.row[:, 0:128], c.col[:, 0:1], None, ALU.is_equal))
                link(v.memset(c.ones[:], 1.0))
                link(v.memset(c.zeros_b[:], 0.0))


def block_gcn(nc, c, io):
    with ExitStack() as ctx:
        m = Memory(nc, ctx, "gcn_")
        rows_i = m.sb("rows_i", [R1, 2, C1, Q1], I32)
        rows_f = m.sb("rows_f", [R1, 2, C1, Q1])
        rows_hi = m.sb("rows_hi", [R1, 2, C1, Q1])
        rows_lo = m.sb("rows_lo", [R1, 2, C1, Q1])
        rows_hi_b = m.sb("rows_hi_b", [R1, C1, Q1], BF16)
        dst_hi = m.sb("dst_hi", [Q1, T1], BF16)
        lo = m.sb("lo", [Q1, 2, T1], BF16)
        lo_hot = m.sb("lo_hot", [Q1, 2, T1, J], BF16)
        hi_line = m.sb("hi_line", [P, 2, G1 * Q1], BF16)
        hi_hot_t = m.sb("hi_hot_t", [P, 2, G1 * Q1], BF16)
        hi_hot = m.sb("hi_hot", [Q1, 2, G1, P], BF16)
        found = m.sb("found", [Q1, G1, J])
        val = m.sb("val", [Q1, G1])
        val_rest = m.sb("val_rest", [Q1, G1])
        val_b = m.sb("val_b", [Q1, 3, G1], BF16)
        payload = m.sb("payload", [Q1, 2, G1, 3, J], BF16)
        st = m.sb("st", [P, J, BN])
        small = m.sb("small", [P, 5, J])
        std = m.sb("std", [P, 2, J])
        gcn_w = m.sb("gcn_w", [P, D])
        gcn_b = m.sb("gcn_b", [P, 1])
        prod = m.sb("prod", [P, J, D])
        h = m.sb("h", [P, J])
        deg = m.sb("deg", [P, J])
        dis = m.sb("dis", [P, J])
        hd = m.sb("hd", [P, J])
        hd_rest = m.sb("hd_rest", [P, J])
        hd_b = m.sb("hd_b", [P, 3, J], BF16)
        sums = m.sb("sums", [P, 3, J])
        spa = m.sb("spa", [P, J])
        w1 = m.sb("w1", [128, K, 128])
        w2 = m.sb("w2", [128, D])
        b1 = m.sb("b1", [128, 1])
        b2 = m.sb("b2", [1, D])
        mean = m.sb("mean", [128, K])
        hidden = m.sb("hidden", [128, 1])
        hidden_row = m.sb("hidden_row", [128, P])
        gate1 = m.sb("gate1", [P, D])
        zeros = m.sb("zeros", [128, D])

        turned = [m.ps(f"turned{i}", [Q1, T1]) for i in range(3)]
        looked = [m.ps(f"looked{i}", [Q1, G1 * J]) for i in range(2)]
        ps_deg = m.ps("ps_deg", [P, J])
        ps_sum = m.ps("ps_sum", [P, 3 * J])
        ps_gate = m.ps("ps_gate", [128, D + 8])

        x_in, edges_in, gcn_in, gate_in = (m.sem(n) for n in ("x_in", "edges_in", "gcn_in", "gate_in"))
        hi_ready, hi_out = m.sem("hi_ready"), m.sem("hi_out")
        line_in = [m.sem(f"line_in{i}") for i in range(2)]
        ids_ready, ids_turned = m.sem("ids_ready"), m.sem("ids_turned")
        var_ready, std_ready = m.sem("var_ready"), m.sem("std_ready")
        xl_ready, mean_sum, mean_ready = m.sem("xl_ready"), m.sem("mean_sum"), m.sem("mean_ready")
        hidden_sum, hidden_ready = m.sem("hidden_sum"), m.sem("hidden_ready")
        gate_sum, gate_ready = m.sem("gate_sum"), m.sem("gate_ready")
        hot_ready, hot_free = m.sem("hot_ready"), m.sem("hot_free")
        deg_summed = m.sem("deg_summed")
        hot_t_ready, looked_up, looked_free = m.sem("hot_t_ready"), m.sem("looked_up"), m.sem("looked_free")
        payload_ready, all_summed = m.sem("payload_ready"), m.sem("all_summed")
        spa_in, spa_ready = m.sem("spa_in"), m.sem("spa_ready")
        zeroed, table_out = m.sem("zeroed"), m.sem("table_out")
        chain = m.sem("gcn_chain")
        with nc.Block() as block:

            @block.sync
            def _(sp):
                sp.dma_start(rows_i[:, 0, :, :], io["src"].rearrange("(c r q) -> r c q", r=R1, q=Q1)).then_inc(edges_in, 16)
                sp.dma_start(rows_i[:, 1, :, :], io["dst"].rearrange("(c r q) -> r c q", r=R1, q=Q1)).then_inc(edges_in, 16)
                sp.dma_start(c.x[:], io["x"].rearrange("(p j) d -> p j d", j=J)).then_inc(x_in, 16)
                sp.dma_start(gcn_w[:], io["L0_gnn_gcn_w"].rearrange("d o -> o d").broadcast_to([P, D])).then_inc(gcn_in, 16)
                sp.dma_start(gcn_b[:], io["L0_gnn_gcn_b"].unsqueeze(0).broadcast_to([P, 1])).then_inc(gcn_in, 16)
                sp.dma_start(w1[:], io["L0_gnn_w1"].rearrange("(k p) r -> p k r", p=128)).then_inc(gate_in, 16)
                sp.dma_start(w2[:], io["L0_gnn_w2"]).then_inc(gate_in, 16)
                sp.dma_start(b1[:], io["L0_gnn_b1"].unsqueeze(1)).then_inc(gate_in, 16)
                sp.dma_start(b2[:], io["L0_gnn_b2"].unsqueeze(0)).then_inc(gate_in, 16)
                sp.wait_ge(hi_ready, 1)
                sp.dma_start(c.hi_line_dram.rearrange("(c r q) -> r c q", r=R1, q=Q1), rows_hi_b[:]).then_inc(hi_out, 16)
                sp.wait_ge(hi_out, 16)
                lines = c.hi_line_dram.rearrange("(b e) -> b e", e=G1 * Q1)
                for s in range(2):
                    sp.dma_start(hi_line[:, s, :], lines[s:s + 1, :].broadcast_to([P, G1 * Q1])).then_inc(line_in[s], 16)
                with sp.Fori(1, B1 // 2) as b:
                    for s in range(2):
                        sp.wait_ge(hot_t_ready, b * 2 + (s - 1))
                        sp.dma_start(hi_line[:, s, :], lines[bass.ds(b * 2 + s, 1), :].broadcast_to([P, G1 * Q1])).then_inc(line_in[s], 16)

            @block.gpsimd
            def _(pool):
                pool.memset(zeros[:], 0.0).then_inc(zeroed, 1)
                pool.wait_ge(zeroed, 1)
                pool.wait_ge(xl_ready, 1)
                pool.dma_start(c.slot_table.rearrange("(t p) d -> p t d", p=128),
                               spread(zeros[:], 1, [128, c.slot_table.shape[0] // 128, D])).then_inc(table_out, 16)
                pool.wait_ge(table_out, 16)

            @block.scalar
            def _(act):
                act.wait_ge(var_ready, 1)
                act.activation(std[:, 0, :], small[:, 2, :], ACT.Sqrt).then_inc(std_ready, 1)
                act.wait_ge(var_ready, 2)
                act.activation(std[:, 1, :], deg[:], ACT.Sqrt).then_inc(std_ready, 1)
                act.wait_ge(gate_sum, 1)
                act.activation(gate1[:], ps_gate[0:P, 0:D], ACT.Sigmoid).then_inc(gate_ready, 1)
                act.wait_ge(spa_in, 1)
                act.activation(spa[:], hd_rest[:], ACT.Sigmoid).then_inc(spa_ready, 1)

            @block.tensor
            def _(pe):
                pe.wait_ge(ids_ready, 1)
                for i, rows in enumerate((rows_hi[:, 1, :, :], rows_lo[:, 0, :, :], rows_lo[:, 1, :, :])):
                    for b in range(C1):
                        ins = pe.transpose(turned[i][:, b * R1:(b + 1) * R1], rows[:, b, :], c.ident[0:R1, 0:R1])
                ins.then_inc(ids_turned, 1)
                pe.wait_ge(xl_ready, 1)
                for k in range(K):
                    for j in range(J):
                        ins = pe.matmul(ps_gate[:, D + k:D + k + 1], c.xl[:, j, k * 128:(k + 1) * 128],
                                        c.ones[0:P, 0:1], start=(j == 0), stop=(j == J - 1))
                ins.then_inc(mean_sum, 1)
                pe.matmul(ps_deg[:], c.zeros_b[0:Q1, 0:P], c.zeros_b[0:Q1, 0:J], start=True, stop=False, skip_group_check=True)
                with pe.Fori(0, B1 // 2) as b:
                    for s in range(2):
                        pe.wait_ge(hot_ready, b * 2 + (s + 1))
                        for g in range(G1):
                            ins = pe.matmul(ps_deg[:], hi_hot[:, s, g, :],
                                            lo_hot[:, 1, bass.ds(b * (2 * G1) + (s * G1 + g), 1), :].squeeze(1),
                                            start=False, stop=False, skip_group_check=True)
                        ins.then_inc(hot_free, 1)
                pe.matmul(ps_deg[:], c.zeros_b[0:Q1, 0:P], c.zeros_b[0:Q1, 0:J], start=False, stop=True,
                          skip_group_check=True).then_inc(deg_summed, 1)
                pe.wait_ge(mean_ready, 1)
                pe.wait_ge(gate_in, 64)
                for k in range(K):
                    ins = pe.matmul(ps_gate[:, D + 4:D + 5], w1[:, k, :], mean[:, k:k + 1], start=(k == 0), stop=(k == K - 1))
                ins.then_inc(hidden_sum, 1)
                pe.wait_ge(hidden_ready, 1)
                pe.matmul(ps_gate[0:P, 0:D], hidden_row[:], w2[:], start=True, stop=False)
                pe.matmul(ps_gate[0:P, 0:D], c.ones[0:1, 0:P], b2[:], start=False, stop=True).then_inc(gate_sum, 1)
                pe.matmul(ps_sum[:], c.zeros_b[0:Q1, 0:P], c.zeros_b[0:Q1, 0:3 * J], start=True, stop=False, skip_group_check=True)

                def look(i, s):
                    pe.wait_ge(hot_t_ready, i + 1)
                    pe.wait_ge(looked_free, i + 1)
                    for g in range(G1):
                        for part in range(3):
                            ins = pe.matmul(looked[s][:, g * J:(g + 1) * J], hi_hot_t[:, s, g * Q1:(g + 1) * Q1],
                                            hd_b[:, part, :], start=(part == 0), stop=(part == 2))
                    ins.then_inc(looked_up, 1)

                def add_up(i, s):
                    pe.wait_ge(payload_ready, i + 1)
                    for g in range(G1):
                        ins = pe.matmul(ps_sum[:], hi_hot[:, s, g, :], payload[:, s, g, :, :],
                                        start=False, stop=False, skip_group_check=True)
                    ins.then_inc(hot_free, 1)

                look(0, 0)
                with pe.Fori(0, B1 // 2 - 1) as b:
                    for s in range(2):
                        look(b * 2 + (s + 1), (s + 1) % 2)
                        add_up(b * 2 + s, s)
                look(B1 - 1, 1)
                add_up(B1 - 2, 0)
                add_up(B1 - 1, 1)
                pe.matmul(ps_sum[:], c.zeros_b[0:Q1, 0:P], c.zeros_b[0:Q1, 0:3 * J], start=False, stop=True,
                          skip_group_check=True).then_inc(all_summed, 1)

            @block.vector
            def _(v):
                link = Link(v, chain)
                v.sem_inc(hot_free, 2)
                v.sem_inc(looked_free, 2)
                v.wait_ge(edges_in, 32)
                link(v.tensor_copy(rows_f[:], rows_i[:]))
                link(v.tensor_scalar(rows_hi[:], rows_f[:], -float(J // 2), 1.0 / J, ALU.add, ALU.mult))
                link(v.tensor_scalar(rows_hi[:], rows_hi[:], ROUND, -ROUND, ALU.add, ALU.add))
                v.tensor_copy(rows_hi_b[:], rows_hi[:, 0, :, :]).then_inc(hi_ready, 1)
                v.scalar_tensor_tensor(rows_lo[:], rows_hi[:], -float(J), rows_f[:], ALU.mult, ALU.add).then_inc(ids_ready, 1)
                v.wait_ge(x_in, 16)
                layernorm_stats(v, link, c.x, st, small, std[:, 0, :], var_ready, 1, std_ready)
                layernorm_apply(v, link, c.xl, c.x, small)
                v.sem_inc(xl_ready, 1)
                v.wait_ge(ids_turned, 1)
                link(v.tensor_copy(dst_hi[:], turned[0][:]))
                link(v.tensor_copy(lo[:, 0, :], turned[1][:]))
                link(v.tensor_copy(lo[:, 1, :], turned[2][:]))
                for i in range(2):
                    link(v.tensor_tensor(lo_hot[:, i, :, :], spread(lo[:, i, :], 2, [Q1, T1, J]),
                                         spread(c.row_b[0:Q1, 0:J], 1, [Q1, T1, J]), ALU.is_equal))

                def hot(b, s):
                    v.tensor_tensor(hi_hot[:, s, :, :], spread(dst_hi[:, bass.ds(b * (2 * G1) + s * G1, G1)], 2, [Q1, G1, P]),
                                    spread(c.row_b[0:Q1, 0:P], 1, [Q1, G1, P]), ALU.is_equal).then_inc(hot_ready, 1)

                with v.Fori(0, B1 // 2) as b:
                    for s in range(2):
                        v.wait_ge(hot_free, b * 2 + (s + 1))
                        hot(b, s)
                v.wait_ge(gcn_in, 32)
                link(v.tensor_tensor(prod[:], c.xl[:], spread(gcn_w[:], 1, [P, J, D]), ALU.mult))
                link(v.tensor_reduce(h[:], prod[:], AX_X, ALU.add))
                v.wait_ge(mean_sum, 1)
                v.tensor_scalar(mean[:], ps_gate[:, D:D + K], 1.0 / N, None, ALU.mult).then_inc(mean_ready, 1)
                v.wait_ge(deg_summed, 1)
                link(v.tensor_copy(c.deg[:], ps_deg[:]))
                v.tensor_scalar(deg[:], ps_deg[:], 1.0, None, ALU.add).then_inc(var_ready, 1)
                v.wait_ge(std_ready, 2)
                link(v.reciprocal(dis[:], std[:, 1, :]))
                link(v.tensor_tensor(hd[:], h[:], dis[:], ALU.mult))
                three_parts(v, link, [hd_b[:, i, :] for i in range(3)], hd_rest[:], hd[:])
                v.wait_ge(hidden_sum, 1)
                link(v.tensor_scalar(hidden[:], ps_gate[:, D + 4:D + 5], b1[:], 0.0, ALU.add, ALU.max))
                v.tensor_copy(hidden_row[:], hidden[:, 0:1].broadcast_to([128, P])).then_inc(hidden_ready, 1)

                def compare(b, i, s):
                    v.wait_ge(line_in[s], b * 16 + 16)
                    v.tensor_scalar(hi_hot_t[:, s, :], hi_line[:, s, :], c.col[0:P, 0:1], None,
                                    ALU.is_equal).then_inc(hot_t_ready, 1)

                def payloads(i, s):
                    v.wait_ge(hot_free, i + (B1 + 1))
                    now = slice(i * G1, (i + 1) * G1) if isinstance(i, int) else bass.ds(i * G1, G1)
                    v.tensor_tensor(hi_hot[:, s, :, :], spread(dst_hi[:, now], 2, [Q1, G1, P]),
                                    spread(c.row_b[0:Q1, 0:P], 1, [Q1, G1, P]), ALU.is_equal)
                    v.wait_ge(looked_up, i + 1)
                    v.tensor_tensor(found[:], looked[s].rearrange("q (g j) -> q g j", j=J), lo_hot[:, 0, now, :],
                                    ALU.mult).then_inc(looked_free, 1)
                    v.wait_ge(looked_free, i + 3)
                    link.at(v.tensor_reduce(val[:], found[:], AX_X, ALU.add), i * 6 + 1)
                    link.at(v.tensor_copy(val_b[:, 0, :], val[:]), i * 6 + 2)
                    link.at(v.tensor_tensor(val_rest[:], val[:], val_b[:, 0, :], ALU.subtract), i * 6 + 3)
                    link.at(v.tensor_copy(val_b[:, 1, :], val_rest[:]), i * 6 + 4)
                    link.at(v.tensor_tensor(val_rest[:], val_rest[:], val_b[:, 1, :], ALU.subtract), i * 6 + 5)
                    link.at(v.tensor_copy(val_b[:, 2, :], val_rest[:]), i * 6 + 6)
                    for part in range(3):
                        ins = v.tensor_tensor(payload[:, s, :, part, :], lo_hot[:, 1, now, :],
                                              spread(val_b[:, part, :], 2, [Q1, G1, J]), ALU.mult)
                    ins.then_inc(payload_ready, 1)

                compare(0, 0, 0)
                with v.Fori(0, B1 // 2 - 1) as b:
                    compare(b, b * 2 + 1, 1)
                    payloads(b * 2, 0)
                    compare(b + 1, b * 2 + 2, 0)
                    payloads(b * 2 + 1, 1)
                compare(B1 // 2 - 1, B1 - 1, 1)
                payloads(B1 - 2, 0)
                payloads(B1 - 1, 1)
                link.loop_end(6 * B1)
                v.wait_ge(all_summed, 1)
                link(v.tensor_copy(sums[:], ps_sum.rearrange("p (i j) -> p i j", j=J)))
                link(v.tensor_tensor(sums[:, 1, :], sums[:, 1, :], sums[:, 2, :], ALU.add))
                link(v.tensor_tensor(sums[:, 0, :], sums[:, 0, :], sums[:, 1, :], ALU.add))
                link(v.tensor_tensor(sums[:, 0, :], sums[:, 0, :], hd[:], ALU.add))
                link(v.tensor_tensor(sums[:, 0, :], sums[:, 0, :], dis[:], ALU.mult))
                v.tensor_scalar(hd_rest[:], sums[:, 0, :], gcn_b[:], None, ALU.add).then_inc(spa_in, 1)
                v.wait_ge(gate_ready, 1)
                link(v.tensor_scalar(gate1[:], gate1[:], 1.0, None, ALU.add))
                v.wait_ge(spa_ready, 1)
                with v.Fori(0, J) as j:
                    v.scalar_tensor_tensor(prod[:, bass.ds(j, 1), :].squeeze(1), gate1[:], spa[:, bass.ds(j, 1)],
                                           c.xl[:, bass.ds(j, 1), :].squeeze(1), ALU.add, ALU.mult).then_inc(chain, 1)
                link.loop_end(J)
                v.wait_ge(chain, link.n)
                link(v.tensor_tensor(c.x[:], c.x[:], prod[:], ALU.add))


def transpose_nodes(pe, c, ps, xl_waited, ps_free, turned, first):
    i = 0
    for k in range(K):
        for j0 in range(0, J, 4):
            js = range(j0, min(j0 + 4, J))
            if i >= 2:
                pe.wait_ge(ps_free, first + i - 1)
            for j in js:
                ins = pe.transpose(ps[i % 2][:, (j - j0) * P:(j - j0 + 1) * P], c.xl[:, j, k * 128:(k + 1) * 128],
                                   c.ident[0:P, 0:P])
            ins.then_inc(turned, 1)
            i += 1


def copy_turned(eng, copy, c, ps, ps_free, turned, first):
    i = 0
    for k in range(K):
        for j0 in range(0, J, 4):
            n = min(4, J - j0) * P
            eng.wait_ge(turned, first + i + 1)
            copy(c.xt[:, k, j0 * P:j0 * P + n], ps[i % 2][:, 0:n]).then_inc(ps_free, 1)
            i += 1


TURNS = K * ((J + 3) // 4)


def top2_gates(v, link, s, gates, chosen, t, big, tri, exp_in, exp_out, n_exp):
    e = s.shape[2]
    s_i = spread(s, 3, [P, J, e, e])
    s_k = spread(s, 2, [P, J, e, e])
    rank, top, rsum = t[:, :, :, 0], t[:, :, 0, 1], t[:, :, 0, 2]
    link(v.tensor_tensor(big, s_k, s_i, ALU.is_equal))
    link(v.tensor_tensor(big.rearrange("p j i k -> p j (i k)"), big.rearrange("p j i k -> p j (i k)"),
                         spread(tri, 1, [P, J, e * e]), ALU.mult))
    link(v.tensor_reduce(rank, big, AX_X, ALU.add))
    link(v.tensor_tensor(big, s_k, s_i, ALU.is_gt))
    link(v.tensor_reduce(t[:, :, :, 3], big, AX_X, ALU.add))
    link(v.tensor_tensor(rank, rank, t[:, :, :, 3], ALU.add))
    link(v.tensor_scalar(rank, rank, 2.0, None, ALU.is_lt))
    link(v.tensor_copy(chosen.rearrange("p e j -> p j e"), rank))
    link(v.tensor_reduce(top, s, AX_X, ALU.max))
    v.tensor_tensor(exp_in, s, spread(top, 2, [P, J, e]), ALU.subtract).then_inc(n_exp[0], 1)
    v.wait_ge(n_exp[1], n_exp[2])
    link(v.tensor_tensor(exp_out, exp_out, rank, ALU.mult))
    link(v.tensor_reduce(rsum, exp_out, AX_X, ALU.add))
    link(v.reciprocal(rsum, rsum))
    link(v.tensor_tensor(gates.rearrange("p e j -> p j e"), exp_out, spread(rsum, 2, [P, J, e]), ALU.mult))


def block_gat_tables(nc, c, io):
    with ExitStack() as ctx:
        m = Memory(nc, ctx, "gat_tables_")
        st = m.sb("st", [P, J, BN])
        small = m.sb("small", [P, 5, J])
        std = m.sb("std", [P, J])
        w_gat = m.sb("w_gat", [128, K, HX])
        att = m.sb("att", [P, 2, HX])
        prod = m.sb("prod", [P, J, HX])
        ps_turn = [m.ps(f"ps_turn{i}", [128, 512]) for i in range(2)]
        ps_h = m.ps("ps_h", [P, J * HX])
        w_in, var_ready, std_ready = m.sem("w_in"), m.sem("var_ready"), m.sem("std_ready")
        xl_ready, turned, turn_free = m.sem("xl_ready"), m.sem("turned"), m.sem("turn_free")
        h_summed, table_ready, table_out = m.sem("h_summed"), m.sem("table_ready"), m.sem("table_out")
        lowest, most_in, most_out = m.sem("lowest"), m.sem("most_in"), m.sem("most_out")
        chain = m.sem("tab_chain")
        with nc.Block() as block:

            @block.sync
            def _(sp):
                sp.dma_start(w_gat[:], io["L0_ffn_W_gat"].rearrange("(k p) r -> p k r", p=128)).then_inc(w_in, 16)
                for i, name in enumerate(("L0_ffn_att_src", "L0_ffn_att_dst")):
                    sp.dma_start(att[:, i, :], io[name].rearrange("h e -> (h e)").unsqueeze(0).broadcast_to([P, HX])).then_inc(w_in, 16)
                sp.wait_ge(table_ready, 1)
                sp.dma_start(c.h_table.rearrange("(p j) f -> p j f", j=J), c.h[:]).then_inc(table_out, 16)
                sp.wait_ge(table_out, 16)

            @block.gpsimd
            def _(pool):
                pool.wait_ge(most_in, 1)
                pool.partition_all_reduce(c.most[:], c.most_of[:], 128, bass.bass_isa.ReduceOp.max).then_inc(most_out, 1)

            @block.scalar
            def _(act):
                act.wait_ge(var_ready, 1)
                act.activation(std[:], small[:, 2, :], ACT.Sqrt).then_inc(std_ready, 1)
                copy_turned(act, act.copy, c, ps_turn, turn_free, turned, 0)

            @block.tensor
            def _(pe):
                pe.wait_ge(xl_ready, 1)
                transpose_nodes(pe, c, ps_turn, None, turn_free, turned, 0)
                pe.wait_ge(turn_free, TURNS)
                pe.wait_ge(w_in, 48)
                for j in range(J):
                    for k in range(K):
                        ins = pe.matmul(ps_h[:, j * HX:(j + 1) * HX], c.xt[:, k, j * P:(j + 1) * P], w_gat[:, k, :],
                                        start=(k == 0), stop=(k == K - 1))
                ins.then_inc(h_summed, 1)

            @block.vector
            def _(v):
                link = Link(v, chain)
                layernorm_stats(v, link, c.x, st, small, std[:], var_ready, 1, std_ready)
                layernorm_apply(v, link, c.xl, c.x, small)
                v.sem_inc(xl_ready, 1)
                link(v.memset(c.most_of[:], -3e38))
                v.wait_ge(h_summed, 1)
                v.wait_ge(w_in, 48)
                link(v.tensor_copy(c.h[:, :, 0:HX], ps_h.rearrange("p (j r) -> p j r", r=HX)))
                for i, out in enumerate((c.h[:, :, HX:HF], c.a_dst[:])):
                    link(v.tensor_tensor(prod[:], c.h[:, :, 0:HX], spread(att[:, i, :], 1, [P, J, HX]), ALU.mult))
                    link(v.tensor_reduce(out, prod.rearrange("p j (h e) -> p j h e", e=NE0), AX_X, ALU.add))
                v.sem_inc(table_ready, 1)
                link(v.tensor_reduce(c.most_of[0:P, :], c.h[:, :, HX:HF].rearrange("p j h -> p h j"), AX_X, ALU.max))
                v.sem_inc(most_in, 1)
                v.wait_ge(most_out, 1)


def block_gat_edges(nc, c, io):
    with ExitStack() as ctx:
        m = Memory(nc, ctx, "gat_edges_")
        rows_i = m.sb("rows_i", [R2, 2, C2, Q2], I32)
        rows_f = m.sb("rows_f", [R2, 2, C2, Q2])
        rows_hi = m.sb("rows_hi", [R2, C2, Q2])
        rows_lo = m.sb("rows_lo", [R2, C2, Q2])
        rows_hi_b = m.sb("rows_hi_b", [R2, C2, Q2], BF16)
        dst_hi = m.sb("dst_hi", [Q2, T2])
        dst_lo = m.sb("dst_lo", [Q2, T2], BF16)
        src_i = m.sb("src_i", [Q2, T2], I32)
        lo_hot = m.sb("lo_hot", [Q2, T2, J], BF16)
        hi_line = m.sb("hi_line", [P, 2, G2 * Q2], BF16)
        hi_hot_t = m.sb("hi_hot_t", [P, 2, G2 * Q2], BF16)
        hi_hot = m.sb("hi_hot", [Q2, 2, G2, P])
        payload = m.sb("payload", [Q2, 2, G2, J * HF])
        zero_i = m.sb("zero_i", [128, U2], I32)
        spare_i = m.sb("spare_i", [128, 1], I32)
        stage = m.sb("stage", [Q2, 2, U2], I32)
        spare = m.sb("spare", [Q2, 2])
        ring = m.sb("ring", [Q2, 2, U2, HF])
        rows = m.sb("rows", [Q2, T2, HF])
        a_dst_e = m.sb("a_dst_e", [Q2, T2, HEADS])
        ex = m.sb("ex", [Q2, T2, HEADS])
        cap = m.sb("cap", [Q2, T2, HEADS])
        found = m.sb("found", [Q2, G2, J, HEADS])
        a_rest = m.sb("a_rest", [P, J, HEADS])
        a_b = m.sb("a_b", [P, 3, J, HEADS], BF16)
        own = m.sb("own", [P, 3, J, HEADS])
        agg = m.sb("agg", [P, J, HF])
        params = m.sb("params", [P, 3, HX])
        sq = m.sb("sq", [P, J, HX])
        stat = m.sb("stat", [P, 4, J])
        score = m.sb("score", [P, J, NE0])
        t = m.sb("gate_t", [P, J, NE0, 4])
        big = m.sb("gate_big", [P, J, NE0, NE0])
        tri = m.sb("tri", [P, NE0 * NE0])
        exp_in = m.sb("exp_in", [P, J, NE0])
        exp_out = m.sb("exp_out", [P, J, NE0])
        turned = [m.ps(f"turned{i}", [Q2, T2]) for i in range(2)]
        looked = [m.ps(f"looked{i}", [Q2, 2, 512]) for i in range(2)]
        ps_sum = m.ps("ps_sum", [P, 512])
        names = ("ids_in", "par_in", "hi_ready", "hi_out", "rows_ready", "ids_turned", "src_ready", "staged", "ring_free",
                 "hot_t_ready", "looked_up", "looked_free", "rows_in", "exp_ready", "exp_done", "self_in",
                 "self_done", "payload_ready", "payload_free", "all_summed", "var_ready", "std_ready", "gate_in", "gate_out",
                 "edge_chain", "found_done")
        s_ = {n: m.sem("ge_" + n) for n in names}
        line_in = [m.sem(f"ge_line_in{i}") for i in range(2)]
        gathered = [m.sem(f"ge_gathered{i}") for i in range(2)]
        with nc.Block() as block:

            @block.sync
            def _(sp):
                for i in range(2):
                    sp.dma_start(rows_i[:, i, :, :], io["L0_ffn_edge_index"][i].rearrange("(c r q) -> r c q", r=R2, q=Q2)).then_inc(s_["ids_in"], 16)
                for i, name in enumerate(("L0_ffn_b_gat", "L0_ffn_ln_gamma", "L0_ffn_ln_beta")):
                    sp.dma_start(params[:, i, :], io[name].unsqueeze(0).broadcast_to([P, HX])).then_inc(s_["par_in"], 16)
                sp.wait_ge(s_["hi_ready"], 1)
                sp.dma_start(c.hi_line_dram2.rearrange("(c r q) -> r c q", r=R2, q=Q2), rows_hi_b[:]).then_inc(s_["hi_out"], 16)
                sp.wait_ge(s_["hi_out"], 16)
                lines = c.hi_line_dram2.rearrange("(b e) -> b e", e=G2 * Q2)
                for s in range(2):
                    sp.dma_start(hi_line[:, s, :], lines[s:s + 1, :].broadcast_to([P, G2 * Q2])).then_inc(line_in[s], 16)
                with sp.Fori(1, B2 // 2) as b:
                    for s in range(2):
                        sp.wait_ge(s_["hot_t_ready"], b * 2 + (s - 1))
                        sp.dma_start(hi_line[:, s, :], lines[bass.ds(b * 2 + s, 1), :].broadcast_to([P, G2 * Q2])).then_inc(line_in[s], 16)

            @block.gpsimd
            def _(pool):
                pool.memset(zero_i[:], 0).then_inc(s_["staged"], 1)
                pool.sem_inc(s_["ring_free"], 2)
                pool.wait_ge(s_["src_ready"], 1)
                pool.wait_ge(s_["staged"], 1)
                with pool.Fori(0, T2 // (2 * U2)) as b:
                    for s in range(2):
                        ids = src_i[:, bass.ds(b * (2 * U2) + s * U2, U2)]
                        pool.wait_ge(s_["ring_free"], b * 2 + (s + 1))
                        pool.tensor_tensor(stage[:, s, :], ids, zero_i[:], ALU.add).then_inc(s_["staged"], 1)
                        pool.wait_ge(s_["staged"], b * 2 + (s + 2))
                        pool.tensor_tensor(spare_i[:], zero_i[:, 0:1], zero_i[:, 1:2], ALU.add)
                        for u in range(U2):
                            pool.indirect_dma_start(ring[:, s, u, :], None, c.h_table,
                                                    bass.IndirectOffsetOnAxis(ap=stage[:, s, u:u + 1], axis=0)).then_inc(gathered[s], 16)

            @block.scalar
            def _(act):
                with act.Fori(0, T2 // (2 * U2)) as b:
                    for s in range(2):
                        act.wait_ge(gathered[s], b * (16 * U2) + 16 * U2)
                        act.copy(spare[:, s:s + 1], ring[:, s, 0, 0:1])
                        act.copy(rows[:, bass.ds(b * (2 * U2) + s * U2, U2), :], ring[:, s, :, :]).then_inc(s_["ring_free"], 1)
                act.wait_ge(s_["ring_free"], 2 + T2 // U2)
                act.sem_inc(s_["rows_in"], 1)
                act.wait_ge(s_["self_in"], 1)
                act.activation(own[:, 2, :, :], own[:, 1, :, :], ACT.Exp).then_inc(s_["self_done"], 1)
                act.wait_ge(s_["exp_ready"], 1)
                act.activation(ex[:], cap[:], ACT.Exp).then_inc(s_["exp_done"], 1)
                act.wait_ge(s_["var_ready"], 1)
                act.activation(stat[:, 2, :], stat[:, 1, :], ACT.Sqrt).then_inc(s_["std_ready"], 1)
                act.wait_ge(s_["gate_in"], 1)
                act.activation(exp_out[:], exp_in[:], ACT.Exp).then_inc(s_["gate_out"], 1)

            @block.tensor
            def _(pe):
                pe.wait_ge(s_["rows_ready"], 1)
                for b in range(C2):
                    pe.transpose(turned[0][:, b * R2:(b + 1) * R2], rows_f[:, 0, b, :], c.ident[:])
                for b in range(C2):
                    ins = pe.transpose(turned[1][:, b * R2:(b + 1) * R2], rows_hi[:, b, :], c.ident[:])
                ins.then_inc(s_["ids_turned"], 1)
                pe.wait_ge(s_["src_ready"], 1)
                for b in range(C2):
                    ins = pe.transpose(turned[0][:, b * R2:(b + 1) * R2], rows_lo[:, b, :], c.ident[:])
                ins.then_inc(s_["ids_turned"], 1)
                with pe.Fori(0, B2 // 2) as b:
                    for s in range(2):
                        pe.wait_ge(s_["hot_t_ready"], b * 2 + (s + 1))
                        pe.wait_ge(s_["looked_free"], b * 2 + (s + 1))
                        for g in range(G2):
                            for i in range(3):
                                ins = pe.matmul(looked[s][:, g // 4, (g % 4) * J * HEADS:(g % 4 + 1) * J * HEADS],
                                                hi_hot_t[:, s, g * Q2:(g + 1) * Q2], a_b[:, i, :, :],
                                                start=(i == 0), stop=(i == 2))
                        ins.then_inc(s_["looked_up"], 1)
                pe.matmul(ps_sum[:, 0:J * HF], c.zeros_b[0:Q2, 0:P], c.zeros_b[:, 0:1].broadcast_to([Q2, J * HF]), start=True, stop=False, skip_group_check=True)
                with pe.Fori(0, B2 // 2) as b:
                    for s in range(2):
                        pe.wait_ge(s_["payload_ready"], b * 2 + (s + 1))
                        for g in range(G2):
                            ins = pe.matmul(ps_sum[:, 0:J * HF], hi_hot[:, s, g, :], payload[:, s, g, :],
                                            start=False, stop=False, skip_group_check=True)
                        ins.then_inc(s_["payload_free"], 1)
                pe.matmul(ps_sum[:, 0:J * HF], c.zeros_b[0:Q2, 0:P], c.zeros_b[:, 0:1].broadcast_to([Q2, J * HF]), start=False, stop=True,
                          skip_group_check=True).then_inc(s_["all_summed"], 1)

            @block.vector
            def _(v):
                link = Link(v, s_["edge_chain"])
                v.sem_inc(s_["looked_free"], 2)
                v.sem_inc(s_["payload_free"], 2)
                v.wait_ge(s_["ids_in"], 32)
                link(v.tensor_copy(rows_f[:], rows_i[:]))
                link(v.tensor_scalar(rows_hi[:], rows_f[:, 1, :, :], -float(J // 2), 1.0 / J, ALU.add, ALU.mult))
                link(v.tensor_scalar(rows_hi[:], rows_hi[:], ROUND, -ROUND, ALU.add, ALU.add))
                v.tensor_copy(rows_hi_b[:], rows_hi[:]).then_inc(s_["hi_ready"], 1)
                v.scalar_tensor_tensor(rows_lo[:], rows_hi[:], -float(J), rows_f[:, 1, :, :], ALU.mult, ALU.add).then_inc(s_["rows_ready"], 1)
                v.wait_ge(s_["ids_turned"], 1)
                v.tensor_copy(src_i[:], turned[0][:]).then_inc(s_["src_ready"], 1)
                link(v.tensor_copy(dst_hi[:], turned[1][:]))
                three_parts(v, link, [a_b[:, i, :, :] for i in range(3)], a_rest[:], c.a_dst[:])
                v.wait_ge(s_["ids_turned"], 2)
                link(v.tensor_copy(dst_lo[:], turned[0][:]))
                link(v.tensor_tensor(lo_hot[:], spread(dst_lo[:], 2, [Q2, T2, J]), spread(c.row_b[0:Q2, 0:J], 1, [Q2, T2, J]), ALU.is_equal))
                with v.Fori(0, B2 // 2) as b:
                    for s in range(2):
                        v.wait_ge(line_in[s], b * 16 + 16)
                        v.tensor_scalar(hi_hot_t[:, s, :], hi_line[:, s, :], c.col[0:P, 0:1], None,
                                        ALU.is_equal).then_inc(s_["hot_t_ready"], 1)
                        v.wait_ge(s_["looked_up"], b * 2 + (s + 1))
                        for half in range(2):
                            ins = v.tensor_tensor(found[:, half * 4:half * 4 + 4, :, :],
                                                  looked[s][:, half, 0:4 * J * HEADS].rearrange("q (g j h) -> q g j h", g=4, j=J),
                                                  spread(lo_hot[:, bass.ds(b * (2 * G2) + s * G2 + half * 4, 4), :], 3, [Q2, 4, J, HEADS]), ALU.mult)
                        ins.then_inc(s_["looked_free"], 1)
                        v.wait_ge(s_["looked_free"], b * 2 + (s + 3))
                        v.tensor_reduce(a_dst_e[:, bass.ds(b * (2 * G2) + s * G2, G2), :],
                                        found.rearrange("q g j h -> q g h j"), AX_X, ALU.add).then_inc(s_["found_done"], 1)
                v.wait_ge(s_["found_done"], B2)

                def logits(out, cap_out, a_src, a_dst, shape):
                    most = spread(c.most[0:shape[0], :], 1, shape)
                    link(v.tensor_tensor(out, a_src, a_dst, ALU.add))
                    link(v.scalar_tensor_tensor(out, out, 0.2, out, ALU.mult, ALU.max))
                    link(v.tensor_tensor(cap_out, a_dst, most, ALU.add))
                    link(v.scalar_tensor_tensor(cap_out, cap_out, 0.2, cap_out, ALU.mult, ALU.max))
                    return v.tensor_tensor(cap_out, out, cap_out, ALU.subtract)

                logits(own[:, 0, :, :], own[:, 1, :, :], c.h[:, :, HX:HF], c.a_dst[:], [P, J, HEADS]).then_inc(s_["self_in"], 1)
                v.wait_ge(s_["rows_in"], 1)
                logits(ex[:], cap[:], rows[:, :, HX:HF], a_dst_e[:], [Q2, T2, HEADS]).then_inc(s_["exp_ready"], 1)
                v.wait_ge(s_["exp_done"], 1)
                link(v.tensor_tensor(rows[:, :, 0:HX].rearrange("q t (h e) -> q t h e", e=NE0), rows[:, :, 0:HX].rearrange("q t (h e) -> q t h e", e=NE0),
                                     spread(ex[:], 3, [Q2, T2, HEADS, NE0]), ALU.mult))
                link(v.tensor_copy(rows[:, :, HX:HF], ex[:]))
                with v.Fori(0, B2 // 2) as b:
                    for s in range(2):
                        v.wait_ge(s_["payload_free"], b * 2 + (s + 1))
                        t0 = b * (2 * G2) + s * G2
                        v.tensor_tensor(hi_hot[:, s, :, :], spread(dst_hi[:, bass.ds(t0, G2)], 2, [Q2, G2, P]),
                                        spread(c.row[0:Q2, 0:P], 1, [Q2, G2, P]), ALU.is_equal)
                        v.tensor_tensor(payload[:, s, :, :].rearrange("q g (j f) -> q g j f", f=HF),
                                        spread(lo_hot[:, bass.ds(t0, G2), :], 3, [Q2, G2, J, HF]),
                                        spread(rows[:, bass.ds(t0, G2), :], 2, [Q2, G2, J, HF]), ALU.mult).then_inc(s_["payload_ready"], 1)
                v.wait_ge(s_["par_in"], 48)
                v.wait_ge(s_["all_summed"], 1)
                v.wait_ge(s_["self_done"], 1)
                link(v.tensor_copy(agg[:], ps_sum[:, 0:J * HF].rearrange("p (j f) -> p j f", f=HF)))
                by_head = lambda ap: ap.rearrange("p j (h e) -> p j h e", e=NE0)
                link(v.tensor_tensor(by_head(sq[:]), by_head(c.h[:, :, 0:HX]), spread(own[:, 2, :, :], 3, [P, J, HEADS, NE0]), ALU.mult))
                link(v.tensor_tensor(agg[:, :, 0:HX], agg[:, :, 0:HX], sq[:], ALU.add))
                link(v.tensor_tensor(agg[:, :, HX:HF], agg[:, :, HX:HF], own[:, 2, :, :], ALU.add))
                link(v.reciprocal(own[:, 0, :, :], agg[:, :, HX:HF]))
                link(v.tensor_tensor(by_head(sq[:]), by_head(agg[:, :, 0:HX]), spread(own[:, 0, :, :], 3, [P, J, HEADS, NE0]), ALU.mult))
                link(v.tensor_tensor(agg[:, :, 0:HX], sq[:], spread(params[:, 0, :], 1, [P, J, HX]), ALU.add))
                a16, mu, var, sd, rs = agg[:, :, 0:HX], stat[:, 0, :], stat[:, 1, :], stat[:, 2, :], stat[:, 3, :]
                link(v.tensor_reduce(mu, a16, AX_X, ALU.add))
                link(v.tensor_scalar(mu, mu, 1.0 / HX, None, ALU.mult))
                link(v.tensor_tensor(a16, a16, spread(mu, 2, [P, J, HX]), ALU.subtract))
                link(v.tensor_tensor(sq[:], a16, a16, ALU.mult))
                link(v.tensor_reduce(var, sq[:], AX_X, ALU.add))
                v.tensor_scalar(var, var, 1.0 / HX, EPS, ALU.mult, ALU.add).then_inc(s_["var_ready"], 1)
                v.wait_ge(s_["std_ready"], 1)
                link(v.reciprocal(rs, sd))
                link(v.tensor_tensor(a16, a16, spread(rs, 2, [P, J, HX]), ALU.mult))
                link(v.tensor_tensor(a16, a16, spread(params[:, 1, :], 1, [P, J, HX]), ALU.mult))
                link(v.tensor_tensor(a16, a16, spread(params[:, 2, :], 1, [P, J, HX]), ALU.add))
                link(v.tensor_reduce(score[:], a16.rearrange("p j (h e) -> p j e h", e=NE0), AX_X, ALU.add))
                link(v.tensor_scalar(score[:], score[:], 1.0 / HEADS, None, ALU.mult))
                lower_triangle(v, link, c, tri, NE0)
                top2_gates(v, link, score[:], c.gates[:, 0:NE0, :], c.chosen[:, 0:NE0, :], t[:], big[:], tri[:], exp_in[:], exp_out[:],
                           (s_["gate_in"], s_["gate_out"], 1))


def lower_triangle(v, link, c, tri, e):
    for i in range(e):
        ins = v.tensor_scalar(tri[:, i * e:(i + 1) * e], c.row[0:P, 0:e], float(i), None, ALU.is_lt)
    link(ins)


def route(v, link, m, c, experts, tiles, scratch, count_ready, counted, ps_cnt):
    e = experts
    count, triangle, before, size, start, run_a, run_b, slot, gate, slot_i, later, passed, expert_of = scratch
    chosen = c.chosen[:, 0:e, :]
    v.tensor_scalar(triangle[:], c.row[0:P, 0:P], c.col[0:P, :], None, ALU.is_gt)
    v.tensor_reduce(count[:], chosen, AX_X, ALU.add).then_inc(count_ready, 1)
    link(v.tensor_copy(run_a[:], chosen))
    a, b, step = run_a, run_b, 1
    while step < J:
        link(v.tensor_copy(b[:, :, 0:step], a[:, :, 0:step]))
        link(v.tensor_tensor(b[:, :, step:J], a[:, :, step:J], a[:, :, 0:J - step], ALU.add))
        a, b, step = b, a, 2 * step
    link(v.tensor_tensor(a[:], a[:], chosen, ALU.subtract))
    v.wait_ge(counted, 1)
    link(v.tensor_scalar(size[:], ps_cnt[:, e:2 * e], 127.0 - 63.5, 1.0 / 128, ALU.add, ALU.mult))
    link(v.tensor_scalar(size[:], size[:], ROUND, -ROUND, ALU.add, ALU.add))
    link(v.memset(start[:], 0.0))
    for i in range(1, e):
        link(v.tensor_tensor(start[:, i:i + 1], start[:, i - 1:i], size[:, i - 1:i], ALU.add))
    link(v.tensor_tensor(later[:], spread(start[0:1, 1:e], 1, [1, tiles, e - 1]),
                         spread(c.row[0:1, 0:tiles], 2, [1, tiles, e - 1]), ALU.is_le))
    link(v.tensor_reduce(passed[:], later[:], AX_X, ALU.add))
    link(v.tensor_copy(expert_of[:], passed[:]))
    link(v.tensor_scalar(start[:], start[:], 128.0, None, ALU.mult))
    link(v.tensor_tensor(before[:], start[0:P, :], ps_cnt[0:P, 0:e], ALU.add))
    link(v.tensor_tensor(a[:], a[:], spread(before[:], 2, [P, e, J]), ALU.add))
    link(v.tensor_tensor(a[:], a[:], chosen, ALU.mult))
    link(v.tensor_reduce(slot[:, 1, :], a.rearrange("p e j -> p j e"), AX_X, ALU.max))
    link(v.tensor_scalar(b[:], chosen, -1e6, 1e6, ALU.mult, ALU.add))
    link(v.tensor_tensor(b[:], b[:], a[:], ALU.add))
    link(v.tensor_reduce(slot[:, 0, :], b.rearrange("p e j -> p j e"), AX_X, ALU.min))
    ins = v.tensor_copy(slot_i[:], slot[:])
    link(ins)
    for i in range(2):
        link(v.tensor_tensor(b[:], a[:], spread(slot[:, i, :], 1, [P, e, J]), ALU.is_equal))
        link(v.tensor_tensor(b[:], b[:], c.gates[:, 0:e, :], ALU.mult))
        link(v.tensor_tensor(b[:], b[:], chosen, ALU.mult))
        link(v.tensor_reduce(gate[:, i, :], b.rearrange("p e j -> p j e"), AX_X, ALU.add))


def block_experts(nc, c, io, pre, experts, edge_table):
    hc = 4
    tiles = (2 * N + experts * 127) // 128
    up_w = K * hc * 128
    groups = 5
    assert tiles % XS == 0
    with ExitStack() as ctx:
        m = Memory(nc, ctx, pre + "_")
        count = m.sb("count", [P, experts])
        triangle = m.sb("triangle", [P, P])
        before = m.sb("before", [P, experts])
        size = m.sb("size", [128, experts])
        start = m.sb("start", [128, experts])
        run_a = m.sb("run_a", [P, experts, J])
        run_b = m.sb("run_b", [P, experts, J])
        slot = m.sb("slot", [P, 2, J])
        gate = m.sb("gate", [P, 2, J])
        slot_i = m.sb("slot_i", [P, 2, J], I32)
        later = m.sb("later", [1, tiles, experts - 1])
        passed = m.sb("passed", [1, tiles])
        expert_of = m.sb("expert_of", [1, tiles], I32)
        w1 = m.sb("w1_all", [128, experts, up_w + hc])
        w2 = m.sb("w2_all", [128, experts, hc, D])
        b1_rows = m.sb("b1_rows", [experts * hc, 128])
        b2 = m.sb("b2_all", [128, experts, D])
        w1_now = m.sb("w1_now", [128, 2, up_w + hc])
        xs = m.sb("xs", [128, XS, D])
        xs_t = m.sb("xs_t", [128, 2, K, 128])
        hidden = m.sb("hidden_s", [128, 2, hc, 128])
        y = m.sb("y", [128, 2, D])
        y_back = m.sb("y_back", [P, J, D])
        ps_x = [m.ps(f"ps_x{s}", [128, 512]) for s in range(2)]
        ps_h = [m.ps(f"ps_h{s}", [128, 512]) for s in range(2)]
        ps_y = [m.ps(f"ps_y{s}", [128, 512]) for s in range(2)]
        ps_cnt = m.ps("ps_cnt", [128, 512])
        if edge_table is not None:
            chunks = tiles - 2
            qe = E1 // R1 // chunks
            attr = m.sb("attr", [R1, 2, qe, FE])
            attr_w = m.sb("attr_w", [R1, FE])
            attr_out = m.sb("attr_out", [R1, E1 // R1])
            attr_in = [m.sem(f"attr_in{i}") for i in range(2)]
            attr_done, attr_w_in, attr_mul, attr_stored = (m.sem(n) for n in ("attr_done", "attr_w_in", "attr_mul", "attr_stored"))
            attrs = io["edge_attr_64"].rearrange("(r b q) f -> b r (q f)", r=R1, q=qe)
        w_in, b_in, b1_turned, b1_ready = (m.sem(n) for n in ("w_in", "b_in", "b1_turned", "b1_ready"))
        count_ready, counted, slots_ready, rows_out = (m.sem(n) for n in ("count_ready", "counted", "slots_ready", "rows_out"))
        xs_in = [m.sem(f"xs_in{i}") for i in range(XS)]
        xs_turned, xs_t_ready, w1_ready, up_done, hidden_ready, down_done, y_ready = (
            m.sem(n) for n in ("xs_turned", "xs_t_ready", "w1_ready", "up_done", "hidden_ready", "down_done", "y_ready"))
        y_out = [m.sem(f"y_out{i}") for i in range(2)]
        chain = m.sem("chain")
        gathered = [m.sem(f"gathered{i}") for i in range(groups)]
        slot_table, y_table = c.slot_table[0:tiles * 128, :], c.y_table[0:tiles * 128, :]
        rows_of = slot_table.rearrange("(t p) d -> t p d", p=128)
        y_of = y_table.rearrange("(t p) d -> t p d", p=128)
        one = lambda t: bass.ds(t, 1) if not isinstance(t, int) else slice(t, t + 1)
        with nc.Block() as block:

            @block.sync
            def _(sp):
                for e in range(experts):
                    sp.dma_start(w1[:, e, 0:up_w].rearrange("p (k h) -> p k h", k=K), io[pre + "_W1"][e].rearrange("(k p) h -> p k h", p=128)).then_inc(w_in, 16)
                    sp.dma_start(w2[:, e, :, :], io[pre + "_W2"][e].rearrange("(k p) h -> p k h", p=128)).then_inc(w_in, 16)
                sp.dma_start(b1_rows[:], io[pre + "_b1"].rearrange("e (k p) -> (e k) p", p=128)).then_inc(b_in, 16)
                sp.dma_start(b2[:], io[pre + "_b2"].unsqueeze(0).broadcast_to([128, experts, D])).then_inc(w_in, 16)
                if edge_table is not None:
                    sp.dma_start(attr_w[:], io["L1_gnn_A"][:, 2 * D:2 * D + FE].broadcast_to([R1, FE])).then_inc(attr_w_in, 16)
                    for s in range(2):
                        sp.dma_start(attr[:, s, :, :].rearrange("r q f -> r (q f)"), attrs[s]).then_inc(attr_in[s], 16)
                sp.wait_ge(rows_out, 16 * 2 * J)
                for s in range(XS):
                    sp.dma_start(xs[:, s, :], rows_of[s]).then_inc(xs_in[s], 16)
                with sp.Fori(0, tiles // XS - 1) as b:
                    for s in range(XS):
                        sp.wait_ge(xs_turned, b * XS + (s + 1))
                        sp.dma_start(xs[:, s, :], rows_of[bass.ds(b * XS + (s + XS), 1)].rearrange("t p d -> p (t d)")).then_inc(xs_in[s], 16)
                        if edge_table is not None:
                            sp.wait_ge(attr_done, b * XS + (s + 1))
                            sp.dma_start(attr[:, s % 2, :, :].rearrange("r q f -> r (q f)"),
                                         attrs[bass.ds(b * XS + (s + 2), 1)].rearrange("b r f -> r (b f)")).then_inc(attr_in[s % 2], 16)
                if edge_table is not None:
                    sp.wait_ge(attr_done, chunks)
                    sp.dma_start(edge_table.rearrange("(r q) -> r q", r=R1), attr_out[:]).then_inc(attr_stored, 16)
                    sp.wait_ge(attr_stored, 16)

            @block.gpsimd
            def _(pool):
                pool.wait_ge(slots_ready, 1)
                for i in range(2):
                    for j in range(J):
                        pool.indirect_dma_start(slot_table, bass.IndirectOffsetOnAxis(ap=slot_i[:, i, j:j + 1], axis=0),
                                                c.xl[:, j, :], None).then_inc(rows_out, 16)

                def store(t, s):
                    pool.wait_ge(y_ready, t + 3)
                    pool.dma_start(y_of[one(t)].rearrange("t p d -> p (t d)"), y[:, s, :]).then_inc(y_out[s], 16)

                with pool.Fori(0, tiles // 2) as b:
                    for s in range(2):
                        store(b * 2 + s, s)
                for s in range(2):
                    pool.wait_ge(y_out[s], 16 * (tiles // 2))
                for j in range(J):
                    for i, to in enumerate((c.xl, y_back)):
                        pool.indirect_dma_start(to[:, j, :], None, y_table,
                                                bass.IndirectOffsetOnAxis(ap=slot_i[:, i, j:j + 1], axis=0)).then_inc(gathered[j // (J // groups)], 16)

            @block.tensor
            def _(pe):
                pe.wait_ge(b_in, 16)
                pe.transpose(ps_x[0][:, 0:experts * hc], b1_rows[:], c.ident[0:experts * hc, 0:experts * hc]).then_inc(b1_turned, 1)
                pe.wait_ge(count_ready, 1)
                pe.matmul(ps_cnt[0:P, 0:experts], triangle[:], count[:], start=True, stop=True)
                pe.matmul(ps_cnt[:, experts:2 * experts], c.ones[0:P, :], count[:], start=True, stop=True).then_inc(counted, 1)
                pe.wait_ge(b1_ready, 1)

                def turn(t, s, seen):
                    pe.wait_ge(xs_in[s], seen)
                    for k in range(K):
                        ins = pe.transpose(ps_x[s % 2][:, k * 128:(k + 1) * 128], xs[:, s, k * 128:(k + 1) * 128], c.ident[:])
                    ins.then_inc(xs_turned, 1)

                def up(t, s):
                    pe.wait_ge(w1_ready, t + 1)
                    pe.wait_ge(xs_t_ready, t + 1)
                    for h in range(hc):
                        for k in range(K):
                            ins = pe.matmul(ps_h[s][:, h * 128:(h + 1) * 128],
                                            w1_now[:, s, k * hc * 128 + h * 128:k * hc * 128 + (h + 1) * 128],
                                            xs_t[:, s, k, :], start=(k == 0), stop=(k == K - 1))
                    ins.then_inc(up_done, 1)

                def down(t, s):
                    e = pe.value_load(expert_of[0:1, one(t)], min_val=0, max_val=experts - 1)
                    pe.wait_ge(hidden_ready, t + 1)
                    pe.wait_ge(y_ready, t + 1)
                    for h in range(hc):
                        ins = pe.matmul(ps_y[s][:, 0:D], hidden[:, s, h, :], w2[:, bass.ds(e, 1), h, :].squeeze(1),
                                        start=(h == 0), stop=(h == hc - 1))
                    ins.then_inc(down_done, 1)

                turn(0, 0, 16)
                pe.wait_ge(w_in, 16 * (2 * experts + 1))
                up(0, 0)
                turn(1, 1, 16)
                up(1, 1)

                def step(t, s, seen):
                    turn(t + 2, (s + 2) % XS, seen)
                    down(t, s % 2)
                    up(t + 2, s % 2)

                with pe.Fori(0, tiles // XS - 1) as b:
                    for s in range(XS):
                        step(b * XS + s, s, b * 16 + 16 * ((s + 2) // XS + 1))
                for s in range(2):
                    step(tiles - XS + s, s, 16 * (tiles // XS))
                for s in range(2):
                    down(tiles - 2 + s, s)

            @block.scalar
            def _(act):
                with act.Fori(0, tiles // 2) as b:
                    for s in range(2):
                        t = b * 2 + s
                        act.wait_ge(up_done, t + 1)
                        act.wait_ge(down_done, t + 1)
                        for h in range(hc):
                            ins = act.activation(hidden[:, s, h, :], ps_h[s][:, h * 128:(h + 1) * 128], ACT.Gelu,
                                                 bias=w1_now[:, s, up_w + h:up_w + h + 1])
                        ins.then_inc(hidden_ready, 1)

            @block.vector
            def _(v):
                link = Link(v, chain)
                v.sem_inc(y_ready, 2)
                v.sem_inc(down_done, 2)
                v.wait_ge(b1_turned, 1)
                v.tensor_copy(w1[:, :, up_w:], ps_x[0][:, 0:experts * hc].rearrange("p (e k) -> p e k", k=hc)).then_inc(b1_ready, 1)
                route(v, link, m, c, experts, tiles,
                      (count, triangle, before, size, start, run_a, run_b, slot, gate, slot_i, later, passed, expert_of),
                      count_ready, counted, ps_cnt)
                v.sem_inc(slots_ready, 1)
                if edge_table is not None:
                    v.wait_ge(attr_w_in, 16)

                def weights(t, s):
                    e = v.value_load(expert_of[0:1, one(t)], min_val=0, max_val=experts - 1)
                    v.tensor_copy(w1_now[:, s, :], w1[:, bass.ds(e, 1), :].squeeze(1)).then_inc(w1_ready, 1)

                def turned(t, s):
                    v.wait_ge(xs_turned, t + 1)
                    v.tensor_copy(xs_t[:, s, :, :].rearrange("p k n -> p (k n)"), ps_x[s][:, 0:K * 128]).then_inc(xs_t_ready, 1)

                def finish(t, s, seen):
                    e = v.value_load(expert_of[0:1, one(t)], min_val=0, max_val=experts - 1)
                    v.wait_ge(down_done, t + 3)
                    if not isinstance(seen, int) or seen:
                        v.wait_ge(y_out[s], seen)
                    v.tensor_tensor(y[:, s, :], ps_y[s][:, 0:D], b2[:, bass.ds(e, 1), :].squeeze(1), ALU.add).then_inc(y_ready, 1)

                v.wait_ge(w_in, 16 * (2 * experts + 1))
                v.wait_ge(b1_ready, 1)
                for s in range(2):
                    weights(s, s)
                    turned(s, s)

                def step(t, s, stored):
                    v.wait_ge(hidden_ready, t + 1)
                    weights(t + 2, s)
                    turned(t + 2, s)
                    finish(t, s, stored)
                    if edge_table is not None:
                        v.wait_ge(attr_in[s], stored + 16)
                        v.tensor_tensor(attr[:, s, :, :], attr[:, s, :, :], spread(attr_w[:], 1, [R1, qe, FE]),
                                        ALU.mult).then_inc(attr_mul, 1)
                        v.wait_ge(attr_mul, t + 1)
                        v.tensor_reduce(attr_out.rearrange("r (b q) -> r b q", q=qe)[:, one(t), :].squeeze(1),
                                        attr[:, s, :, :], AX_X, ALU.add).then_inc(attr_done, 1)

                for s in range(2):
                    step(s, s, 0)
                with v.Fori(1, tiles // 2 - 1) as b:
                    for s in range(2):
                        step(b * 2 + s, s, b * 16)
                for s in range(2):
                    finish(tiles - 2 + s, s, 16 * (tiles // 2 - 1))
                for g in range(groups):
                    v.wait_ge(gathered[g], 16 * 2 * J // groups)
                    for i, back in enumerate((c.xl, y_back)):
                        for j in range(g * (J // groups), (g + 1) * (J // groups)):
                            ins = v.scalar_tensor_tensor(c.x[:, j, :], back[:, j, :], gate[:, i, j:j + 1], c.x[:, j, :], ALU.mult, ALU.add)
                        link(ins)


def block_z(nc, c, io):
    with ExitStack() as ctx:
        m = Memory(nc, ctx, "z_")
        st = m.sb("st", [P, J, BN])
        small = m.sb("small", [P, 5, J])
        std = m.sb("std", [P, J])
        w = m.sb("w", [128, K, D])
        wt = m.sb("wt", [128, K, ZF])
        a_rows = m.sb("a_rows", [2 * K, 128])
        a_cols = m.sb("a_cols", [128, 2, K])
        z = m.sb("z", [P, J, ZF])
        ps_turn = [m.ps(f"ps_turn{i}", [128, 512]) for i in range(2)]
        ps_w = m.ps("ps_w", [128, 512])
        ps_wa = m.ps("ps_wa", [128, 2 * K + 4])
        ps_z = [m.ps(f"ps_z{i}", [P, 512]) for i in range(2)]
        w_in, var_ready, std_ready, xl_ready = (m.sem(n) for n in ("w_in", "var_ready", "std_ready", "xl_ready"))
        turned, turn_free, a_turned, a_ready = (m.sem(n) for n in ("turned", "turn_free", "a_turned", "a_ready"))
        w_turned, w_ready, wa_summed, wt_ready = (m.sem(n) for n in ("w_turned", "w_ready", "wa_summed", "wt_ready"))
        z_summed, z_copied, ones_set = (m.sem(n) for n in ("z_summed", "z_copied", "ones_set"))
        x_out, z_out, a_set, line_out, chain = (m.sem(n) for n in ("x_out", "z_out", "a_set", "line_out", "chain"))
        with nc.Block() as block:

            @block.sync
            def _(sp):
                sp.dma_start(w[:], io["L1_gnn_W"].rearrange("(k p) c -> p k c", p=128)).then_inc(w_in, 16)
                sp.dma_start(a_rows[:], io["L1_gnn_A"][0, 0:2 * D].rearrange("(k p) -> k p", p=128)).then_inc(w_in, 16)
                sp.dma_start(c.x_table.rearrange("(p j) d -> p j d", j=J), c.x[:]).then_inc(x_out, 16)
                for j in range(0, J, 5):
                    sp.wait_ge(ones_set, j // 5 + 1)
                    sp.dma_start(c.z_table.rearrange("(p j) f -> p j f", j=J)[:, j:j + 5, :], z[:, j:j + 5, :]).then_inc(z_out, 16)
                sp.wait_ge(z_out, 16 * 5)
                sp.wait_ge(x_out, 16)

            @block.tensor
            def _(pe):
                pe.wait_ge(w_in, 32)
                pe.transpose(ps_wa[:, 2 * K:2 * K + 4], a_rows[:], c.ident[0:4, 0:4]).then_inc(a_turned, 1)
                for k in range(K):
                    for f in range(K):
                        ins = pe.transpose(ps_w[:, (k * K + f) * 128:(k * K + f + 1) * 128], w[:, f, k * 128:(k + 1) * 128], c.ident[:])
                ins.then_inc(w_turned, 1)
                pe.wait_ge(a_ready, 1)
                for k in range(K):
                    for f in range(K):
                        ins = pe.matmul(ps_wa[:, 2 * k:2 * k + 2], w[:, f, k * 128:(k + 1) * 128], a_cols[:, :, f],
                                        start=(f == 0), stop=(f == K - 1))
                ins.then_inc(wa_summed, 1)
                pe.wait_ge(xl_ready, 1)
                transpose_nodes(pe, c, ps_turn, None, turn_free, turned, 0)
                pe.wait_ge(turn_free, TURNS)
                pe.wait_ge(wt_ready, 2)
                for j in range(J):
                    if j >= 2:
                        pe.wait_ge(z_copied, j - 1)
                    for k in range(K):
                        ins = pe.matmul(ps_z[j % 2][:, 0:ZF], c.xt[:, k, j * P:(j + 1) * P], wt[:, k, :],
                                        start=(k == 0), stop=(k == K - 1))
                    ins.then_inc(z_summed, 1)

            @block.scalar
            def _(act):
                act.wait_ge(w_turned, 1)
                act.copy(wt[:, :, 0:D], ps_w.rearrange("p (k f) -> p k f", k=K)).then_inc(wt_ready, 1)
                act.wait_ge(var_ready, 1)
                act.activation(std[:], small[:, 2, :], ACT.Sqrt).then_inc(std_ready, 1)
                copy_turned(act, act.copy, c, ps_turn, turn_free, turned, 0)
                for j in range(J):
                    act.wait_ge(z_summed, j + 1)
                    act.copy(z[:, j, :], ps_z[j % 2][:, 0:ZF]).then_inc(z_copied, 1)

            @block.vector
            def _(v):
                link = Link(v, chain)
                v.wait_ge(a_turned, 1)
                v.tensor_copy(a_cols.rearrange("p s k -> p (s k)"), ps_wa[:, 2 * K:2 * K + 4]).then_inc(a_ready, 1)
                link(v.memset(wt[:, :, D:D + 1], 0.0))
                layernorm_stats(v, link, c.x, st, small, std[:], var_ready, 1, std_ready)
                layernorm_apply(v, link, c.xl, c.x, small)
                v.sem_inc(xl_ready, 1)
                v.wait_ge(wa_summed, 1)
                v.tensor_copy(wt[:, :, D + 1:D + 3], ps_wa[:, 0:2 * K].rearrange("p (k s) -> p k s", k=K)).then_inc(wt_ready, 1)
                for j in range(0, J, 5):
                    v.wait_ge(z_copied, j + 5)
                    v.memset(z[:, j:j + 5, D:D + 1], 1.0).then_inc(ones_set, 1)
                link(v.tensor_copy(c.ad_nodes[:], z[:, :, D + 2]))
                link(v.memset(c.most_of[:], -3e38))
                link(v.tensor_reduce(c.most_of[0:P, 0:1], z[:, :, D + 1], AX_X, ALU.max))


def block_windows(nc, c, io):
    with ExitStack() as ctx:
        m = Memory(nc, ctx, "windows_")
        acc = m.sb("acc", [P, J, D + 1])
        first = m.sb("first", [128, J])
        item_w = m.sb("item_w", [128, I4])
        item_t = m.sb("item_t", [128, I4])
        item_n = m.sb("item_n", [128, I4])
        item_t_i = m.sb("item_t_i", [128, I4], I32)
        w_rows = m.sb("w_rows", [I4, 128], I32)
        w_line = m.sb("w_line", [1, I4 * 128], I32)
        less = m.sb("less", [128, J])
        five = m.sb("five", [P, J])
        count = m.sb("count", [P, 1])
        count_row = m.sb("count_row", [P, 128])
        src_rows_i = m.sb("src_rows_i", [128, I4, Q1], I32)
        dst_rows_i = m.sb("dst_rows_i", [128, I4, Q1], I32)
        src_rows = m.sb("src_rows", [128, I4, Q1])
        dst_rows = m.sb("dst_rows", [128, I4, Q1])
        hi_rows = m.sb("hi_rows", [128, I4, Q1])
        hi_rows_b = m.sb("hi_rows_b", [128, I4, Q1], BF16)
        edge_rows = m.sb("edge_rows", [128, I4, Q1])
        src_i = m.sb("src_i", [Q1, I4 * 128], I32)
        dst = m.sb("dst", [Q1, I4 * 128])
        dst_lo = m.sb("dst_lo", [Q1, I4 * 128], BF16)
        lo_hot = m.sb("lo_hot", [Q1, IP, J], BF16)
        edge = m.sb("edge", [Q1, I4 * 128])
        ad = m.sb("ad", [Q1, IP])
        cap = m.sb("cap", [Q1, IP])
        most = m.sb("most", [128, 4])
        hi_line = m.sb("hi_line", [P, 2, G1 * Q1], BF16)
        hi_hot_t = m.sb("hi_hot_t", [P, 2, G1 * Q1], BF16)
        found = m.sb("found", [Q1, G1, J])
        ad_rest = m.sb("ad_rest", [P, J])
        ad_b = m.sb("ad_b", [P, 3, J], BF16)
        zero_i = m.sb("zero_i", [128, UW], I32)
        spare_i = m.sb("spare_i", [128, 1], I32)
        stage = m.sb("stage", [Q1, SW, UW], I32)
        ring = m.sb("ring", [Q1, SW, UW, ZF])
        logit = m.sb("logit", [Q1, 2, UW])
        lrelu = m.sb("lrelu", [Q1, 2, UW])
        below = m.sb("below", [Q1, 2, UW])
        ex = m.sb("ex", [Q1, 2, UW])
        prob = m.sb("prob", [Q1, 2, UW, P])
        rden = m.sb("rden", [P, J])
        ps_a = m.ps("ps_a", [128, 512])
        ps_b = m.ps("ps_b", [128, 512])
        looked = [m.ps(f"looked{i}", [Q1, 512]) for i in range(2)]
        part = [m.ps(f"part{i}", [P, 512]) for i in range(4)]
        names = ("count_ready", "count_summed", "items_ready", "w_turned", "w_ready", "w_out", "rows_in", "hi_ready",
                 "hi_out", "rows_ready", "turned", "turn_free", "src_ready", "most_in", "most_out", "hot_t_ready",
                 "looked_up", "looked_free", "found_done", "x_in", "staged", "used", "below_ready", "ex_ready",
                 "prob_ready", "part_ready", "part_free", "small_chain", "chain", "z_line")
        s_ = {n: m.sem(n) for n in names}
        line_in = [m.sem(f"line_in{i}") for i in range(2)]
        gathered = [m.sem(f"gathered{i}") for i in range(SW)]
        table = lambda ap: ap.rearrange("(t q) -> t q", q=Q1)
        with nc.Block() as block:

            @block.sync
            def _(sp):
                sp.dma_start(c.x[:], c.x_table.rearrange("(w d) f -> d w f", d=P)).then_inc(s_["x_in"], 16)
                sp.wait_ge(s_["w_ready"], 1)
                sp.dma_start(c.w_dram.rearrange("(k p) -> k p", p=128), w_rows[:]).then_inc(s_["w_out"], 16)
                sp.wait_ge(s_["w_out"], 16)
                sp.dma_start(w_line[:], c.w_dram.unsqueeze(0)).then_inc(s_["z_line"], 16)
                sp.wait_ge(s_["hi_ready"], 1)
                sp.dma_start(c.hi_line_dram3.rearrange("(k p q) -> p k q", p=128, q=Q1), hi_rows_b[:]).then_inc(s_["hi_out"], 16)
                sp.wait_ge(s_["hi_out"], 16)
                lines = c.hi_line_dram3[0:IP * Q1].rearrange("(b e) -> b e", e=G1 * Q1)
                for s in range(2):
                    sp.dma_start(hi_line[:, s, :], lines[s:s + 1, :].broadcast_to([P, G1 * Q1])).then_inc(line_in[s], 16)
                with sp.Fori(1, IP // G1 // 2) as b:
                    for s in range(2):
                        sp.wait_ge(s_["hot_t_ready"], b * 2 + (s - 1))
                        sp.dma_start(hi_line[:, s, :], lines[bass.ds(b * 2 + s, 1), :].broadcast_to([P, G1 * Q1])).then_inc(line_in[s], 16)

            @block.gpsimd
            def _(pool):
                pool.memset(zero_i[:], 0).then_inc(s_["staged"], 1)
                pool.wait_ge(s_["items_ready"], 1)
                for k in range(I4):
                    at = bass.IndirectOffsetOnAxis(ap=item_t_i[:, k:k + 1], axis=0)
                    pool.indirect_dma_start(src_rows_i[:, k, :], None, table(io["src"]), at).then_inc(s_["rows_in"], 16)
                    pool.indirect_dma_start(dst_rows_i[:, k, :], None, table(io["dst"]), at).then_inc(s_["rows_in"], 16)
                    pool.indirect_dma_start(edge_rows[:, k, :], None, table(c.edge_table), at).then_inc(s_["rows_in"], 16)
                pool.wait_ge(s_["src_ready"], 1)
                pool.wait_ge(s_["staged"], 1)

                def gather(g, s):
                    pool.wait_ge(s_["used"], g + 1)
                    pool.tensor_tensor(stage[:, s, :], src_i[:, bass.ds(g * UW, UW)], zero_i[0:Q1, :], ALU.add).then_inc(s_["staged"], 1)
                    pool.wait_ge(s_["staged"], g + 2)
                    pool.tensor_tensor(spare_i[:], zero_i[:, 0:1], zero_i[:, 1:2], ALU.add)
                    for u in range(UW):
                        pool.indirect_dma_start(ring[:, s, u, :], None, c.z_table,
                                                bass.IndirectOffsetOnAxis(ap=stage[:, s, u:u + 1], axis=0)).then_inc(gathered[s], 16)

                gather(0, 0)
                pool.wait_ge(s_["most_in"], 1)
                pool.partition_all_reduce(most[:, 0:2], c.most_of[:, 0:2], 128, bass.bass_isa.ReduceOp.max).then_inc(s_["most_out"], 1)
                with pool.Fori(0, GW // SW) as b:
                    for s in range(SW):
                        gather(b * SW + (s + 1), (s + 1) % SW)

            @block.tensor
            def _(pe):
                pe.wait_ge(s_["count_ready"], 1)
                pe.matmul(ps_a[:, 0:J], count_row[:], five[:], start=True, stop=True).then_inc(s_["count_summed"], 1)
                pe.wait_ge(s_["items_ready"], 1)
                pe.transpose(ps_b[0:I4, 0:128], item_w[:], c.ident[:]).then_inc(s_["w_turned"], 1)
                pe.wait_ge(s_["w_ready"], 1)
                pe.wait_ge(s_["rows_ready"], 1)
                for i, rows in enumerate((src_rows, dst_rows, hi_rows, edge_rows)):
                    if i >= 2:
                        pe.wait_ge(s_["turn_free"], i - 1)
                    for k in range(I4):
                        ins = pe.transpose((ps_a, ps_b)[i % 2][0:Q1, k * 128:(k + 1) * 128], rows[:, k, :], c.ident[:])
                    ins.then_inc(s_["turned"], 1)
                with pe.Fori(0, IP // G1 // 2) as b:
                    for s in range(2):
                        pe.wait_ge(s_["hot_t_ready"], b * 2 + (s + 1))
                        pe.wait_ge(s_["looked_free"], b * 2 + (s + 1))
                        for g in range(G1):
                            for i in range(3):
                                ins = pe.matmul(looked[s][:, g * J:(g + 1) * J], hi_hot_t[:, s, g * Q1:(g + 1) * Q1],
                                                ad_b[:, i, :], start=(i == 0), stop=(i == 2))
                        ins.then_inc(s_["looked_up"], 1)

                def group(g, s, half):
                    for u in range(UW):
                        pe.wait_ge(s_["prob_ready"], g * UW + (u + 1))
                        pe.wait_ge(s_["part_free"], g * UW + (u + 1))
                        ins = pe.matmul(part[u % 4][:, 0:D + 1], prob[:, half, u, :], ring[:, s, u, 0:D + 1], start=True, stop=True)
                        ins.then_inc(s_["part_ready"], 1)

                with pe.Fori(0, GW // SW) as b:
                    for s in range(SW):
                        group(b * SW + s, s, s % 2)
                group(GW - 1, (GW - 1) % SW, (GW - 1) % 2)

            @block.scalar
            def _(act):
                def exps(g, half):
                    act.wait_ge(s_["below_ready"], g + 1)
                    act.activation(ex[:, half, :], below[:, half, :], ACT.Exp).then_inc(s_["ex_ready"], 1)

                with act.Fori(0, (GW - 1) // 2) as b:
                    for s in range(2):
                        exps(b * 2 + s, s)
                exps(GW - 1, (GW - 1) % 2)

            @block.vector
            def _(v):
                link = Link(v, s_["chain"])
                v.sem_inc(s_["looked_free"], 2)
                v.sem_inc(s_["part_free"], 4)
                v.sem_inc(s_["used"], SW)
                link(v.tensor_scalar(five[:], c.row[0:P, 0:J], float(P // J), None, ALU.mult))
                link(v.tensor_scalar(five[:], five[:], c.col[0:P, :], None, ALU.is_gt))
                link(v.tensor_reduce(count[:], c.deg[:], AX_X, ALU.add))
                v.tensor_copy(count_row[:], count[:, 0:1].broadcast_to([P, 128])).then_inc(s_["count_ready"], 1)
                link(v.memset(acc[:], 0.0))
                v.wait_ge(s_["count_summed"], 1)
                link(v.tensor_scalar(first[:], ps_a[:, 0:J], -float(Q1 // 2), 1.0 / Q1, ALU.add, ALU.mult))
                link(v.tensor_scalar(first[:], first[:], ROUND, -ROUND, ALU.add, ALU.add))
                link(v.tensor_scalar(first[:], first[:], float(T1 - 1), None, ALU.min))
                link(v.tensor_tensor(first[:], first[:], c.row[:, 0:J], ALU.add))
                for k in range(I4):
                    link(v.tensor_scalar(item_n[:, k:k + 1], c.col[:], 128.0 * k, None, ALU.add))
                    link(v.tensor_scalar(less[:, 0:J - 1], first[:, 1:J], item_n[:, k:k + 1], None, ALU.is_le))
                    link(v.tensor_reduce(item_w[:, k:k + 1], less[:, 0:J - 1], AX_X, ALU.add))
                link(v.tensor_tensor(item_t[:], item_n[:], item_w[:], ALU.subtract))
                link(v.tensor_scalar(item_t[:], item_t[:], float(T1 - 1), None, ALU.min))
                v.tensor_copy(item_t_i[:], item_t[:]).then_inc(s_["items_ready"], 1)
                v.wait_ge(s_["w_turned"], 1)
                v.tensor_copy(w_rows[:], ps_b[0:I4, 0:128]).then_inc(s_["w_ready"], 1)
                link(v.tensor_scalar(item_w[:], item_w[:], float(P), None, ALU.mult))
                three_parts(v, link, [ad_b[:, i, :] for i in range(3)], ad_rest[:], c.ad_nodes[:])
                v.wait_ge(s_["rows_in"], 16 * 3 * I4)
                link(v.tensor_copy(src_rows[:], src_rows_i[:]))
                link(v.tensor_copy(dst_rows[:], dst_rows_i[:]))
                link(v.tensor_scalar(hi_rows[:], dst_rows[:], -float(J // 2), 1.0 / J, ALU.add, ALU.mult))
                link(v.tensor_scalar(hi_rows[:], hi_rows[:], ROUND, -ROUND, ALU.add, ALU.add))
                link(v.tensor_copy(hi_rows_b[:], hi_rows[:]))
                v.sem_inc(s_["hi_ready"], 1)
                link(v.scalar_tensor_tensor(hi_rows[:], hi_rows[:], -float(J), dst_rows[:], ALU.mult, ALU.add))
                for k in range(I4):
                    link(v.tensor_scalar(dst_rows[:, k, :], dst_rows[:, k, :], item_w[:, k:k + 1], None, ALU.subtract))
                v.sem_inc(s_["rows_ready"], 1)
                link(v.tensor_reduce(c.most_of[:, 1:2], edge_rows.rearrange("p k q -> p (k q)"), AX_X, ALU.max))
                v.sem_inc(s_["most_in"], 1)
                for i, to in enumerate((src_i, dst, dst_lo, edge)):
                    v.wait_ge(s_["turned"], i + 1)
                    ins = v.tensor_copy(to[:], (ps_a, ps_b)[i % 2][0:Q1, :])
                    link(ins)
                    v.sem_inc(s_["turn_free"], 1)
                    if i == 0:
                        v.sem_inc(s_["src_ready"], 1)
                link(v.tensor_tensor(lo_hot[:], spread(dst_lo[:, 0:IP], 2, [Q1, IP, J]), spread(c.row_b[0:Q1, 0:J], 1, [Q1, IP, J]), ALU.is_equal))
                with v.Fori(0, IP // G1 // 2) as b:
                    for s in range(2):
                        v.wait_ge(line_in[s], b * 16 + 16)
                        v.tensor_scalar(hi_hot_t[:, s, :], hi_line[:, s, :], c.col[0:P, 0:1], None,
                                        ALU.is_equal).then_inc(s_["hot_t_ready"], 1)
                        v.wait_ge(s_["looked_up"], b * 2 + (s + 1))
                        t0 = b * (2 * G1) + s * G1
                        v.tensor_tensor(found[:], looked[s][:, 0:G1 * J].rearrange("q (g j) -> q g j", j=J),
                                        lo_hot[:, bass.ds(t0, G1), :], ALU.mult).then_inc(s_["looked_free"], 1)
                        v.wait_ge(s_["looked_free"], b * 2 + (s + 3))
                        v.tensor_reduce(ad[:, bass.ds(t0, G1)], found[:], AX_X, ALU.add).then_inc(s_["found_done"], 1)
                v.wait_ge(s_["found_done"], IP // G1)
                v.wait_ge(s_["most_out"], 1)
                link(v.tensor_tensor(most[:, 2:3], most[:, 0:1], most[:, 1:2], ALU.add))
                link(v.tensor_scalar(cap[:], ad[:], most[0:Q1, 2:3], None, ALU.add))
                link(v.scalar_tensor_tensor(cap[:], cap[:], 0.2, cap[:], ALU.mult, ALU.max))
                link(v.tensor_tensor(ad[:], ad[:], edge[:, 0:IP], ALU.add))

                def logits(g, s, half, seen):
                    now = bass.ds(g * UW, UW) if not isinstance(g, int) else slice(g * UW, (g + 1) * UW)
                    v.wait_ge(gathered[s], seen)
                    v.tensor_tensor(logit[:, half, :], ring[:, s, :, D + 1], ad[:, now], ALU.add).then_inc(s_["small_chain"], 1)
                    v.wait_ge(s_["small_chain"], g * 2 + 1)
                    v.scalar_tensor_tensor(lrelu[:, half, :], logit[:, half, :], 0.2, logit[:, half, :], ALU.mult, ALU.max).then_inc(s_["small_chain"], 1)
                    v.wait_ge(s_["small_chain"], g * 2 + 2)
                    v.tensor_tensor(below[:, half, :], lrelu[:, half, :], cap[:, now], ALU.subtract).then_inc(s_["below_ready"], 1)

                def one_hot(g, u, half):
                    i = g * UW + u
                    at = bass.ds(i, 1) if not isinstance(g, int) else slice(i, i + 1)
                    v.tensor_scalar(prob[:, half, u, :], c.row[0:Q1, 0:P], dst[:, at], ex[:, half, u:u + 1],
                                    ALU.is_equal, ALU.mult).then_inc(s_["prob_ready"], 1)

                def add(g, u):
                    i = g * UW + u
                    at = bass.ds(i, 1) if not isinstance(g, int) else slice(i, i + 1)
                    w = v.value_load(w_line[0:1, at], min_val=0, max_val=J - 1)
                    v.wait_ge(s_["part_ready"], i + 1)
                    v.wait_ge(s_["part_free"], i + 4)
                    row = acc[:, bass.ds(w, 1), :].squeeze(1)
                    v.tensor_tensor(row, part[u % 4][:, 0:D + 1], row, ALU.add).then_inc(s_["part_free"], 1)
                    if u == UW - 1:
                        v.sem_inc(s_["used"], 1)

                v.wait_ge(s_["z_line"], 16)
                logits(0, 0, 0, 16 * UW)
                v.wait_ge(s_["ex_ready"], 1)
                for u in range(UW):
                    one_hot(0, u, 0)
                with v.Fori(0, (GW - 1) // SW) as b:
                    for k in range(SW):
                        g, s, half = b * SW + (k + 1), (k + 1) % SW, (k + 1) % 2
                        logits(g, s, half, b * (16 * UW) + 16 * UW * (1 + (k + 1) // SW))
                        for u in range(UW):
                            add(b * SW + k, u)
                            if u == 0:
                                v.wait_ge(s_["ex_ready"], g + 1)
                            one_hot(g, u, half)
                for u in range(UW):
                    add(GW - 1, u)
                v.wait_ge(s_["part_free"], GW * UW + 4)
                link(v.tensor_scalar(rden[:], acc[:, :, D], 1e-37, None, ALU.max))
                link(v.reciprocal(rden[:], rden[:]))
                v.wait_ge(s_["x_in"], 16)
                with v.Fori(0, J) as j:
                    v.scalar_tensor_tensor(c.x[:, bass.ds(j, 1), :].squeeze(1), acc[:, bass.ds(j, 1), 0:D].squeeze(1), rden[:, bass.ds(j, 1)],
                                           c.x[:, bass.ds(j, 1), :].squeeze(1), ALU.mult, ALU.add).then_inc(link.sem, 1)
                link.loop_end(J)
                v.wait_ge(link.sem, link.n)


def block_router(nc, c, io):
    with ExitStack() as ctx:
        m = Memory(nc, ctx, "router_")
        st = m.sb("st", [P, J, BN])
        small = m.sb("small", [P, 5, J])
        std = m.sb("std", [P, 2, J])
        scale = m.sb("scale", [P, 2, D])
        wr = m.sb("wr", [128, K, NE1])
        br = m.sb("br", [P, NE1])
        score = m.sb("score", [P, J, NE1])
        t = m.sb("t", [P, J, NE1, 4])
        big = m.sb("big", [P, J, NE1, NE1])
        tri = m.sb("tri", [P, NE1 * NE1])
        exp_in = m.sb("exp_in", [P, J, NE1])
        exp_out = m.sb("exp_out", [P, J, NE1])
        ps_turn = [m.ps(f"ps_turn{i}", [128, 512]) for i in range(2)]
        ps_r = m.ps("ps_r", [P, J * NE1])
        w_in, var_ready, std_ready, xl_ready = (m.sem(n) for n in ("w_in", "var_ready", "std_ready", "xl_ready"))
        turned, turn_free, summed, gate_in, gate_out, chain = (
            m.sem(n) for n in ("turned", "turn_free", "summed", "gate_in", "gate_out", "chain"))
        with nc.Block() as block:

            @block.sync
            def _(sp):
                sp.dma_start(wr[:], io["L1_ffn_Wr"].rearrange("(k p) e -> p k e", p=128)).then_inc(w_in, 16)
                sp.dma_start(br[:], io["L1_ffn_br"].unsqueeze(0).broadcast_to([P, NE1])).then_inc(w_in, 16)
                sp.dma_start(scale[:, 0, :], io["L1_ffn_gamma"].unsqueeze(0).broadcast_to([P, D])).then_inc(w_in, 16)
                sp.dma_start(scale[:, 1, :], io["L1_ffn_beta"].unsqueeze(0).broadcast_to([P, D])).then_inc(w_in, 16)

            @block.scalar
            def _(act):
                for i in range(2):
                    act.wait_ge(var_ready, i + 1)
                    act.activation(std[:, i, :], small[:, 2, :], ACT.Sqrt).then_inc(std_ready, 1)
                copy_turned(act, act.copy, c, ps_turn, turn_free, turned, 0)
                act.wait_ge(gate_in, 1)
                act.activation(exp_out[:], exp_in[:], ACT.Exp).then_inc(gate_out, 1)

            @block.tensor
            def _(pe):
                pe.wait_ge(xl_ready, 1)
                transpose_nodes(pe, c, ps_turn, None, turn_free, turned, 0)
                pe.wait_ge(turn_free, TURNS)
                pe.wait_ge(w_in, 64)
                for j in range(J):
                    for k in range(K):
                        ins = pe.matmul(ps_r[:, j * NE1:(j + 1) * NE1], c.xt[:, k, j * P:(j + 1) * P], wr[:, k, :],
                                        start=(k == 0), stop=(k == K - 1))
                ins.then_inc(summed, 1)

            @block.vector
            def _(v):
                link = Link(v, chain)
                layernorm_stats(v, link, c.x, st, small, std[:, 0, :], var_ready, 1, std_ready)
                layernorm_apply(v, link, c.xl, c.x, small)
                layernorm_stats(v, link, c.xl, st, small, std[:, 1, :], var_ready, 2, std_ready)
                layernorm_apply(v, link, c.xl, c.xl, small)
                v.wait_ge(w_in, 64)
                link(v.tensor_tensor(c.xl[:], c.xl[:], spread(scale[:, 0, :], 1, [P, J, D]), ALU.mult))
                link(v.tensor_tensor(c.xl[:], c.xl[:], spread(scale[:, 1, :], 1, [P, J, D]), ALU.add))
                v.sem_inc(xl_ready, 1)
                lower_triangle(v, link, c, tri, NE1)
                v.wait_ge(summed, 1)
                link(v.tensor_tensor(score[:], ps_r.rearrange("p (j e) -> p j e", e=NE1), spread(br[:], 1, [P, J, NE1]), ALU.add))
                top2_gates(v, link, score[:], c.gates[:, 0:NE1, :], c.chosen[:, 0:NE1, :], t[:], big[:], tri[:], exp_in[:], exp_out[:],
                           (gate_in, gate_out, 1))


def store_x(nc, c, io):
    with ExitStack() as ctx:
        m = Memory(nc, ctx, "store_x_")
        stored = m.sem("stored")
        with nc.Block() as block:

            @block.sync
            def _(sp):
                sp.dma_start(io["out"].rearrange("(w d) f -> d w f", d=P), c.x[:]).then_inc(stored, 16)
                sp.wait_ge(stored, 16)


class Common:
    pass


def program(nc, io, stages=4):
    with ExitStack() as ctx:
        m = Memory(nc, ctx)
        c = Common()
        c.x = m.sb("x_nodes", [P, J, D])
        c.xl = m.sb("xl_nodes", [P, J, D])
        c.row = m.sb("row", [128, N])
        c.row_b = m.sb("row_b", [128, 128], BF16)
        c.col = m.sb("col", [128, 1])
        c.ident = m.sb("ident", [128, 128])
        c.ones = m.sb("ones", [128, 128])
        c.zeros_b = m.sb("zeros_b", [128, 128], BF16)
        c.hi_line_dram = nc.dram_tensor("hi_line_dram", [E1], BF16, kind="Internal").ap()
        c.hi_line_dram2 = nc.dram_tensor("hi_line_dram2", [E2], BF16, kind="Internal").ap()
        c.hi_line_dram3 = nc.dram_tensor("hi_line_dram3", [I4 * 128 * Q1], BF16, kind="Internal").ap()
        c.w_dram = nc.dram_tensor("w_dram", [I4 * 128], I32, kind="Internal").ap()
        c.edge_table = nc.dram_tensor("edge_table", [E1], F32, kind="Internal").ap()
        c.x_table = nc.dram_tensor("x_table", [N, D], F32, kind="Internal").ap()
        c.z_table = nc.dram_tensor("z_table", [N, ZF], F32, kind="Internal").ap()
        c.deg = m.sb("deg_nodes", [P, J])
        c.ad_nodes = m.sb("ad_nodes", [P, J])
        c.h_table = nc.dram_tensor("h_table", [N, HF], F32, kind="Internal").ap()
        c.h = m.sb("h_nodes", [P, J, HF])
        c.a_dst = m.sb("a_dst", [P, J, HEADS])
        c.most_of = m.sb("most_of", [128, HEADS])
        c.most = m.sb("most", [128, HEADS])
        c.gates = m.sb("gates", [P, NE1, J])
        c.chosen = m.sb("chosen", [P, NE1, J])
        most_tiles = (2 * N + NE1 * 127) // 128
        c.slot_table = nc.dram_tensor("slot_table", [most_tiles * 128, D], F32, kind="Internal").ap()
        c.y_table = nc.dram_tensor("y_table", [most_tiles * 128, D], F32, kind="Internal").ap()
        constants(nc, c)
        block_gcn(nc, c, io)

        def with_xt(block):
            with ExitStack() as inner:
                c.xt = Memory(nc, inner).sb(block.__name__ + "_xt", [128, K, N])
                block(nc, c, io)

        with_xt(block_gat_tables)
        block_gat_edges(nc, c, io)
        block_experts(nc, c, io, "L0_ffn", NE0, c.edge_table)
        with_xt(block_z)
        block_windows(nc, c, io)
        with_xt(block_router)
        block_experts(nc, c, io, "L1_ffn", NE1, None)
        store_x(nc, c, io)


_INS = ['x', 'src', 'dst', 'edge_attr_64', 'L0_gnn_w1', 'L0_gnn_b1', 'L0_gnn_w2', 'L0_gnn_b2', 'L0_gnn_gcn_w',
        'L0_gnn_gcn_b', 'L0_ffn_W_gat', 'L0_ffn_att_src', 'L0_ffn_att_dst', 'L0_ffn_b_gat', 'L0_ffn_ln_gamma',
        'L0_ffn_ln_beta', 'L0_ffn_W1', 'L0_ffn_b1', 'L0_ffn_W2', 'L0_ffn_b2', 'L0_ffn_edge_index', 'L1_gnn_W',
        'L1_gnn_A', 'L1_ffn_gamma', 'L1_ffn_beta', 'L1_ffn_Wr', 'L1_ffn_br', 'L1_ffn_W1', 'L1_ffn_b1', 'L1_ffn_W2',
        'L1_ffn_b2']


def kernel(**inputs):
    import numpy as _np
    import concourse.bacc as _bacc
    from concourse import mybir as _mybir
    from concourse.bass_utils import run_bass_kernel_spmd as _run

    nc = _bacc.Bacc("TRN2", target_bir_lowering=False, num_devices=1)
    arrays, io = {}, {}
    for name in _INS:
        a = _np.ascontiguousarray(inputs[name])
        arrays[f"in_{name}_dram"] = a
        io[name] = nc.dram_tensor(f"in_{name}_dram", a.shape, _mybir.dt.from_np(a.dtype), kind="ExternalInput").ap()
    io["out"] = nc.dram_tensor("out_dram", (N, D), F32, kind="ExternalOutput").ap()
    program(nc, io)
    r = _run(nc, [arrays], core_ids=[0])
    return r.results[0]["out_dram"]
```

```python
from contextlib import ExitStack

import concourse.bass as bass
from concourse import mybir

F32 = mybir.dt.float32
BF16 = mybir.dt.bfloat16
I32 = mybir.dt.int32
ALU = mybir.AluOpType
ACT = mybir.ActivationFunctionType
AX_X = mybir.AxisListType.X

N = 3125
P = 125
J = N // P
D = 256
K = D // 128
E1 = 50000
Q1 = 125
T1 = E1 // Q1
R1 = 100
C1 = T1 // R1
G1 = 20
B1 = T1 // G1
NE0 = 4
HEADS = 4
HX = HEADS * NE0
HF = HX + HEADS
E2 = 32768
Q2 = 128
T2 = E2 // Q2
R2 = 128
C2 = T2 // R2
G2 = 8
B2 = T2 // G2
S2 = 4
NE1 = 8
FE = 64
ZF = D + 3
UW = 6
SW = 10
ITEMS = T1 + J - 1
GW = -(-ITEMS // UW)
assert (GW - 1) % SW == 0
LS = 4
PART = 4
I4 = -(-ITEMS // 128)
GL = 3 * UW
IP = LS * GL * -(-ITEMS // (LS * GL))
assert IP <= I4 * 128
XS = 4
ROUND = 12582912.0
EPS = 1e-5
BN = 6


class Link:

    def __init__(self, eng, sem):
        self.eng, self.sem, self.n = eng, sem, 0

    def __call__(self, ins, n=1):
        ins.then_inc(self.sem, 1)
        self.n += n
        self.eng.wait_ge(self.sem, self.n)

    def at(self, ins, n):
        ins.then_inc(self.sem, 1)
        self.eng.wait_ge(self.sem, n + self.n)

    def loop_end(self, steps):
        self.n += steps


def spread(ap, axis, shape):
    return ap.unsqueeze(axis).broadcast_to(shape)


class Memory:
    def __init__(self, nc, ctx, prefix=""):
        self.nc, self.ctx, self.prefix, self.sems = nc, ctx, prefix, []
        ctx.callback(self.clear)

    def clear(self):
        if self.sems:
            self.nc.clear_and_free_semaphores(self.sems)
            self.nc.all_engine_barrier()

    def sb(self, name, shape, dt=F32):
        return self.ctx.enter_context(self.nc.sbuf_tensor(self.prefix + name, shape, dt))

    def ps(self, name, shape, dt=F32):
        return self.ctx.enter_context(self.nc.psum_tensor(self.prefix + name, shape, dt))

    def sem(self, name):
        self.sems.append(self.nc.alloc_semaphore(self.prefix + name))
        return self.sems[-1]


def layernorm_stats(v, link, x, st, small, std, var_ready, n_var, std_ready):
    for j in range(J):
        v.bn_stats(st[:, j, :], x[:, j, :]).then_inc(link.sem, 1)
    link.loop_end(J)
    v.wait_ge(link.sem, link.n)
    mean, rstd, a, b, c = (small[:, i, :] for i in range(5))
    link(v.tensor_tensor(a, st[:, :, 1], st[:, :, 4], ALU.add))
    link(v.tensor_scalar(mean, a, 0.5, None, ALU.mult))
    link(v.tensor_tensor(b, st[:, :, 1], st[:, :, 4], ALU.subtract))
    link(v.tensor_tensor(b, b, b, ALU.mult))
    link(v.tensor_tensor(c, st[:, :, 2], st[:, :, 5], ALU.add))
    link(v.scalar_tensor_tensor(c, b, D / 4.0, c, ALU.mult, ALU.add))
    v.tensor_scalar(a, c, 1.0 / D, EPS, ALU.mult, ALU.add).then_inc(var_ready, 1)
    v.wait_ge(std_ready, n_var)
    link(v.reciprocal(rstd, std))


def layernorm_apply(v, link, xl, x, small, ready=None):
    for j in range(J):
        v.tensor_scalar(xl[:, j, :], x[:, j, :],
                        small[:, 0, j:j + 1], small[:, 1, j:j + 1],
                        ALU.subtract, ALU.mult).then_inc(ready or link.sem, 1)
    if ready:
        v.wait_ge(ready, J)
    else:
        link.loop_end(J)
        v.wait_ge(link.sem, link.n)


def three_parts(v, link, parts, rest, value):
    link(v.tensor_copy(parts[0], value))
    link(v.tensor_tensor(rest, value, parts[0], ALU.subtract))
    link(v.tensor_copy(parts[1], rest))
    link(v.tensor_tensor(rest, rest, parts[1], ALU.subtract))
    link(v.tensor_copy(parts[2], rest))


def constants(nc, c):
    with ExitStack() as ctx:
        m = Memory(nc, ctx, "constants_")
        row_i = m.sb("row_i", [128, 128], I32)
        col_i = m.sb("col_i", [128, 1], I32)
        iotas = m.sem("iotas")
        chain = m.sem("const_chain")
        with nc.Block() as block:

            @block.gpsimd
            def _(pool):
                pool.iota(row_i[:], pattern=[[1, 128]], base=0, channel_multiplier=0).then_inc(iotas, 1)
                pool.iota(col_i[:], pattern=[[0, 1]], base=0, channel_multiplier=1).then_inc(iotas, 1)

            @block.vector
            def _(v):
                link = Link(v, chain)
                v.wait_ge(iotas, 2)
                link(v.tensor_copy(c.row[:], row_i[:]))
                link(v.tensor_copy(c.col[:], col_i[:]))
                link(v.tensor_copy(c.row_b[:], c.row[:, 0:128]))
                link(v.tensor_scalar(c.ident[:], c.row[:, 0:128], c.col[:, 0:1], None, ALU.is_equal))
                link(v.memset(c.ones[:], 1.0))
                link(v.memset(c.zeros_b[:], 0.0))


def block_gcn(nc, c, io):
    with ExitStack() as ctx:
        m = Memory(nc, ctx, "gcn_")
        rows_i = m.sb("rows_i", [R1, 2, C1, Q1], I32)
        rows_f = m.sb("rows_f", [R1, 2, C1, Q1])
        rows_hi = m.sb("rows_hi", [R1, 2, C1, Q1])
        rows_lo = m.sb("rows_lo", [R1, 2, C1, Q1])
        rows_hi_b = m.sb("rows_hi_b", [R1, C1, Q1], BF16)
        dst_hi = m.sb("dst_hi", [Q1, T1])
        lo = m.sb("lo", [Q1, 2, T1], BF16)
        lo_hot = m.sb("lo_hot", [Q1, 2, T1, J], BF16)
        hi_line = m.sb("hi_line", [P, 2, G1 * Q1], BF16)
        hi_hot_t = m.sb("hi_hot_t", [P, 2, G1 * Q1], BF16)
        hi_hot = m.sb("hi_hot", [Q1, 2, G1, P], BF16)
        found = m.sb("found", [Q1, G1, J])
        val = m.sb("val", [Q1, G1])
        val_rest = m.sb("val_rest", [Q1, G1])
        val_b = m.sb("val_b", [Q1, 3, G1], BF16)
        payload = m.sb("payload", [Q1, 2, G1, 3, J], BF16)
        st = m.sb("st", [P, J, BN])
        small = m.sb("small", [P, 5, J])
        std = m.sb("std", [P, 2, J])
        gcn_w = m.sb("gcn_w", [P, D])
        gcn_b = m.sb("gcn_b", [P, 1])
        prod = m.sb("prod", [P, J, D])
        h = m.sb("h", [P, J])
        deg = m.sb("deg", [P, J])
        dis = m.sb("dis", [P, J])
        hd = m.sb("hd", [P, J])
        hd_rest = m.sb("hd_rest", [P, J])
        hd_b = m.sb("hd_b", [P, 3, J], BF16)
        sums = m.sb("sums", [P, 3, J])
        spa = m.sb("spa", [P, J])
        w1 = m.sb("w1", [128, K, 128])
        w2 = m.sb("w2", [128, D])
        b1 = m.sb("b1", [128, 1])
        b2 = m.sb("b2", [1, D])
        mean = m.sb("mean", [128, K])
        hidden = m.sb("hidden", [128, 1])
        hidden_row = m.sb("hidden_row", [128, P])
        gate1 = m.sb("gate1", [P, D])
        zeros = m.sb("zeros", [128, D])

        turned = [m.ps(f"turned{i}", [Q1, T1]) for i in range(3)]
        looked = [m.ps(f"looked{i}", [Q1, G1 * J]) for i in range(2)]
        ps_deg = m.ps("ps_deg", [P, J])
        ps_sum = m.ps("ps_sum", [P, 3 * J])
        ps_gate = m.ps("ps_gate", [128, D + 8])

        x_in, edges_in, gcn_in, gate_in = (m.sem(n) for n in ("x_in", "edges_in", "gcn_in", "gate_in"))
        hi_ready, hi_out = m.sem("hi_ready"), m.sem("hi_out")
        line_in = [m.sem(f"line_in{i}") for i in range(2)]
        ids_ready, ids_turned = m.sem("ids_ready"), m.sem("ids_turned")
        var_ready, std_ready = m.sem("var_ready"), m.sem("std_ready")
        xl_ready, mean_sum, mean_ready = m.sem("xl_ready"), m.sem("mean_sum"), m.sem("mean_ready")
        hidden_sum, hidden_ready = m.sem("hidden_sum"), m.sem("hidden_ready")
        gate_sum, gate_ready = m.sem("gate_sum"), m.sem("gate_ready")
        hot_ready, hot_free = m.sem("hot_ready"), m.sem("hot_free")
        deg_summed = m.sem("deg_summed")
        hot_t_ready, looked_up, looked_free = m.sem("hot_t_ready"), m.sem("looked_up"), m.sem("looked_free")
        payload_ready, all_summed = m.sem("payload_ready"), m.sem("all_summed")
        spa_in, spa_ready = m.sem("spa_in"), m.sem("spa_ready")
        zeroed, table_out = m.sem("zeroed"), m.sem("table_out")
        chain = m.sem("gcn_chain")
        with nc.Block() as block:

            @block.sync
            def _(sp):
                sp.dma_start(rows_i[:, 0, :, :], io["src"].rearrange("(c r q) -> r c q", r=R1, q=Q1)).then_inc(edges_in, 16)
                sp.dma_start(rows_i[:, 1, :, :], io["dst"].rearrange("(c r q) -> r c q", r=R1, q=Q1)).then_inc(edges_in, 16)
                sp.dma_start(c.x[:], io["x"].rearrange("(p j) d -> p j d", j=J)).then_inc(x_in, 16)
                sp.dma_start(gcn_w[:], io["L0_gnn_gcn_w"].rearrange("d o -> o d").broadcast_to([P, D])).then_inc(gcn_in, 16)
                sp.dma_start(gcn_b[:], io["L0_gnn_gcn_b"].unsqueeze(0).broadcast_to([P, 1])).then_inc(gcn_in, 16)
                sp.dma_start(w1[:], io["L0_gnn_w1"].rearrange("(k p) r -> p k r", p=128)).then_inc(gate_in, 16)
                sp.dma_start(w2[:], io["L0_gnn_w2"]).then_inc(gate_in, 16)
                sp.dma_start(b1[:], io["L0_gnn_b1"].unsqueeze(1)).then_inc(gate_in, 16)
                sp.dma_start(b2[:], io["L0_gnn_b2"].unsqueeze(0)).then_inc(gate_in, 16)
                sp.wait_ge(hi_ready, 1)
                sp.dma_start(c.hi_line_dram.rearrange("(c r q) -> r c q", r=R1, q=Q1), rows_hi_b[:]).then_inc(hi_out, 16)
                sp.wait_ge(hi_out, 16)
                lines = c.hi_line_dram.rearrange("(b e) -> b e", e=G1 * Q1)
                for s in range(2):
                    sp.dma_start(hi_line[:, s, :], lines[s:s + 1, :].broadcast_to([P, G1 * Q1])).then_inc(line_in[s], 16)
                with sp.Fori(1, B1 // 2) as b:
                    for s in range(2):
                        sp.wait_ge(hot_t_ready, b * 2 + (s - 1))
                        sp.dma_start(hi_line[:, s, :], lines[bass.ds(b * 2 + s, 1), :].broadcast_to([P, G1 * Q1])).then_inc(line_in[s], 16)

            @block.gpsimd
            def _(pool):
                pool.memset(zeros[:], 0.0).then_inc(zeroed, 1)
                pool.wait_ge(zeroed, 1)
                pool.wait_ge(xl_ready, 1)
                pool.dma_start(c.slot_table.rearrange("(t p) d -> p t d", p=128),
                               spread(zeros[:], 1, [128, c.slot_table.shape[0] // 128, D])).then_inc(table_out, 16)
                pool.wait_ge(table_out, 16)

            @block.scalar
            def _(act):
                act.wait_ge(var_ready, 1)
                act.activation(std[:, 0, :], small[:, 2, :], ACT.Sqrt).then_inc(std_ready, 1)
                act.wait_ge(var_ready, 2)
                act.activation(std[:, 1, :], deg[:], ACT.Sqrt).then_inc(std_ready, 1)
                act.wait_ge(gate_sum, 1)
                act.activation(gate1[:], ps_gate[0:P, 0:D], ACT.Sigmoid).then_inc(gate_ready, 1)
                act.wait_ge(spa_in, 1)
                act.activation(spa[:], hd_rest[:], ACT.Sigmoid).then_inc(spa_ready, 1)

            @block.tensor
            def _(pe):
                pe.wait_ge(ids_ready, 1)
                for i, rows in enumerate((rows_hi[:, 1, :, :], rows_lo[:, 0, :, :], rows_lo[:, 1, :, :])):
                    for b in range(C1):
                        ins = pe.transpose(turned[i][:, b * R1:(b + 1) * R1], rows[:, b, :], c.ident[0:R1, 0:R1])
                ins.then_inc(ids_turned, 1)
                pe.wait_ge(xl_ready, 1)
                for k in range(K):
                    for j in range(J):
                        ins = pe.matmul(ps_gate[:, D + k:D + k + 1], c.xl[:, j, k * 128:(k + 1) * 128],
                                        c.ones[0:P, 0:1], start=(j == 0), stop=(j == J - 1))
                ins.then_inc(mean_sum, 1)
                pe.matmul(ps_deg[:], c.zeros_b[0:Q1, 0:P], c.zeros_b[0:Q1, 0:J], start=True, stop=False, skip_group_check=True)
                with pe.Fori(0, B1 // 2) as b:
                    for s in range(2):
                        pe.wait_ge(hot_ready, b * 2 + (s + 1))
                        for g in range(G1):
                            ins = pe.matmul(ps_deg[:], hi_hot[:, s, g, :],
                                            lo_hot[:, 1, bass.ds(b * (2 * G1) + (s * G1 + g), 1), :].squeeze(1),
                                            start=False, stop=False, skip_group_check=True)
                        ins.then_inc(hot_free, 1)
                pe.matmul(ps_deg[:], c.zeros_b[0:Q1, 0:P], c.zeros_b[0:Q1, 0:J], start=False, stop=True,
                          skip_group_check=True).then_inc(deg_summed, 1)
                pe.wait_ge(mean_ready, 1)
                pe.wait_ge(gate_in, 64)
                for k in range(K):
                    ins = pe.matmul(ps_gate[:, D + 4:D + 5], w1[:, k, :], mean[:, k:k + 1], start=(k == 0), stop=(k == K - 1))
                ins.then_inc(hidden_sum, 1)
                pe.wait_ge(hidden_ready, 1)
                pe.matmul(ps_gate[0:P, 0:D], hidden_row[:], w2[:], start=True, stop=False)
                pe.matmul(ps_gate[0:P, 0:D], c.ones[0:1, 0:P], b2[:], start=False, stop=True).then_inc(gate_sum, 1)
                pe.matmul(ps_sum[:], c.zeros_b[0:Q1, 0:P], c.zeros_b[0:Q1, 0:3 * J], start=True, stop=False, skip_group_check=True)

                def look(i, s):
                    pe.wait_ge(hot_t_ready, i + 1)
                    pe.wait_ge(looked_free, i + 1)
                    for g in range(G1):
                        for part in range(3):
                            ins = pe.matmul(looked[s][:, g * J:(g + 1) * J], hi_hot_t[:, s, g * Q1:(g + 1) * Q1],
                                            hd_b[:, part, :], start=(part == 0), stop=(part == 2))
                    ins.then_inc(looked_up, 1)

                def add_up(i, s):
                    pe.wait_ge(payload_ready, i + 1)
                    for g in range(G1):
                        ins = pe.matmul(ps_sum[:], hi_hot[:, s, g, :], payload[:, s, g, :, :],
                                        start=False, stop=False, skip_group_check=True)
                    ins.then_inc(hot_free, 1)

                look(0, 0)
                with pe.Fori(0, B1 // 2 - 1) as b:
                    for s in range(2):
                        look(b * 2 + (s + 1), (s + 1) % 2)
                        add_up(b * 2 + s, s)
                look(B1 - 1, 1)
                add_up(B1 - 2, 0)
                add_up(B1 - 1, 1)
                pe.matmul(ps_sum[:], c.zeros_b[0:Q1, 0:P], c.zeros_b[0:Q1, 0:3 * J], start=False, stop=True,
                          skip_group_check=True).then_inc(all_summed, 1)

            @block.vector
            def _(v):
                link = Link(v, chain)
                v.sem_inc(hot_free, 2)
                v.sem_inc(looked_free, 2)
                v.wait_ge(edges_in, 32)
                link(v.tensor_copy(rows_f[:], rows_i[:]))
                link(v.tensor_scalar(rows_hi[:], rows_f[:], -float(J // 2), 1.0 / J, ALU.add, ALU.mult))
                link(v.tensor_scalar(rows_hi[:], rows_hi[:], ROUND, -ROUND, ALU.add, ALU.add))
                v.tensor_copy(rows_hi_b[:], rows_hi[:, 0, :, :]).then_inc(hi_ready, 1)
                v.scalar_tensor_tensor(rows_lo[:], rows_hi[:], -float(J), rows_f[:], ALU.mult, ALU.add).then_inc(ids_ready, 1)
                v.wait_ge(x_in, 16)
                layernorm_stats(v, link, c.x, st, small, std[:, 0, :], var_ready, 1, std_ready)
                layernorm_apply(v, link, c.xl, c.x, small)
                v.sem_inc(xl_ready, 1)
                v.wait_ge(ids_turned, 1)
                link(v.tensor_copy(dst_hi[:], turned[0][:]))
                link(v.tensor_copy(lo[:, 0, :], turned[1][:]))
                link(v.tensor_copy(lo[:, 1, :], turned[2][:]))
                for i in range(2):
                    link(v.tensor_tensor(lo_hot[:, i, :, :], spread(lo[:, i, :], 2, [Q1, T1, J]),
                                         spread(c.row_b[0:Q1, 0:J], 1, [Q1, T1, J]), ALU.is_equal))

                def hot(b, s):
                    v.tensor_tensor(hi_hot[:, s, :, :], spread(dst_hi[:, bass.ds(b * (2 * G1) + s * G1, G1)], 2, [Q1, G1, P]),
                                    spread(c.row_b[0:Q1, 0:P], 1, [Q1, G1, P]), ALU.is_equal).then_inc(hot_ready, 1)

                with v.Fori(0, B1 // 2) as b:
                    for s in range(2):
                        v.wait_ge(hot_free, b * 2 + (s + 1))
                        hot(b, s)
                v.wait_ge(gcn_in, 32)
                link(v.tensor_tensor(prod[:], c.xl[:], spread(gcn_w[:], 1, [P, J, D]), ALU.mult))
                link(v.tensor_reduce(h[:], prod[:], AX_X, ALU.add))
                v.wait_ge(mean_sum, 1)
                v.tensor_scalar(mean[:], ps_gate[:, D:D + K], 1.0 / N, None, ALU.mult).then_inc(mean_ready, 1)
                v.wait_ge(deg_summed, 1)
                link(v.tensor_copy(c.deg[:], ps_deg[:]))
                v.tensor_scalar(deg[:], ps_deg[:], 1.0, None, ALU.add).then_inc(var_ready, 1)
                v.wait_ge(std_ready, 2)
                link(v.reciprocal(dis[:], std[:, 1, :]))
                link(v.tensor_tensor(hd[:], h[:], dis[:], ALU.mult))
                three_parts(v, link, [hd_b[:, i, :] for i in range(3)], hd_rest[:], hd[:])
                v.wait_ge(hidden_sum, 1)
                link(v.tensor_scalar(hidden[:], ps_gate[:, D + 4:D + 5], b1[:], 0.0, ALU.add, ALU.max))
                v.tensor_copy(hidden_row[:], hidden[:, 0:1].broadcast_to([128, P])).then_inc(hidden_ready, 1)

                def compare(b, s):
                    v.wait_ge(line_in[s], b * 16 + 16)
                    v.tensor_scalar(hi_hot_t[:, s, :], hi_line[:, s, :], c.col[0:P, 0:1], None,
                                    ALU.is_equal).then_inc(hot_t_ready, 1)

                def payloads(i, s):
                    v.wait_ge(hot_free, i + (B1 + 1))
                    now = slice(i * G1, (i + 1) * G1) if isinstance(i, int) else bass.ds(i * G1, G1)
                    v.tensor_tensor(hi_hot[:, s, :, :], spread(dst_hi[:, now], 2, [Q1, G1, P]),
                                    spread(c.row_b[0:Q1, 0:P], 1, [Q1, G1, P]), ALU.is_equal)
                    v.wait_ge(looked_up, i + 1)
                    v.tensor_tensor(found[:], looked[s].rearrange("q (g j) -> q g j", j=J), lo_hot[:, 0, now, :],
                                    ALU.mult).then_inc(looked_free, 1)
                    v.wait_ge(looked_free, i + 3)
                    link.at(v.tensor_reduce(val[:], found[:], AX_X, ALU.add), i * 6 + 1)
                    link.at(v.tensor_copy(val_b[:, 0, :], val[:]), i * 6 + 2)
                    link.at(v.tensor_tensor(val_rest[:], val[:], val_b[:, 0, :], ALU.subtract), i * 6 + 3)
                    link.at(v.tensor_copy(val_b[:, 1, :], val_rest[:]), i * 6 + 4)
                    link.at(v.tensor_tensor(val_rest[:], val_rest[:], val_b[:, 1, :], ALU.subtract), i * 6 + 5)
                    link.at(v.tensor_copy(val_b[:, 2, :], val_rest[:]), i * 6 + 6)
                    for part in range(3):
                        ins = v.tensor_tensor(payload[:, s, :, part, :], lo_hot[:, 1, now, :],
                                              spread(val_b[:, part, :], 2, [Q1, G1, J]), ALU.mult)
                    ins.then_inc(payload_ready, 1)

                compare(0, 0)
                with v.Fori(0, B1 // 2 - 1) as b:
                    compare(b, 1)
                    payloads(b * 2, 0)
                    compare(b + 1, 0)
                    payloads(b * 2 + 1, 1)
                compare(B1 // 2 - 1, 1)
                payloads(B1 - 2, 0)
                payloads(B1 - 1, 1)
                link.loop_end(6 * B1)
                v.wait_ge(all_summed, 1)
                link(v.tensor_copy(sums[:], ps_sum.rearrange("p (i j) -> p i j", j=J)))
                link(v.tensor_tensor(sums[:, 1, :], sums[:, 1, :], sums[:, 2, :], ALU.add))
                link(v.tensor_tensor(sums[:, 0, :], sums[:, 0, :], sums[:, 1, :], ALU.add))
                link(v.tensor_tensor(sums[:, 0, :], sums[:, 0, :], hd[:], ALU.add))
                link(v.tensor_tensor(sums[:, 0, :], sums[:, 0, :], dis[:], ALU.mult))
                v.tensor_scalar(hd_rest[:], sums[:, 0, :], gcn_b[:], None, ALU.add).then_inc(spa_in, 1)
                v.wait_ge(gate_ready, 1)
                link(v.tensor_scalar(gate1[:], gate1[:], 1.0, None, ALU.add))
                v.wait_ge(spa_ready, 1)
                for j in range(J):
                    v.scalar_tensor_tensor(prod[:, j, :], gate1[:], spa[:, j:j + 1],
                                           c.xl[:, j, :], ALU.add, ALU.mult).then_inc(chain, 1)
                link.loop_end(J)
                v.wait_ge(chain, link.n)
                link(v.tensor_tensor(c.x[:], c.x[:], prod[:], ALU.add))


def transpose_nodes(pe, c, ps, xl_ready, ps_free, turned):
    i = 0
    for j0 in range(0, J, 4):
        js = range(j0, min(j0 + 4, J))
        pe.wait_ge(xl_ready, js[-1] + 1)
        for k in range(K):
            if i >= 2:
                pe.wait_ge(ps_free, i - 1)
            for j in js:
                ins = pe.transpose(ps[i % 2][:, (j - j0) * P:(j - j0 + 1) * P], c.xl[:, j, k * 128:(k + 1) * 128],
                                   c.ident[0:P, 0:P])
            ins.then_inc(turned, 1)
            i += 1


def copy_turned(act, c, ps, ps_free, turned):
    i = 0
    for j0 in range(0, J, 4):
        n = min(4, J - j0) * P
        for k in range(K):
            act.wait_ge(turned, i + 1)
            act.copy(c.xt[:, k, j0 * P:j0 * P + n], ps[i % 2][:, 0:n]).then_inc(ps_free, 1)
            i += 1


TURNS = K * ((J + 3) // 4)


def top2_gates(v, link, s, gates, chosen, t, big, tri, exp_in, exp_out, n_exp):
    e = s.shape[2]
    s_i = spread(s, 3, [P, J, e, e])
    s_k = spread(s, 2, [P, J, e, e])
    rank, top, rsum = t[:, :, :, 0], t[:, :, 0, 1], t[:, :, 0, 2]
    link(v.tensor_tensor(big, s_k, s_i, ALU.is_equal))
    link(v.tensor_tensor(big.rearrange("p j i k -> p j (i k)"), big.rearrange("p j i k -> p j (i k)"),
                         spread(tri, 1, [P, J, e * e]), ALU.mult))
    link(v.tensor_reduce(rank, big, AX_X, ALU.add))
    link(v.tensor_tensor(big, s_k, s_i, ALU.is_gt))
    link(v.tensor_reduce(t[:, :, :, 3], big, AX_X, ALU.add))
    link(v.tensor_tensor(rank, rank, t[:, :, :, 3], ALU.add))
    link(v.tensor_scalar(rank, rank, 2.0, None, ALU.is_lt))
    link(v.tensor_copy(chosen.rearrange("p e j -> p j e"), rank))
    link(v.tensor_reduce(top, s, AX_X, ALU.max))
    v.tensor_tensor(exp_in, s, spread(top, 2, [P, J, e]), ALU.subtract).then_inc(n_exp[0], 1)
    v.wait_ge(n_exp[1], n_exp[2])
    link(v.tensor_tensor(exp_out, exp_out, rank, ALU.mult))
    link(v.tensor_reduce(rsum, exp_out, AX_X, ALU.add))
    link(v.reciprocal(rsum, rsum))
    link(v.tensor_tensor(gates.rearrange("p e j -> p j e"), exp_out, spread(rsum, 2, [P, J, e]), ALU.mult))


def block_gat_tables(nc, c, io):
    with ExitStack() as ctx:
        m = Memory(nc, ctx, "gat_tables_")
        st = m.sb("st", [P, J, BN])
        small = m.sb("small", [P, 5, J])
        std = m.sb("std", [P, J])
        w_gat = m.sb("w_gat", [128, K, HX])
        att = m.sb("att", [P, 2, HX])
        prod = m.sb("prod", [P, J, HX])
        ps_turn = [m.ps(f"ps_turn{i}", [128, 512]) for i in range(2)]
        ps_h = m.ps("ps_h", [P, J * HX])
        w_in, var_ready, std_ready = m.sem("w_in"), m.sem("var_ready"), m.sem("std_ready")
        xl_ready, turned, turn_free = m.sem("xl_ready"), m.sem("turned"), m.sem("turn_free")
        h_summed, table_ready, table_out = m.sem("h_summed"), m.sem("table_ready"), m.sem("table_out")
        most_in, most_out = m.sem("most_in"), m.sem("most_out")
        chain = m.sem("tab_chain")
        with nc.Block() as block:

            @block.sync
            def _(sp):
                sp.dma_start(w_gat[:], io["L0_ffn_W_gat"].rearrange("(k p) r -> p k r", p=128)).then_inc(w_in, 16)
                for i, name in enumerate(("L0_ffn_att_src", "L0_ffn_att_dst")):
                    sp.dma_start(att[:, i, :], io[name].rearrange("h e -> (h e)").unsqueeze(0).broadcast_to([P, HX])).then_inc(w_in, 16)
                sp.wait_ge(table_ready, 1)
                sp.dma_start(c.h_table.rearrange("(p j) f -> p j f", j=J), c.h[:]).then_inc(table_out, 16)
                sp.wait_ge(table_out, 16)

            @block.gpsimd
            def _(pool):
                pool.wait_ge(most_in, 1)
                pool.partition_all_reduce(c.most[:], c.most_of[:], 128, bass.bass_isa.ReduceOp.max).then_inc(most_out, 1)

            @block.scalar
            def _(act):
                act.wait_ge(var_ready, 1)
                act.activation(std[:], small[:, 2, :], ACT.Sqrt).then_inc(std_ready, 1)
                copy_turned(act, c, ps_turn, turn_free, turned)

            @block.tensor
            def _(pe):
                transpose_nodes(pe, c, ps_turn, xl_ready, turn_free, turned)
                pe.wait_ge(turn_free, TURNS)
                pe.wait_ge(w_in, 48)
                for j in range(J):
                    for k in range(K):
                        ins = pe.matmul(ps_h[:, j * HX:(j + 1) * HX], c.xt[:, k, j * P:(j + 1) * P], w_gat[:, k, :],
                                        start=(k == 0), stop=(k == K - 1))
                ins.then_inc(h_summed, 1)

            @block.vector
            def _(v):
                link = Link(v, chain)
                layernorm_stats(v, link, c.x, st, small, std[:], var_ready, 1, std_ready)
                layernorm_apply(v, link, c.xl, c.x, small, xl_ready)
                link(v.memset(c.most_of[:], -3e38))
                v.wait_ge(h_summed, 1)
                v.wait_ge(w_in, 48)
                link(v.tensor_copy(c.h[:, :, 0:HX], ps_h.rearrange("p (j r) -> p j r", r=HX)))
                for i, out in enumerate((c.h[:, :, HX:HF], c.a_dst[:])):
                    link(v.tensor_tensor(prod[:], c.h[:, :, 0:HX], spread(att[:, i, :], 1, [P, J, HX]), ALU.mult))
                    link(v.tensor_reduce(out, prod.rearrange("p j (h e) -> p j h e", e=NE0), AX_X, ALU.add))
                v.sem_inc(table_ready, 1)
                link(v.tensor_reduce(c.most_of[0:P, :], c.h[:, :, HX:HF].rearrange("p j h -> p h j"), AX_X, ALU.max))
                v.sem_inc(most_in, 1)
                v.wait_ge(most_out, 1)


def block_gat_edges(nc, c, io):
    with ExitStack() as ctx:
        m = Memory(nc, ctx, "gat_edges_")
        rows_i = m.sb("rows_i", [R2, 2, C2, Q2], I32)
        rows_f = m.sb("rows_f", [R2, 2, C2, Q2])
        rows_hi = m.sb("rows_hi", [R2, C2, Q2])
        rows_lo = m.sb("rows_lo", [R2, C2, Q2])
        rows_hi_b = m.sb("rows_hi_b", [R2, C2, Q2], BF16)
        dst_hi = m.sb("dst_hi", [Q2, T2])
        dst_lo = m.sb("dst_lo", [Q2, T2], BF16)
        src_i = m.sb("src_i", [Q2, T2], I32)
        lo_hot = m.sb("lo_hot", [Q2, T2, J], BF16)
        hi_line = m.sb("hi_line", [P, 2, G2 * Q2], BF16)
        hi_hot_t = m.sb("hi_hot_t", [P, 2, G2 * Q2], BF16)
        hi_hot = m.sb("hi_hot", [Q2, 2, G2, P])
        payload = m.sb("payload", [Q2, 2, G2, J * HF])
        zero_i = m.sb("zero_i", [128, G2], I32)
        spare_i = m.sb("spare_i", [128, 1], I32)
        stage = m.sb("stage", [Q2, S2, G2], I32)
        ring = m.sb("ring", [Q2, S2, G2, HF])
        rows = m.sb("rows", [Q2, 2, G2, HF])
        a_dst_e = m.sb("a_dst_e", [Q2, 2, G2, HEADS])
        logit = m.sb("logit", [Q2, 2, G2, HEADS])
        cap = m.sb("cap", [Q2, 2, G2, HEADS])
        below = m.sb("below", [Q2, 2, G2, HEADS])
        ex = m.sb("ex", [Q2, 2, G2, HEADS])
        found = m.sb("found", [Q2, 2, G2, J, HEADS])
        a_rest = m.sb("a_rest", [P, J, HEADS])
        a_b = m.sb("a_b", [P, 3, J, HEADS], BF16)
        own = m.sb("own", [P, 3, J, HEADS])
        agg = m.sb("agg", [P, J, HF])
        params = m.sb("params", [P, 3, HX])
        sq = m.sb("sq", [P, J, HX])
        stat = m.sb("stat", [P, 4, J])
        score = m.sb("score", [P, J, NE0])
        t = m.sb("gate_t", [P, J, NE0, 4])
        big = m.sb("gate_big", [P, J, NE0, NE0])
        tri = m.sb("tri", [P, NE0 * NE0])
        exp_in = m.sb("exp_in", [P, J, NE0])
        exp_out = m.sb("exp_out", [P, J, NE0])
        turned = [m.ps(f"turned{i}", [Q2, T2]) for i in range(2)]
        looked = [m.ps(f"looked{i}", [Q2, 2, 512]) for i in range(2)]
        ps_sum = m.ps("ps_sum", [P, 512])
        names = ("ids_in", "par_in", "hi_ready", "hi_out", "rows_ready", "ids_turned", "src_ready", "staged", "ring_free",
                 "hot_t_ready", "looked_up", "looked_free", "logit_chain", "exp_ready", "exp_done", "self_in",
                 "self_done", "payload_ready", "payload_free", "all_summed", "var_ready", "std_ready", "gate_in", "gate_out",
                 "edge_chain", "found_done")
        s_ = {n: m.sem("ge_" + n) for n in names}
        line_in = [m.sem(f"ge_line_in{i}") for i in range(2)]
        gathered = [m.sem(f"ge_gathered{i}") for i in range(S2)]
        some = lambda i, n: bass.ds(i, n) if not isinstance(i, int) else slice(i, i + n)
        with nc.Block() as block:

            @block.sync
            def _(sp):
                for i in range(2):
                    sp.dma_start(rows_i[:, i, :, :], io["L0_ffn_edge_index"][i].rearrange("(c r q) -> r c q", r=R2, q=Q2)).then_inc(s_["ids_in"], 16)
                for i, name in enumerate(("L0_ffn_b_gat", "L0_ffn_ln_gamma", "L0_ffn_ln_beta")):
                    sp.dma_start(params[:, i, :], io[name].unsqueeze(0).broadcast_to([P, HX])).then_inc(s_["par_in"], 16)
                sp.wait_ge(s_["hi_ready"], 1)
                sp.dma_start(c.hi_line_dram2.rearrange("(c r q) -> r c q", r=R2, q=Q2), rows_hi_b[:]).then_inc(s_["hi_out"], 16)
                sp.wait_ge(s_["hi_out"], 16)
                lines = c.hi_line_dram2.rearrange("(b e) -> b e", e=G2 * Q2)
                for s in range(2):
                    sp.dma_start(hi_line[:, s, :], lines[s:s + 1, :].broadcast_to([P, G2 * Q2])).then_inc(line_in[s], 16)
                with sp.Fori(1, B2 // 2) as b:
                    for s in range(2):
                        sp.wait_ge(s_["hot_t_ready"], b * 2 + (s - 1))
                        sp.dma_start(hi_line[:, s, :], lines[bass.ds(b * 2 + s, 1), :].broadcast_to([P, G2 * Q2])).then_inc(line_in[s], 16)

            @block.gpsimd
            def _(pool):
                pool.memset(zero_i[:], 0).then_inc(s_["staged"], 1)
                pool.sem_inc(s_["ring_free"], S2)
                pool.wait_ge(s_["src_ready"], 1)
                pool.wait_ge(s_["staged"], 1)
                with pool.Fori(0, B2 // S2) as b:
                    for s in range(S2):
                        ids = src_i[:, bass.ds(b * (S2 * G2) + s * G2, G2)]
                        pool.wait_ge(s_["ring_free"], b * S2 + (s + 1))
                        pool.tensor_tensor(stage[:, s, :], ids, zero_i[:], ALU.add).then_inc(s_["staged"], 1)
                        pool.wait_ge(s_["staged"], b * S2 + (s + 2))
                        pool.tensor_tensor(spare_i[:], zero_i[:, 0:1], zero_i[:, 1:2], ALU.add)
                        for u in range(G2):
                            pool.indirect_dma_start(ring[:, s, u, :], None, c.h_table,
                                                    bass.IndirectOffsetOnAxis(ap=stage[:, s, u:u + 1], axis=0)).then_inc(gathered[s], 16)

            @block.scalar
            def _(act):
                act.wait_ge(s_["self_in"], 1)
                act.activation(own[:, 2, :, :], own[:, 1, :, :], ACT.Exp).then_inc(s_["self_done"], 1)
                with act.Fori(0, B2 // 2) as b:
                    for s in range(2):
                        act.wait_ge(s_["exp_ready"], b * 2 + (s + 1))
                        act.activation(ex[:, s, :, :], below[:, s, :, :], ACT.Exp).then_inc(s_["exp_done"], 1)
                act.wait_ge(s_["var_ready"], 1)
                act.activation(stat[:, 2, :], stat[:, 1, :], ACT.Sqrt).then_inc(s_["std_ready"], 1)
                act.wait_ge(s_["gate_in"], 1)
                act.activation(exp_out[:], exp_in[:], ACT.Exp).then_inc(s_["gate_out"], 1)

            @block.tensor
            def _(pe):
                pe.wait_ge(s_["rows_ready"], 1)
                for b in range(C2):
                    pe.transpose(turned[0][:, b * R2:(b + 1) * R2], rows_f[:, 0, b, :], c.ident[:])
                for b in range(C2):
                    ins = pe.transpose(turned[1][:, b * R2:(b + 1) * R2], rows_hi[:, b, :], c.ident[:])
                ins.then_inc(s_["ids_turned"], 1)
                pe.wait_ge(s_["src_ready"], 1)
                for b in range(C2):
                    ins = pe.transpose(turned[0][:, b * R2:(b + 1) * R2], rows_lo[:, b, :], c.ident[:])
                ins.then_inc(s_["ids_turned"], 1)

                def look(i, s):
                    pe.wait_ge(s_["hot_t_ready"], i + 1)
                    pe.wait_ge(s_["looked_free"], i + 1)
                    for g in range(G2):
                        for part in range(3):
                            ins = pe.matmul(looked[s][:, g // 4, (g % 4) * J * HEADS:(g % 4 + 1) * J * HEADS],
                                            hi_hot_t[:, s, g * Q2:(g + 1) * Q2], a_b[:, part, :, :],
                                            start=(part == 0), stop=(part == 2))
                    ins.then_inc(s_["looked_up"], 1)

                def add_up(i, s):
                    pe.wait_ge(s_["payload_ready"], i + 1)
                    for g in range(G2):
                        ins = pe.matmul(ps_sum[:, 0:J * HF], hi_hot[:, s, g, :], payload[:, s, g, :],
                                        start=False, stop=False, skip_group_check=True)
                    ins.then_inc(s_["payload_free"], 1)

                pe.matmul(ps_sum[:, 0:J * HF], c.zeros_b[0:Q2, 0:P], c.zeros_b[:, 0:1].broadcast_to([Q2, J * HF]), start=True, stop=False, skip_group_check=True)
                look(0, 0)
                look(1, 1)
                with pe.Fori(0, B2 // 2 - 1) as b:
                    for s in range(2):
                        look(b * 2 + (s + 2), s)
                        add_up(b * 2 + s, s)
                for s in range(2):
                    add_up(B2 - 2 + s, s)
                pe.matmul(ps_sum[:, 0:J * HF], c.zeros_b[0:Q2, 0:P], c.zeros_b[:, 0:1].broadcast_to([Q2, J * HF]), start=False, stop=True,
                          skip_group_check=True).then_inc(s_["all_summed"], 1)

            @block.vector
            def _(v):
                link = Link(v, s_["edge_chain"])
                v.sem_inc(s_["looked_free"], 2)
                v.sem_inc(s_["payload_free"], 2)
                v.wait_ge(s_["ids_in"], 32)
                link(v.tensor_copy(rows_f[:], rows_i[:]))
                link(v.tensor_scalar(rows_hi[:], rows_f[:, 1, :, :], -float(J // 2), 1.0 / J, ALU.add, ALU.mult))
                link(v.tensor_scalar(rows_hi[:], rows_hi[:], ROUND, -ROUND, ALU.add, ALU.add))
                v.tensor_copy(rows_hi_b[:], rows_hi[:]).then_inc(s_["hi_ready"], 1)
                v.scalar_tensor_tensor(rows_lo[:], rows_hi[:], -float(J), rows_f[:, 1, :, :], ALU.mult, ALU.add).then_inc(s_["rows_ready"], 1)
                v.wait_ge(s_["ids_turned"], 1)
                v.tensor_copy(src_i[:], turned[0][:]).then_inc(s_["src_ready"], 1)
                link(v.tensor_copy(dst_hi[:], turned[1][:]))
                three_parts(v, link, [a_b[:, i, :, :] for i in range(3)], a_rest[:], c.a_dst[:])
                v.wait_ge(s_["ids_turned"], 2)
                link(v.tensor_copy(dst_lo[:], turned[0][:]))
                link(v.tensor_tensor(lo_hot[:], spread(dst_lo[:], 2, [Q2, T2, J]), spread(c.row_b[0:Q2, 0:J], 1, [Q2, T2, J]), ALU.is_equal))
                most = spread(c.most[0:P, :], 1, [P, J, HEADS])
                link(v.tensor_tensor(own[:, 0, :, :], c.h[:, :, HX:HF], c.a_dst[:], ALU.add))
                link(v.scalar_tensor_tensor(own[:, 0, :, :], own[:, 0, :, :], 0.2, own[:, 0, :, :], ALU.mult, ALU.max))
                link(v.tensor_tensor(own[:, 1, :, :], c.a_dst[:], most, ALU.add))
                link(v.scalar_tensor_tensor(own[:, 1, :, :], own[:, 1, :, :], 0.2, own[:, 1, :, :], ALU.mult, ALU.max))
                v.tensor_tensor(own[:, 1, :, :], own[:, 0, :, :], own[:, 1, :, :], ALU.subtract).then_inc(s_["self_in"], 1)

                def compare(s, seen):
                    v.wait_ge(line_in[s], seen)
                    v.tensor_scalar(hi_hot_t[:, s, :], hi_line[:, s, :], c.col[0:P, 0:1], None,
                                    ALU.is_equal).then_inc(s_["hot_t_ready"], 1)

                def find(i, s):
                    v.wait_ge(s_["looked_up"], i + 1)
                    for half in range(2):
                        ins = v.tensor_tensor(found[:, s, half * 4:half * 4 + 4, :, :],
                                              looked[s][:, half, 0:4 * J * HEADS].rearrange("q (g j h) -> q g j h", g=4, j=J),
                                              spread(lo_hot[:, some(i * G2 + half * 4, 4), :], 3, [Q2, 4, J, HEADS]), ALU.mult)
                    ins.then_inc(s_["looked_free"], 1)
                    v.wait_ge(s_["looked_free"], i + 3)
                    v.tensor_reduce(a_dst_e[:, s, :, :], found[:, s, :, :, :].rearrange("q g j h -> q g h j"), AX_X, ALU.add).then_inc(s_["found_done"], 1)

                def logits(i, s, slot, seen):
                    v.wait_ge(s_["found_done"], i + 1)
                    v.tensor_tensor(cap[:, s, :, :], a_dst_e[:, s, :, :], spread(c.most[:], 1, [Q2, G2, HEADS]), ALU.add).then_inc(s_["logit_chain"], 1)
                    v.wait_ge(gathered[slot], seen)
                    v.tensor_tensor(logit[:, s, :, :], ring[:, slot, :, HX:HF], a_dst_e[:, s, :, :], ALU.add).then_inc(s_["logit_chain"], 1)
                    v.wait_ge(s_["logit_chain"], i * 4 + 2)
                    v.scalar_tensor_tensor(cap[:, s, :, :], cap[:, s, :, :], 0.2, cap[:, s, :, :], ALU.mult, ALU.max).then_inc(s_["logit_chain"], 1)
                    v.scalar_tensor_tensor(logit[:, s, :, :], logit[:, s, :, :], 0.2, logit[:, s, :, :], ALU.mult, ALU.max).then_inc(s_["logit_chain"], 1)
                    v.wait_ge(s_["logit_chain"], i * 4 + 4)
                    v.tensor_tensor(below[:, s, :, :], logit[:, s, :, :], cap[:, s, :, :], ALU.subtract).then_inc(s_["exp_ready"], 1)

                def payloads(i, s, slot):
                    v.wait_ge(s_["exp_done"], i + 1)
                    v.tensor_copy(rows[:, s, :, HX:HF], ex[:, s, :, :])
                    v.tensor_tensor(rows[:, s, :, 0:HX].rearrange("q t (h e) -> q t h e", e=NE0), ring[:, slot, :, 0:HX].rearrange("q t (h e) -> q t h e", e=NE0),
                                    spread(ex[:, s, :, :], 3, [Q2, G2, HEADS, NE0]), ALU.mult).then_inc(s_["ring_free"], 1)
                    v.wait_ge(s_["payload_free"], i + 1)
                    v.tensor_tensor(hi_hot[:, s, :, :], spread(dst_hi[:, some(i * G2, G2)], 2, [Q2, G2, P]),
                                    spread(c.row[0:Q2, 0:P], 1, [Q2, G2, P]), ALU.is_equal)
                    v.wait_ge(s_["ring_free"], i + (S2 + 1))
                    v.tensor_tensor(payload[:, s, :, :].rearrange("q g (j f) -> q g j f", f=HF),
                                    spread(lo_hot[:, some(i * G2, G2), :], 3, [Q2, G2, J, HF]),
                                    spread(rows[:, s, :, :], 2, [Q2, G2, J, HF]), ALU.mult).then_inc(s_["payload_ready"], 1)

                def step(i, k, rounds):
                    if not isinstance(i, int) or i + 1 < B2:
                        compare((k + 1) % 2, rounds * (16 * S2 // 2) + 16 * ((k + 1) // 2 + 1))
                    find(i, k % 2)
                    logits(i, k % 2, k % S2, rounds * (16 * G2) + 16 * G2 * (k // S2 + 1))
                    if not isinstance(i, int) or i:
                        payloads(i + (-1), (k - 1) % 2, (k - 1) % S2)

                compare(0, 16)
                step(0, 0, 0)
                with v.Fori(0, B2 // S2 - 1) as b:
                    for k in range(1, S2 + 1):
                        step(b * S2 + k, k, b)
                for k in range(1, S2):
                    step(B2 - S2 + k, k, B2 // S2 - 1)
                payloads(B2 - 1, (B2 - 1) % 2, (B2 - 1) % S2)
                v.wait_ge(s_["par_in"], 48)
                v.wait_ge(s_["all_summed"], 1)
                v.wait_ge(s_["self_done"], 1)
                link(v.tensor_copy(agg[:], ps_sum[:, 0:J * HF].rearrange("p (j f) -> p j f", f=HF)))
                by_head = lambda ap: ap.rearrange("p j (h e) -> p j h e", e=NE0)
                link(v.tensor_tensor(by_head(sq[:]), by_head(c.h[:, :, 0:HX]), spread(own[:, 2, :, :], 3, [P, J, HEADS, NE0]), ALU.mult))
                link(v.tensor_tensor(agg[:, :, 0:HX], agg[:, :, 0:HX], sq[:], ALU.add))
                link(v.tensor_tensor(agg[:, :, HX:HF], agg[:, :, HX:HF], own[:, 2, :, :], ALU.add))
                link(v.reciprocal(own[:, 0, :, :], agg[:, :, HX:HF]))
                link(v.tensor_tensor(by_head(sq[:]), by_head(agg[:, :, 0:HX]), spread(own[:, 0, :, :], 3, [P, J, HEADS, NE0]), ALU.mult))
                link(v.tensor_tensor(agg[:, :, 0:HX], sq[:], spread(params[:, 0, :], 1, [P, J, HX]), ALU.add))
                a16, mu, var, sd, rs = agg[:, :, 0:HX], stat[:, 0, :], stat[:, 1, :], stat[:, 2, :], stat[:, 3, :]
                link(v.tensor_reduce(mu, a16, AX_X, ALU.add))
                link(v.tensor_scalar(mu, mu, 1.0 / HX, None, ALU.mult))
                link(v.tensor_tensor(a16, a16, spread(mu, 2, [P, J, HX]), ALU.subtract))
                link(v.tensor_tensor(sq[:], a16, a16, ALU.mult))
                link(v.tensor_reduce(var, sq[:], AX_X, ALU.add))
                v.tensor_scalar(var, var, 1.0 / HX, EPS, ALU.mult, ALU.add).then_inc(s_["var_ready"], 1)
                v.wait_ge(s_["std_ready"], 1)
                link(v.reciprocal(rs, sd))
                link(v.tensor_tensor(a16, a16, spread(rs, 2, [P, J, HX]), ALU.mult))
                link(v.tensor_tensor(a16, a16, spread(params[:, 1, :], 1, [P, J, HX]), ALU.mult))
                link(v.tensor_tensor(a16, a16, spread(params[:, 2, :], 1, [P, J, HX]), ALU.add))
                link(v.tensor_reduce(score[:], a16.rearrange("p j (h e) -> p j e h", e=NE0), AX_X, ALU.add))
                link(v.tensor_scalar(score[:], score[:], 1.0 / HEADS, None, ALU.mult))
                lower_triangle(v, link, c, tri, NE0)
                top2_gates(v, link, score[:], c.gates[:, 0:NE0, :], c.chosen[:, 0:NE0, :], t[:], big[:], tri[:], exp_in[:], exp_out[:],
                           (s_["gate_in"], s_["gate_out"], 1))


def lower_triangle(v, link, c, tri, e):
    for i in range(e):
        ins = v.tensor_scalar(tri[:, i * e:(i + 1) * e], c.row[0:P, 0:e], float(i), None, ALU.is_lt)
    link(ins)


def route(v, link, c, experts, tiles, scratch, count_ready, counted, ps_cnt):
    e = experts
    count, triangle, before, size, start, run_a, run_b, slot, gate, slot_i, later, passed, expert_of = scratch
    chosen = c.chosen[:, 0:e, :]
    v.tensor_scalar(triangle[:], c.row[0:P, 0:P], c.col[0:P, :], None, ALU.is_gt)
    v.tensor_reduce(count[:], chosen, AX_X, ALU.add).then_inc(count_ready, 1)
    link(v.tensor_copy(run_a[:], chosen))
    a, b, step = run_a, run_b, 1
    while step < J:
        link(v.tensor_copy(b[:, :, 0:step], a[:, :, 0:step]))
        link(v.tensor_tensor(b[:, :, step:J], a[:, :, step:J], a[:, :, 0:J - step], ALU.add))
        a, b, step = b, a, 2 * step
    link(v.tensor_tensor(a[:], a[:], chosen, ALU.subtract))
    v.wait_ge(counted, 1)
    link(v.tensor_scalar(size[:], ps_cnt[:, e:2 * e], 127.0 - 63.5, 1.0 / 128, ALU.add, ALU.mult))
    link(v.tensor_scalar(size[:], size[:], ROUND, -ROUND, ALU.add, ALU.add))
    link(v.memset(start[:], 0.0))
    for i in range(1, e):
        link(v.tensor_tensor(start[:, i:i + 1], start[:, i - 1:i], size[:, i - 1:i], ALU.add))
    link(v.tensor_tensor(later[:], spread(start[0:1, 1:e], 1, [1, tiles, e - 1]),
                         spread(c.row[0:1, 0:tiles], 2, [1, tiles, e - 1]), ALU.is_le))
    link(v.tensor_reduce(passed[:], later[:], AX_X, ALU.add))
    link(v.tensor_copy(expert_of[:], passed[:]))
    link(v.tensor_scalar(start[:], start[:], 128.0, None, ALU.mult))
    link(v.tensor_tensor(before[:], start[0:P, :], ps_cnt[0:P, 0:e], ALU.add))
    link(v.tensor_tensor(a[:], a[:], spread(before[:], 2, [P, e, J]), ALU.add))
    link(v.tensor_tensor(a[:], a[:], chosen, ALU.mult))
    link(v.tensor_reduce(slot[:, 1, :], a.rearrange("p e j -> p j e"), AX_X, ALU.max))
    link(v.tensor_scalar(b[:], chosen, -1e6, 1e6, ALU.mult, ALU.add))
    link(v.tensor_tensor(b[:], b[:], a[:], ALU.add))
    link(v.tensor_reduce(slot[:, 0, :], b.rearrange("p e j -> p j e"), AX_X, ALU.min))
    ins = v.tensor_copy(slot_i[:], slot[:])
    link(ins)
    for i in range(2):
        link(v.tensor_tensor(b[:], a[:], spread(slot[:, i, :], 1, [P, e, J]), ALU.is_equal))
        link(v.tensor_tensor(b[:], b[:], c.gates[:, 0:e, :], ALU.mult))
        link(v.tensor_tensor(b[:], b[:], chosen, ALU.mult))
        link(v.tensor_reduce(gate[:, i, :], b.rearrange("p e j -> p j e"), AX_X, ALU.add))


def block_experts(nc, c, io, pre, experts, edge_table):
    hc = 4
    tiles = (2 * N + experts * 127) // 128
    up_w = K * hc * 128
    groups = 5
    assert tiles % XS == 0
    with ExitStack() as ctx:
        m = Memory(nc, ctx, pre + "_")
        count = m.sb("count", [P, experts])
        triangle = m.sb("triangle", [P, P])
        before = m.sb("before", [P, experts])
        size = m.sb("size", [128, experts])
        start = m.sb("start", [128, experts])
        run_a = m.sb("run_a", [P, experts, J])
        run_b = m.sb("run_b", [P, experts, J])
        slot = m.sb("slot", [P, 2, J])
        gate = m.sb("gate", [P, 2, J])
        slot_i = m.sb("slot_i", [P, 2, J], I32)
        later = m.sb("later", [1, tiles, experts - 1])
        passed = m.sb("passed", [1, tiles])
        expert_of = m.sb("expert_of", [1, tiles], I32)
        w1 = m.sb("w1_all", [128, experts, up_w + hc])
        w2 = m.sb("w2_all", [128, experts, hc, D])
        b1_rows = m.sb("b1_rows", [experts * hc, 128])
        b2 = m.sb("b2_all", [128, experts, D])
        w1_now = m.sb("w1_now", [128, 2, up_w + hc])
        xs = m.sb("xs", [128, XS, D])
        xs_t = m.sb("xs_t", [128, 2, K, 128])
        hidden = m.sb("hidden_s", [128, 2, hc, 128])
        y = m.sb("y", [128, 2, D])
        y_back = m.sb("y_back", [P, J, D])
        ps_x = [m.ps(f"ps_x{s}", [128, 512]) for s in range(2)]
        ps_h = [m.ps(f"ps_h{s}", [128, 512]) for s in range(2)]
        ps_y = [m.ps(f"ps_y{s}", [128, 512]) for s in range(2)]
        ps_cnt = m.ps("ps_cnt", [128, 512])
        if edge_table is not None:
            chunks = tiles - 2
            qe = E1 // R1 // chunks
            attr = m.sb("attr", [R1, 2, qe, FE])
            attr_w = m.sb("attr_w", [R1, FE])
            attr_out = m.sb("attr_out", [R1, E1 // R1])
            attr_in = [m.sem(f"attr_in{i}") for i in range(2)]
            attr_done, attr_w_in, attr_mul, attr_stored = (m.sem(n) for n in ("attr_done", "attr_w_in", "attr_mul", "attr_stored"))
            attrs = io["edge_attr_64"].rearrange("(r b q) f -> b r (q f)", r=R1, q=qe)
        w_in, b_in, b1_turned, b1_ready = (m.sem(n) for n in ("w_in", "b_in", "b1_turned", "b1_ready"))
        count_ready, counted, slots_ready, rows_out = (m.sem(n) for n in ("count_ready", "counted", "slots_ready", "rows_out"))
        xs_in = [m.sem(f"xs_in{i}") for i in range(XS)]
        xs_turned, xs_t_ready, w1_ready, up_done, hidden_ready, down_done, y_ready = (
            m.sem(n) for n in ("xs_turned", "xs_t_ready", "w1_ready", "up_done", "hidden_ready", "down_done", "y_ready"))
        y_out = [m.sem(f"y_out{i}") for i in range(2)]
        chain = m.sem("chain")
        gathered = [m.sem(f"gathered{i}") for i in range(groups)]
        slot_table, y_table = c.slot_table[0:tiles * 128, :], c.y_table[0:tiles * 128, :]
        rows_of = slot_table.rearrange("(t p) d -> t p d", p=128)
        y_of = y_table.rearrange("(t p) d -> t p d", p=128)
        one = lambda t: bass.ds(t, 1) if not isinstance(t, int) else slice(t, t + 1)
        with nc.Block() as block:

            @block.sync
            def _(sp):
                sp.dma_start(b1_rows[:], io[pre + "_b1"].rearrange("e (k p) -> (e k) p", p=128)).then_inc(b_in, 16)
                for e in range(experts):
                    sp.dma_start(w1[:, e, 0:up_w].rearrange("p (k h) -> p k h", k=K), io[pre + "_W1"][e].rearrange("(k p) h -> p k h", p=128)).then_inc(w_in, 16)
                    sp.dma_start(w2[:, e, :, :], io[pre + "_W2"][e].rearrange("(k p) h -> p k h", p=128)).then_inc(w_in, 16)
                sp.dma_start(b2[:], io[pre + "_b2"].unsqueeze(0).broadcast_to([128, experts, D])).then_inc(w_in, 16)
                if edge_table is not None:
                    sp.dma_start(attr_w[:], io["L1_gnn_A"][:, 2 * D:2 * D + FE].broadcast_to([R1, FE])).then_inc(attr_w_in, 16)
                    for s in range(2):
                        sp.dma_start(attr[:, s, :, :].rearrange("r q f -> r (q f)"), attrs[s]).then_inc(attr_in[s], 16)
                sp.wait_ge(rows_out, 16 * 2 * J)
                for s in range(XS):
                    sp.dma_start(xs[:, s, :], rows_of[s]).then_inc(xs_in[s], 16)
                with sp.Fori(0, tiles // XS - 1) as b:
                    for s in range(XS):
                        sp.wait_ge(xs_turned, b * XS + (s + 1))
                        sp.dma_start(xs[:, s, :], rows_of[bass.ds(b * XS + (s + XS), 1)].rearrange("t p d -> p (t d)")).then_inc(xs_in[s], 16)
                        if edge_table is not None:
                            sp.wait_ge(attr_done, b * XS + (s + 1))
                            sp.dma_start(attr[:, s % 2, :, :].rearrange("r q f -> r (q f)"),
                                         attrs[bass.ds(b * XS + (s + 2), 1)].rearrange("b r f -> r (b f)")).then_inc(attr_in[s % 2], 16)
                if edge_table is not None:
                    sp.wait_ge(attr_done, chunks)
                    sp.dma_start(edge_table.rearrange("(r q) -> r q", r=R1), attr_out[:]).then_inc(attr_stored, 16)
                    sp.wait_ge(attr_stored, 16)

            @block.gpsimd
            def _(pool):
                pool.wait_ge(slots_ready, 1)
                for i in range(2):
                    for j in range(J):
                        pool.indirect_dma_start(slot_table, bass.IndirectOffsetOnAxis(ap=slot_i[:, i, j:j + 1], axis=0),
                                                c.xl[:, j, :], None).then_inc(rows_out, 16)

                def store(t, s):
                    pool.wait_ge(y_ready, t + 3)
                    pool.dma_start(y_of[one(t)].rearrange("t p d -> p (t d)"), y[:, s, :]).then_inc(y_out[s], 16)

                with pool.Fori(0, tiles // 2) as b:
                    for s in range(2):
                        store(b * 2 + s, s)
                for s in range(2):
                    pool.wait_ge(y_out[s], 16 * (tiles // 2))
                for j in range(J):
                    for i, to in enumerate((c.xl, y_back)):
                        pool.indirect_dma_start(to[:, j, :], None, y_table,
                                                bass.IndirectOffsetOnAxis(ap=slot_i[:, i, j:j + 1], axis=0)).then_inc(gathered[j // (J // groups)], 16)

            @block.tensor
            def _(pe):
                pe.wait_ge(b_in, 16)
                pe.transpose(ps_x[0][:, 0:experts * hc], b1_rows[:], c.ident[0:experts * hc, 0:experts * hc]).then_inc(b1_turned, 1)
                pe.wait_ge(count_ready, 1)
                pe.matmul(ps_cnt[0:P, 0:experts], triangle[:], count[:], start=True, stop=True)
                pe.matmul(ps_cnt[:, experts:2 * experts], c.ones[0:P, :], count[:], start=True, stop=True).then_inc(counted, 1)
                pe.wait_ge(b1_ready, 1)

                def turn(t, s, seen):
                    pe.wait_ge(xs_in[s], seen)
                    for k in range(K):
                        ins = pe.transpose(ps_x[s % 2][:, k * 128:(k + 1) * 128], xs[:, s, k * 128:(k + 1) * 128], c.ident[:])
                    ins.then_inc(xs_turned, 1)

                def up(t, s):
                    pe.wait_ge(w1_ready, t + 1)
                    pe.wait_ge(xs_t_ready, t + 1)
                    for h in range(hc):
                        for k in range(K):
                            ins = pe.matmul(ps_h[s][:, h * 128:(h + 1) * 128],
                                            w1_now[:, s, k * hc * 128 + h * 128:k * hc * 128 + (h + 1) * 128],
                                            xs_t[:, s, k, :], start=(k == 0), stop=(k == K - 1))
                    ins.then_inc(up_done, 1)

                def down(t, s):
                    e = pe.value_load(expert_of[0:1, one(t)], min_val=0, max_val=experts - 1)
                    pe.wait_ge(hidden_ready, t + 1)
                    pe.wait_ge(y_ready, t + 1)
                    for h in range(hc):
                        ins = pe.matmul(ps_y[s][:, 0:D], hidden[:, s, h, :], w2[:, bass.ds(e, 1), h, :].squeeze(1),
                                        start=(h == 0), stop=(h == hc - 1))
                    ins.then_inc(down_done, 1)

                turn(0, 0, 16)
                pe.wait_ge(w_in, 16 * (2 * experts + 1))
                up(0, 0)
                turn(1, 1, 16)
                up(1, 1)

                def step(t, s, seen):
                    turn(t + 2, (s + 2) % XS, seen)
                    down(t, s % 2)
                    up(t + 2, s % 2)

                with pe.Fori(0, tiles // XS - 1) as b:
                    for s in range(XS):
                        step(b * XS + s, s, b * 16 + 16 * ((s + 2) // XS + 1))
                for s in range(2):
                    step(tiles - XS + s, s, 16 * (tiles // XS))
                for s in range(2):
                    down(tiles - 2 + s, s)

            @block.scalar
            def _(act):
                with act.Fori(0, tiles // 2) as b:
                    for s in range(2):
                        t = b * 2 + s
                        act.wait_ge(up_done, t + 1)
                        act.wait_ge(down_done, t + 1)
                        for h in range(hc):
                            ins = act.activation(hidden[:, s, h, :], ps_h[s][:, h * 128:(h + 1) * 128], ACT.Gelu,
                                                 bias=w1_now[:, s, up_w + h:up_w + h + 1])
                        ins.then_inc(hidden_ready, 1)

            @block.vector
            def _(v):
                link = Link(v, chain)
                v.sem_inc(y_ready, 2)
                v.sem_inc(down_done, 2)
                v.wait_ge(b1_turned, 1)
                v.tensor_copy(w1[:, :, up_w:], ps_x[0][:, 0:experts * hc].rearrange("p (e k) -> p e k", k=hc)).then_inc(b1_ready, 1)
                route(v, link, c, experts, tiles,
                      (count, triangle, before, size, start, run_a, run_b, slot, gate, slot_i, later, passed, expert_of),
                      count_ready, counted, ps_cnt)
                v.sem_inc(slots_ready, 1)
                if edge_table is not None:
                    v.wait_ge(attr_w_in, 16)

                def weights(t, s):
                    e = v.value_load(expert_of[0:1, one(t)], min_val=0, max_val=experts - 1)
                    v.tensor_copy(w1_now[:, s, :], w1[:, bass.ds(e, 1), :].squeeze(1)).then_inc(w1_ready, 1)

                def turned(t, s):
                    v.wait_ge(xs_turned, t + 1)
                    v.tensor_copy(xs_t[:, s, :, :].rearrange("p k n -> p (k n)"), ps_x[s][:, 0:K * 128]).then_inc(xs_t_ready, 1)

                def finish(t, s, seen):
                    e = v.value_load(expert_of[0:1, one(t)], min_val=0, max_val=experts - 1)
                    v.wait_ge(down_done, t + 3)
                    if not isinstance(seen, int) or seen:
                        v.wait_ge(y_out[s], seen)
                    v.tensor_tensor(y[:, s, :], ps_y[s][:, 0:D], b2[:, bass.ds(e, 1), :].squeeze(1), ALU.add).then_inc(y_ready, 1)

                v.wait_ge(w_in, 16 * (2 * experts + 1))
                v.wait_ge(b1_ready, 1)
                for s in range(2):
                    weights(s, s)
                    turned(s, s)

                def step(t, s, stored):
                    v.wait_ge(hidden_ready, t + 1)
                    weights(t + 2, s)
                    turned(t + 2, s)
                    finish(t, s, stored)
                    if edge_table is not None:
                        v.wait_ge(attr_in[s], stored + 16)
                        v.tensor_tensor(attr[:, s, :, :], attr[:, s, :, :], spread(attr_w[:], 1, [R1, qe, FE]),
                                        ALU.mult).then_inc(attr_mul, 1)
                        v.wait_ge(attr_mul, t + 1)
                        v.tensor_reduce(attr_out.rearrange("r (b q) -> r b q", q=qe)[:, one(t), :].squeeze(1),
                                        attr[:, s, :, :], AX_X, ALU.add).then_inc(attr_done, 1)

                for s in range(2):
                    step(s, s, 0)
                with v.Fori(1, tiles // 2 - 1) as b:
                    for s in range(2):
                        step(b * 2 + s, s, b * 16)
                for s in range(2):
                    finish(tiles - 2 + s, s, 16 * (tiles // 2 - 1))
                for g in range(groups):
                    v.wait_ge(gathered[g], 16 * 2 * J // groups)
                    for i, back in enumerate((c.xl, y_back)):
                        for j in range(g * (J // groups), (g + 1) * (J // groups)):
                            ins = v.scalar_tensor_tensor(c.x[:, j, :], back[:, j, :], gate[:, i, j:j + 1], c.x[:, j, :], ALU.mult, ALU.add)
                        link(ins)


class WindowTables:

    def __init__(self, m):
        self.src_i = m.sb("src_i", [Q1, I4 * 128], I32)
        self.dst = m.sb("dst", [Q1, I4 * 128])
        self.edge = m.sb("edge", [Q1, I4 * 128])
        self.w_line = m.sb("w_line", [1, I4 * 128], I32)

    def scratch(self, m):
        self.first = m.sb("first", [128, J])
        self.item_w = m.sb("item_w", [128, I4])
        self.item_t = m.sb("item_t", [128, I4])
        self.item_n = m.sb("item_n", [128, I4])
        self.item_t_i = m.sb("item_t_i", [128, I4], I32)
        self.w_rows = m.sb("w_rows", [I4, 128], I32)
        self.less = m.sb("less", [128, J])
        self.five = m.sb("five", [P, J])
        self.count = m.sb("count", [P, 1])
        self.count_row = m.sb("count_row", [P, 128])
        self.src_rows_i = m.sb("src_rows_i", [128, I4, Q1], I32)
        self.dst_rows_i = m.sb("dst_rows_i", [128, I4, Q1], I32)
        self.src_rows = m.sb("src_rows", [128, I4, Q1])
        self.dst_rows = m.sb("dst_rows", [128, I4, Q1])
        self.dst_rows_b = m.sb("dst_rows_b", [128, I4, Q1], BF16)
        self.edge_rows = m.sb("edge_rows", [128, I4, Q1])
        self.ps_a = m.ps("ps_a", [128, 512])
        self.ps_b = m.ps("ps_b", [128, 512])
        self.count_ready, self.count_summed, self.items_ready, self.items_turned = (
            m.sem(n) for n in ("count_ready", "count_summed", "items_ready", "items_turned"))
        self.w_ready, self.w_out, self.w_line_in, self.rows_in = (m.sem(n) for n in ("w_rows_ready", "w_out", "w_line_in", "rows_in"))
        self.line_ready, self.line_out, self.rows_ready, self.rows_turned, self.rows_free = (
            m.sem(n) for n in ("line_ready", "line_out", "rows_ready", "rows_turned", "rows_free"))

    def sync(self, sp, c):
        sp.wait_ge(self.w_ready, 1)
        sp.dma_start(c.w_dram.rearrange("(k p) -> k p", p=128), self.w_rows[:]).then_inc(self.w_out, 16)
        sp.wait_ge(self.w_out, 16)
        sp.dma_start(self.w_line[:], c.w_dram.unsqueeze(0)).then_inc(self.w_line_in, 16)
        sp.wait_ge(self.line_ready, 1)
        sp.dma_start(c.dst_line_dram.rearrange("(k p q) -> p k q", p=128, q=Q1), self.dst_rows_b[:]).then_inc(self.line_out, 16)

    def sync_end(self, sp):
        sp.wait_ge(self.w_line_in, 16)
        sp.wait_ge(self.line_out, 16)

    def gpsimd(self, pool, c, io):
        table = lambda ap: ap.rearrange("(t q) -> t q", q=Q1)
        pool.wait_ge(self.items_ready, 1)
        for k in range(I4):
            at = bass.IndirectOffsetOnAxis(ap=self.item_t_i[:, k:k + 1], axis=0)
            pool.indirect_dma_start(self.src_rows_i[:, k, :], None, table(io["src"]), at).then_inc(self.rows_in, 16)
            pool.indirect_dma_start(self.dst_rows_i[:, k, :], None, table(io["dst"]), at).then_inc(self.rows_in, 16)
            pool.indirect_dma_start(self.edge_rows[:, k, :], None, table(c.edge_table), at).then_inc(self.rows_in, 16)

    def tensor_items(self, pe, c):
        pe.wait_ge(self.count_ready, 1)
        pe.matmul(self.ps_a[:, 0:J], self.count_row[:], self.five[:], start=True, stop=True).then_inc(self.count_summed, 1)
        pe.wait_ge(self.items_ready, 1)
        pe.transpose(self.ps_b[0:I4, 0:128], self.item_w[:], c.ident[:]).then_inc(self.items_turned, 1)

    def tensor_rows(self, pe, c):
        pe.wait_ge(self.w_ready, 1)
        pe.wait_ge(self.rows_ready, 1)
        for i, rows in enumerate((self.src_rows, self.dst_rows, self.edge_rows)):
            if i >= 2:
                pe.wait_ge(self.rows_free, i - 1)
            for k in range(I4):
                ins = pe.transpose((self.ps_a, self.ps_b)[i % 2][0:Q1, k * 128:(k + 1) * 128], rows[:, k, :], c.ident[:])
            ins.then_inc(self.rows_turned, 1)

    def vector_items(self, v, link, c):
        link(v.tensor_scalar(self.five[:], c.row[0:P, 0:J], float(P // J), None, ALU.mult))
        link(v.tensor_scalar(self.five[:], self.five[:], c.col[0:P, :], None, ALU.is_gt))
        link(v.tensor_reduce(self.count[:], c.deg[:], AX_X, ALU.add))
        v.tensor_copy(self.count_row[:], self.count[:, 0:1].broadcast_to([P, 128])).then_inc(self.count_ready, 1)
        v.wait_ge(self.count_summed, 1)
        link(v.tensor_scalar(self.first[:], self.ps_a[:, 0:J], -float(Q1 // 2), 1.0 / Q1, ALU.add, ALU.mult))
        link(v.tensor_scalar(self.first[:], self.first[:], ROUND, -ROUND, ALU.add, ALU.add))
        link(v.tensor_scalar(self.first[:], self.first[:], float(T1 - 1), None, ALU.min))
        link(v.tensor_tensor(self.first[:], self.first[:], c.row[:, 0:J], ALU.add))
        for k in range(I4):
            link(v.tensor_scalar(self.item_n[:, k:k + 1], c.col[:], 128.0 * k, None, ALU.add))
            link(v.tensor_scalar(self.less[:, 0:J - 1], self.first[:, 1:J], self.item_n[:, k:k + 1], None, ALU.is_le))
            link(v.tensor_reduce(self.item_w[:, k:k + 1], self.less[:, 0:J - 1], AX_X, ALU.add))
        link(v.tensor_tensor(self.item_t[:], self.item_n[:], self.item_w[:], ALU.subtract))
        link(v.tensor_scalar(self.item_t[:], self.item_t[:], float(T1 - 1), None, ALU.min))
        v.tensor_copy(self.item_t_i[:], self.item_t[:]).then_inc(self.items_ready, 1)
        v.wait_ge(self.items_turned, 1)
        v.tensor_copy(self.w_rows[:], self.ps_b[0:I4, 0:128]).then_inc(self.w_ready, 1)
        link(v.tensor_scalar(self.item_w[:], self.item_w[:], float(P), None, ALU.mult))
    def vector_rows(self, v, link, c):
        v.wait_ge(self.rows_in, 16 * 3 * I4)
        link(v.tensor_copy(self.src_rows[:], self.src_rows_i[:]))
        link(v.tensor_copy(self.dst_rows[:], self.dst_rows_i[:]))
        for k in range(I4):
            link(v.tensor_scalar(self.dst_rows[:, k, :], self.dst_rows[:, k, :], self.item_w[:, k:k + 1], None, ALU.subtract))
        v.sem_inc(self.rows_ready, 1)
        link(v.tensor_copy(self.dst_rows_b[:], self.dst_rows[:]))
        v.sem_inc(self.line_ready, 1)
        link(v.tensor_reduce(c.most_of[:, 1:2], self.edge_rows.rearrange("p k q -> p (k q)"), AX_X, ALU.max))
        for i, to in enumerate((self.src_i, self.dst, self.edge)):
            v.wait_ge(self.rows_turned, i + 1)
            ins = v.tensor_copy(to[:], (self.ps_a, self.ps_b)[i % 2][0:Q1, :])
            link(ins)
            v.sem_inc(self.rows_free, 1)
        link(v.memset(self.dst[:, ITEMS:IP], -1.0))


def block_z(nc, c, io):
    with ExitStack() as ctx:
        m = Memory(nc, ctx, "z_")
        st = m.sb("st", [P, J, BN])
        small = m.sb("small", [P, 5, J])
        std = m.sb("std", [P, J])
        w = m.sb("w", [128, K, D])
        wt = m.sb("wt", [128, K, ZF])
        a_rows = m.sb("a_rows", [2 * K, 128])
        a_cols = m.sb("a_cols", [128, 2, K])
        z = m.sb("z", [P, J, ZF])
        ad_nodes = m.sb("ad_nodes", [P, J])
        ad_ready, ad_out = m.sem("ad_ready"), m.sem("ad_out")
        ps_turn = [m.ps(f"ps_turn{i}", [128, 512]) for i in range(2)]
        ps_w = m.ps("ps_w", [128, 512])
        ps_wa = m.ps("ps_wa", [128, 2 * K + 4])
        ps_z = [m.ps(f"ps_z{i}", [P, 512]) for i in range(2)]
        w_in, var_ready, std_ready, xl_ready = (m.sem(n) for n in ("w_in", "var_ready", "std_ready", "xl_ready"))
        turned, turn_free, a_turned, a_ready = (m.sem(n) for n in ("turned", "turn_free", "a_turned", "a_ready"))
        w_turned, w_ready, wa_summed, wt_ready = (m.sem(n) for n in ("w_turned", "w_ready", "wa_summed", "wt_ready"))
        z_summed, z_copied, ones_set = (m.sem(n) for n in ("z_summed", "z_copied", "ones_set"))
        x_out, z_out, chain = (m.sem(n) for n in ("x_out", "z_out", "chain"))
        tab = c.tables
        tab.scratch(m)
        with nc.Block() as block:

            @block.sync
            def _(sp):
                sp.dma_start(w[:], io["L1_gnn_W"].rearrange("(k p) c -> p k c", p=128)).then_inc(w_in, 16)
                sp.dma_start(a_rows[:], io["L1_gnn_A"][0, 0:2 * D].rearrange("(k p) -> k p", p=128)).then_inc(w_in, 16)
                sp.dma_start(c.x_table.rearrange("(p j) d -> p j d", j=J), c.x[:]).then_inc(x_out, 16)
                tab.sync(sp, c)
                for j in range(0, J, 5):
                    sp.wait_ge(ones_set, j // 5 + 1)
                    sp.dma_start(c.z_table.rearrange("(p j) f -> p j f", j=J)[:, j:j + 5, :], z[:, j:j + 5, :]).then_inc(z_out, 16)
                sp.wait_ge(ad_ready, 1)
                sp.dma_start(c.ad_dram.rearrange("(p j) -> p j", j=J), ad_nodes[:]).then_inc(ad_out, 16)
                sp.wait_ge(ad_out, 16)
                sp.wait_ge(z_out, 16 * 5)
                sp.wait_ge(x_out, 16)
                tab.sync_end(sp)

            @block.gpsimd
            def _(pool):
                tab.gpsimd(pool, c, io)

            @block.tensor
            def _(pe):
                tab.tensor_items(pe, c)
                pe.wait_ge(w_in, 32)
                pe.transpose(ps_wa[:, 2 * K:2 * K + 4], a_rows[:], c.ident[0:4, 0:4]).then_inc(a_turned, 1)
                for k in range(K):
                    for f in range(K):
                        ins = pe.transpose(ps_w[:, (k * K + f) * 128:(k * K + f + 1) * 128], w[:, f, k * 128:(k + 1) * 128], c.ident[:])
                ins.then_inc(w_turned, 1)
                pe.wait_ge(a_ready, 1)
                for k in range(K):
                    for f in range(K):
                        ins = pe.matmul(ps_wa[:, 2 * k:2 * k + 2], w[:, f, k * 128:(k + 1) * 128], a_cols[:, :, f],
                                        start=(f == 0), stop=(f == K - 1))
                ins.then_inc(wa_summed, 1)
                transpose_nodes(pe, c, ps_turn, xl_ready, turn_free, turned)
                tab.tensor_rows(pe, c)
                pe.wait_ge(turn_free, TURNS)
                pe.wait_ge(wt_ready, 2)
                for j in range(J):
                    if j >= 2:
                        pe.wait_ge(z_copied, j - 1)
                    for k in range(K):
                        ins = pe.matmul(ps_z[j % 2][:, 0:ZF], c.xt[:, k, j * P:(j + 1) * P], wt[:, k, :],
                                        start=(k == 0), stop=(k == K - 1))
                    ins.then_inc(z_summed, 1)

            @block.scalar
            def _(act):
                act.wait_ge(w_turned, 1)
                act.copy(wt[:, :, 0:D], ps_w.rearrange("p (k f) -> p k f", k=K)).then_inc(wt_ready, 1)
                act.wait_ge(var_ready, 1)
                act.activation(std[:], small[:, 2, :], ACT.Sqrt).then_inc(std_ready, 1)
                copy_turned(act, c, ps_turn, turn_free, turned)
                for j in range(J):
                    act.wait_ge(z_summed, j + 1)
                    act.copy(z[:, j, :], ps_z[j % 2][:, 0:ZF]).then_inc(z_copied, 1)

            @block.vector
            def _(v):
                link = Link(v, chain)
                link(v.memset(c.most_of[:], -3e38))
                tab.vector_items(v, link, c)
                v.wait_ge(a_turned, 1)
                v.tensor_copy(a_cols.rearrange("p s k -> p (s k)"), ps_wa[:, 2 * K:2 * K + 4]).then_inc(a_ready, 1)
                link(v.memset(wt[:, :, D:D + 1], 0.0))
                layernorm_stats(v, link, c.x, st, small, std[:], var_ready, 1, std_ready)
                layernorm_apply(v, link, c.xl, c.x, small, xl_ready)
                v.wait_ge(wa_summed, 1)
                v.tensor_copy(wt[:, :, D + 1:D + 3], ps_wa[:, 0:2 * K].rearrange("p (k s) -> p k s", k=K)).then_inc(wt_ready, 1)
                tab.vector_rows(v, link, c)
                for j in range(0, J, 5):
                    v.wait_ge(z_copied, j + 5)
                    v.memset(z[:, j:j + 5, D:D + 1], 1.0).then_inc(ones_set, 1)
                link(v.tensor_copy(ad_nodes[:], z[:, :, D + 2]))
                v.sem_inc(ad_ready, 1)
                link(v.tensor_reduce(c.most_of[0:P, 0:1], z[:, :, D + 1], AX_X, ALU.max))


def window(pack, w0, u):
    w = w0 + ((pack >> (5 + 3 * (u - 1))) & 7) if u else w0
    return w.with_bounds(min_val=0, max_val=J - 1)


def block_windows(nc, c, io):
    with ExitStack() as ctx:
        m = Memory(nc, ctx, "windows_")
        tab = c.tables
        acc = m.sb("acc", [P, J, D + 1])
        ad = m.sb("ad", [Q1, IP])
        cap = m.sb("cap", [Q1, IP])
        most = m.sb("most", [128, 4])
        dst_line = m.sb("dst_line", [P, LS, GL * Q1], BF16)
        dst_hot_t = m.sb("dst_hot_t", [P, 2, GL * Q1], BF16)
        ad_rest = m.sb("ad_rest", [P, I4 * 128])
        ad_rows = m.sb("ad_rows", [J, P])
        ad_b = m.sb("ad_b", [P, I4 * 128, 3], BF16)
        ad_now = m.sb("ad_now", [P, 2, GL, 3], BF16)
        w_rows = m.sb("w_rows", [J, I4 * 128], I32)
        w_hot = m.sb("w_hot", [J, I4 * 128])
        w_of = m.sb("w_of", [1, GW, UW])
        w_pack = m.sb("w_pack", [1, GW])
        w_pack_i = m.sb("w_pack_i", [1, GW], I32)
        spare = m.sb("spare", [128, 3], I32)
        stage = m.sb("stage", [Q1, SW, UW], I32)
        ring = m.sb("ring", [Q1, SW, UW, ZF])
        logit = m.sb("logit", [Q1, 2, UW])
        lrelu = m.sb("lrelu", [Q1, 2, UW])
        below = m.sb("below", [Q1, 2, UW])
        ex = m.sb("ex", [Q1, 2, UW])
        prob = m.sb("prob", [Q1, 2, UW, P])
        rden = m.sb("rden", [P, J])
        looked = [m.ps(f"looked{i}", [Q1, 512]) for i in range(2)]
        part = [m.ps(f"part{i}", [P, 512]) for i in range(PART)]
        most_out, hot_t_ready, looked_up, looked_free, x_in, ad_in, w_hot_ready, ad_spread = (
            m.sem(n) for n in ("most_out", "hot_t_ready", "looked_up", "looked_free", "x_in", "ad_in", "w_hot_ready", "ad_spread"))
        staged, below_ready, ex_ready, prob_ready, part_ready, part_free, small_chain, spare_set, chain = (
            m.sem(n) for n in ("staged", "below_ready", "ex_ready", "prob_ready", "part_ready", "part_free",
                               "small_chain", "spare_set", "chain"))
        line_in = [m.sem(f"line_in{i}") for i in range(LS)]
        gathered = [m.sem(f"gathered{i}") for i in range(SW)]
        chunks = IP // GL
        some = lambda i, n: bass.ds(i, n) if not isinstance(i, int) else slice(i, i + n)
        with nc.Block() as block:

            @block.sync
            def _(sp):
                lines = c.dst_line_dram[0:IP * Q1].rearrange("(b e) -> b e", e=GL * Q1)
                def load(i, s):
                    sp.dma_start(dst_line[:, s, :], lines[some(i, 1), :].broadcast_to([P, GL * Q1])).then_inc(line_in[s], 16)

                sp.dma_start(ad_rows[:], c.ad_dram.rearrange("(w d) -> w d", d=P)).then_inc(ad_in, 16)
                sp.dma_start(w_rows[:], c.w_dram.unsqueeze(0).broadcast_to([J, I4 * 128])).then_inc(ad_in, 16)
                for s in range(LS):
                    load(s, s)
                with sp.Fori(1, chunks // LS) as b:
                    for s in range(LS):
                        sp.wait_ge(hot_t_ready, b * LS + (s + 1 - LS))
                        load(b * LS + s, s)
                sp.dma_start(c.x[:], c.x_table.rearrange("(w d) f -> d w f", d=P)).then_inc(x_in, 16)

            @block.gpsimd
            def _(pool):
                pool.memset(spare[:], 0).then_inc(spare_set, 1)

                def gather(g, s):
                    pool.wait_ge(spare_set, g + 1)
                    pool.tensor_tensor(spare[:, 1:2], spare[:, 0:1], spare[:, 0:1], ALU.add)
                    pool.wait_ge(staged, g + 1)
                    pool.tensor_tensor(spare[:, 2:3], spare[:, 0:1], spare[:, 0:1], ALU.add).then_inc(spare_set, 1)
                    for u in range(UW):
                        pool.indirect_dma_start(ring[:, s, u, :], None, c.z_table,
                                                bass.IndirectOffsetOnAxis(ap=stage[:, s, u:u + 1], axis=0)).then_inc(gathered[s], 16)

                gather(0, 0)
                pool.partition_all_reduce(most[:, 0:2], c.most_of[:, 0:2], 128, bass.bass_isa.ReduceOp.max).then_inc(most_out, 1)
                with pool.Fori(0, GW // SW) as b:
                    for s in range(SW):
                        gather(b * SW + (s + 1), (s + 1) % SW)

            @block.tensor
            def _(pe):
                pe.wait_ge(w_hot_ready, 1)
                pe.matmul(part[0][:], ad_rows[:], w_hot[:], start=True, stop=True).then_inc(ad_spread, 1)
                with pe.Fori(0, chunks // 2) as b:
                    for s in range(2):
                        pe.wait_ge(hot_t_ready, b * 2 + (s + 1))
                        pe.wait_ge(looked_free, b * 2 + (s + 1))
                        for g in range(GL):
                            ins = pe.matmul(looked[s][:, g * 3:(g + 1) * 3], dst_hot_t[:, s, g * Q1:(g + 1) * Q1],
                                            ad_now[:, s, g, :], start=True, stop=True)
                        ins.then_inc(looked_up, 1)

                def group(g, s, half):
                    for u in range(UW):
                        bank = (s * UW + u) % PART
                        pe.wait_ge(prob_ready, g * UW + (u + 1))
                        pe.wait_ge(part_free, g * UW + (u + 1))
                        ins = pe.matmul(part[bank][:, 0:D + 1], prob[:, half, u, :], ring[:, s, u, 0:D + 1], start=True, stop=True)
                        ins.then_inc(part_ready, 1)

                with pe.Fori(0, GW // SW) as b:
                    for s in range(SW):
                        group(b * SW + s, s, s % 2)
                group(GW - 1, (GW - 1) % SW, (GW - 1) % 2)

            @block.scalar
            def _(act):
                def exps(g, half):
                    act.wait_ge(below_ready, g + 1)
                    act.activation(ex[:, half, :], below[:, half, :], ACT.Exp).then_inc(ex_ready, 1)

                with act.Fori(0, (GW - 1) // 2) as b:
                    for s in range(2):
                        exps(b * 2 + s, s)
                exps(GW - 1, (GW - 1) % 2)

            @block.vector
            def _(v):
                link = Link(v, chain)
                v.sem_inc(looked_free, 2)
                v.sem_inc(part_free, PART)
                for s in range(SW):
                    v.tensor_copy(stage[:, s, :], tab.src_i[:, s * UW:(s + 1) * UW]).then_inc(staged, 1)
                link(v.memset(acc[:], 0.0))
                v.wait_ge(ad_in, 32)
                link(v.tensor_copy(w_hot[:], w_rows[:]))
                v.tensor_scalar(w_hot[:], w_hot[:], c.col[0:J, 0:1], None, ALU.is_equal).then_inc(w_hot_ready, 1)
                link(v.tensor_copy(w_of.rearrange("o g u -> o (g u)"), tab.w_line[:, 0:GW * UW]))
                link(v.tensor_copy(w_pack[:], w_of[:, :, 0]))
                for u in range(1, UW):
                    link(v.tensor_tensor(w_of[:, :, u], w_of[:, :, u], w_of[:, :, 0], ALU.subtract))
                    link(v.scalar_tensor_tensor(w_pack[:], w_of[:, :, u], float(32 * 8 ** (u - 1)), w_pack[:], ALU.mult, ALU.add))
                link(v.tensor_copy(w_pack_i[:], w_pack[:]))
                v.wait_ge(ad_spread, 1)
                three_parts(v, link, [ad_b[:, :, i] for i in range(3)], ad_rest[:], part[0][:])

                def compare(i, line, s, seen):
                    v.tensor_copy(ad_now[:, s, :, :], ad_b[:, some(i * GL, GL), :])
                    v.wait_ge(line_in[line], seen)
                    v.tensor_scalar(dst_hot_t[:, s, :], dst_line[:, line, :], c.col[0:P, 0:1], None,
                                    ALU.is_equal).then_inc(hot_t_ready, 1)

                def find(i, s):
                    v.wait_ge(looked_up, i + 1)
                    v.tensor_reduce(ad[:, some(i * GL, GL)], looked[s][:, 0:GL * 3].rearrange("q (g i) -> q g i", i=3),
                                    AX_X, ALU.add).then_inc(looked_free, 1)

                compare(0, 0, 0, 16)
                with v.Fori(0, chunks // LS - 1) as b:
                    for s in range(LS):
                        compare(b * LS + (s + 1), (s + 1) % LS, (s + 1) % 2, b * 16 + 16 * (1 + (s + 1) // LS))
                        find(b * LS + s, s % 2)
                for i in range(chunks - LS, chunks):
                    if i + 1 < chunks:
                        compare(i + 1, (i + 1) % LS, (i + 1) % 2, 16 * ((i + 1) // LS + 1))
                    find(i, i % 2)
                v.wait_ge(looked_free, chunks + 2)
                v.wait_ge(most_out, 1)
                link(v.tensor_tensor(most[:, 2:3], most[:, 0:1], most[:, 1:2], ALU.add))
                link(v.tensor_scalar(cap[:], ad[:], most[0:Q1, 2:3], None, ALU.add))
                link(v.scalar_tensor_tensor(cap[:], cap[:], 0.2, cap[:], ALU.mult, ALU.max))
                link(v.tensor_tensor(ad[:], ad[:], tab.edge[:, 0:IP], ALU.add))

                def logits(g, s, half, seen):
                    now = some(g * UW, UW)
                    v.wait_ge(gathered[s], seen)
                    v.tensor_tensor(logit[:, half, :], ring[:, s, :, D + 1], ad[:, now], ALU.add).then_inc(small_chain, 1)
                    v.wait_ge(small_chain, g * 2 + 1)
                    v.scalar_tensor_tensor(lrelu[:, half, :], logit[:, half, :], 0.2, logit[:, half, :], ALU.mult, ALU.max).then_inc(small_chain, 1)
                    v.wait_ge(small_chain, g * 2 + 2)
                    v.tensor_tensor(below[:, half, :], lrelu[:, half, :], cap[:, now], ALU.subtract).then_inc(below_ready, 1)

                def one_hot(g, u, half):
                    v.tensor_scalar(prob[:, half, u, :], c.row[0:Q1, 0:P], tab.dst[:, some(g * UW + u, 1)], ex[:, half, u:u + 1],
                                    ALU.is_equal, ALU.mult).then_inc(prob_ready, 1)

                def windows_of(g):
                    pack = v.value_load(w_pack_i[0:1, some(g, 1)], min_val=0, max_val=2 ** 20 - 1)
                    return pack, pack & 31

                def add(g, s, u, pack, w0):
                    i = g * UW + u
                    w = window(pack, w0, u)
                    v.wait_ge(part_ready, i + 1)
                    v.wait_ge(part_free, i + PART)
                    row = acc[:, bass.ds(w, 1), :].squeeze(1)
                    v.tensor_tensor(row, part[(s * UW + u) % PART][:, 0:D + 1], row, ALU.add).then_inc(part_free, 1)

                logits(0, 0, 0, 16 * UW)
                v.wait_ge(ex_ready, 1)
                for u in range(UW):
                    one_hot(0, u, 0)

                def step(g, k, seen, stage_next):
                    s, half = (k + 1) % SW, (k + 1) % 2
                    pack, w0 = windows_of(g)
                    logits(g + 1, s, half, seen)
                    for u in range(UW):
                        add(g, k, u, pack, w0)
                        if u == 0:
                            v.wait_ge(ex_ready, g + 2)
                        one_hot(g + 1, u, half)
                    if stage_next:
                        v.tensor_copy(stage[:, k, :], tab.src_i[:, some((g + SW) * UW, UW)]).then_inc(staged, 1)

                with v.Fori(0, GW // SW - 1) as b:
                    for k in range(SW):
                        step(b * SW + k, k, b * (16 * UW) + 16 * UW * (1 + (k + 1) // SW), True)
                for k in range(SW):
                    g = GW - 1 - SW + k
                    step(g, k, 16 * UW * (GW // SW + (k + 1) // SW), k == 0)
                pack, w0 = windows_of(GW - 1)
                for u in range(UW):
                    add(GW - 1, (GW - 1) % SW, u, pack, w0)
                v.wait_ge(part_free, GW * UW + PART)
                link(v.tensor_scalar(rden[:], acc[:, :, D], 1e-37, None, ALU.max))
                link(v.reciprocal(rden[:], rden[:]))
                v.wait_ge(x_in, 16)
                for j in range(J):
                    v.scalar_tensor_tensor(c.x[:, j, :], acc[:, j, 0:D], rden[:, j:j + 1],
                                           c.x[:, j, :], ALU.mult, ALU.add).then_inc(link.sem, 1)
                link.loop_end(J)
                v.wait_ge(link.sem, link.n)


def block_router(nc, c, io):
    with ExitStack() as ctx:
        m = Memory(nc, ctx, "router_")
        st = m.sb("st", [P, J, BN])
        small = m.sb("small", [P, 5, J])
        std = m.sb("std", [P, 2, J])
        scale = m.sb("scale", [P, 2, D])
        wr = m.sb("wr", [128, K, NE1])
        br = m.sb("br", [P, NE1])
        score = m.sb("score", [P, J, NE1])
        t = m.sb("t", [P, J, NE1, 4])
        big = m.sb("big", [P, J, NE1, NE1])
        tri = m.sb("tri", [P, NE1 * NE1])
        exp_in = m.sb("exp_in", [P, J, NE1])
        exp_out = m.sb("exp_out", [P, J, NE1])
        ps_turn = [m.ps(f"ps_turn{i}", [128, 512]) for i in range(2)]
        ps_r = m.ps("ps_r", [P, J * NE1])
        w_in, var_ready, std_ready, xl_ready = (m.sem(n) for n in ("w_in", "var_ready", "std_ready", "xl_ready"))
        turned, turn_free, summed, gate_in, gate_out, chain = (
            m.sem(n) for n in ("turned", "turn_free", "summed", "gate_in", "gate_out", "chain"))
        with nc.Block() as block:

            @block.sync
            def _(sp):
                sp.dma_start(wr[:], io["L1_ffn_Wr"].rearrange("(k p) e -> p k e", p=128)).then_inc(w_in, 16)
                sp.dma_start(br[:], io["L1_ffn_br"].unsqueeze(0).broadcast_to([P, NE1])).then_inc(w_in, 16)
                sp.dma_start(scale[:, 0, :], io["L1_ffn_gamma"].unsqueeze(0).broadcast_to([P, D])).then_inc(w_in, 16)
                sp.dma_start(scale[:, 1, :], io["L1_ffn_beta"].unsqueeze(0).broadcast_to([P, D])).then_inc(w_in, 16)

            @block.scalar
            def _(act):
                for i in range(2):
                    act.wait_ge(var_ready, i + 1)
                    act.activation(std[:, i, :], small[:, 2, :], ACT.Sqrt).then_inc(std_ready, 1)
                copy_turned(act, c, ps_turn, turn_free, turned)
                act.wait_ge(gate_in, 1)
                act.activation(exp_out[:], exp_in[:], ACT.Exp).then_inc(gate_out, 1)

            @block.tensor
            def _(pe):
                transpose_nodes(pe, c, ps_turn, xl_ready, turn_free, turned)
                pe.wait_ge(turn_free, TURNS)
                pe.wait_ge(w_in, 64)
                for j in range(J):
                    for k in range(K):
                        ins = pe.matmul(ps_r[:, j * NE1:(j + 1) * NE1], c.xt[:, k, j * P:(j + 1) * P], wr[:, k, :],
                                        start=(k == 0), stop=(k == K - 1))
                ins.then_inc(summed, 1)

            @block.vector
            def _(v):
                link = Link(v, chain)
                layernorm_stats(v, link, c.x, st, small, std[:, 0, :], var_ready, 1, std_ready)
                layernorm_apply(v, link, c.xl, c.x, small)
                layernorm_stats(v, link, c.xl, st, small, std[:, 1, :], var_ready, 2, std_ready)
                layernorm_apply(v, link, c.xl, c.xl, small)
                v.wait_ge(w_in, 64)
                for j0 in range(0, J, 5):
                    now = c.xl[:, j0:j0 + 5, :]
                    link(v.tensor_tensor(now, now, spread(scale[:, 0, :], 1, [P, 5, D]), ALU.mult))
                    v.tensor_tensor(now, now, spread(scale[:, 1, :], 1, [P, 5, D]), ALU.add).then_inc(xl_ready, 5)
                lower_triangle(v, link, c, tri, NE1)
                v.wait_ge(summed, 1)
                link(v.tensor_tensor(score[:], ps_r.rearrange("p (j e) -> p j e", e=NE1), spread(br[:], 1, [P, J, NE1]), ALU.add))
                top2_gates(v, link, score[:], c.gates[:, 0:NE1, :], c.chosen[:, 0:NE1, :], t[:], big[:], tri[:], exp_in[:], exp_out[:],
                           (gate_in, gate_out, 1))


def store_x(nc, c, io):
    with ExitStack() as ctx:
        m = Memory(nc, ctx, "store_x_")
        stored = m.sem("stored")
        with nc.Block() as block:

            @block.sync
            def _(sp):
                sp.dma_start(io["out"].rearrange("(w d) f -> d w f", d=P), c.x[:]).then_inc(stored, 16)
                sp.wait_ge(stored, 16)


class Common:
    pass


def program(nc, io):
    with ExitStack() as ctx:
        m = Memory(nc, ctx)
        c = Common()
        c.x = m.sb("x_nodes", [P, J, D])
        c.row = m.sb("row", [128, 128])
        c.row_b = m.sb("row_b", [128, 128], BF16)
        c.col = m.sb("col", [128, 1])
        c.ident = m.sb("ident", [128, 128])
        c.ones = m.sb("ones", [128, 128])
        c.zeros_b = m.sb("zeros_b", [128, 128], BF16)
        c.hi_line_dram = nc.dram_tensor("hi_line_dram", [E1], BF16, kind="Internal").ap()
        c.hi_line_dram2 = nc.dram_tensor("hi_line_dram2", [E2], BF16, kind="Internal").ap()
        c.dst_line_dram = nc.dram_tensor("dst_line_dram", [I4 * 128 * Q1], BF16, kind="Internal").ap()
        c.w_dram = nc.dram_tensor("w_dram", [I4 * 128], I32, kind="Internal").ap()
        c.edge_table = nc.dram_tensor("edge_table", [E1], F32, kind="Internal").ap()
        c.ad_dram = nc.dram_tensor("ad_dram", [N], F32, kind="Internal").ap()
        c.x_table = nc.dram_tensor("x_table", [N, D], F32, kind="Internal").ap()
        c.z_table = nc.dram_tensor("z_table", [N, ZF], F32, kind="Internal").ap()
        c.deg = m.sb("deg_nodes", [P, J])
        c.h_table = nc.dram_tensor("h_table", [N, HF], F32, kind="Internal").ap()
        c.h = m.sb("h_nodes", [P, J, HF])
        c.a_dst = m.sb("a_dst", [P, J, HEADS])
        c.most_of = m.sb("most_of", [128, HEADS])
        c.most = m.sb("most", [128, HEADS])
        c.gates = m.sb("gates", [P, NE1, J])
        c.chosen = m.sb("chosen", [P, NE1, J])
        most_tiles = (2 * N + NE1 * 127) // 128
        c.slot_table = nc.dram_tensor("slot_table", [most_tiles * 128, D], F32, kind="Internal").ap()
        c.y_table = nc.dram_tensor("y_table", [most_tiles * 128, D], F32, kind="Internal").ap()
        def with_xt(block):
            with ExitStack() as inner:
                c.xt = Memory(nc, inner).sb(block.__name__ + "_xt", [128, K, N])
                block(nc, c, io)

        constants(nc, c)
        with ExitStack() as of_xl:
            c.xl = Memory(nc, of_xl).sb("xl_gcn", [P, J, D])
            block_gcn(nc, c, io)
        with ExitStack() as of_tables:
            c.tables = WindowTables(Memory(nc, of_tables, "tables_"))
            with ExitStack() as of_xl:
                c.xl = Memory(nc, of_xl).sb("xl_nodes", [P, J, D])
                with_xt(block_gat_tables)
                block_gat_edges(nc, c, io)
                block_experts(nc, c, io, "L0_ffn", NE0, c.edge_table)
                with_xt(block_z)
            block_windows(nc, c, io)
        with ExitStack() as of_xl:
            c.xl = Memory(nc, of_xl).sb("xl_windows", [P, J, D])
            with_xt(block_router)
            block_experts(nc, c, io, "L1_ffn", NE1, None)
        store_x(nc, c, io)


_INS = ['x', 'src', 'dst', 'edge_attr_64', 'L0_gnn_w1', 'L0_gnn_b1', 'L0_gnn_w2', 'L0_gnn_b2', 'L0_gnn_gcn_w',
        'L0_gnn_gcn_b', 'L0_ffn_W_gat', 'L0_ffn_att_src', 'L0_ffn_att_dst', 'L0_ffn_b_gat', 'L0_ffn_ln_gamma',
        'L0_ffn_ln_beta', 'L0_ffn_W1', 'L0_ffn_b1', 'L0_ffn_W2', 'L0_ffn_b2', 'L0_ffn_edge_index', 'L1_gnn_W',
        'L1_gnn_A', 'L1_ffn_gamma', 'L1_ffn_beta', 'L1_ffn_Wr', 'L1_ffn_br', 'L1_ffn_W1', 'L1_ffn_b1', 'L1_ffn_W2',
        'L1_ffn_b2']


def kernel(**inputs):
    import numpy as _np
    import concourse.bacc as _bacc
    from concourse import mybir as _mybir
    from concourse.bass_utils import run_bass_kernel_spmd as _run

    nc = _bacc.Bacc("TRN2", target_bir_lowering=False, num_devices=1)
    arrays, io = {}, {}
    for name in _INS:
        a = _np.ascontiguousarray(inputs[name])
        arrays[f"in_{name}_dram"] = a
        io[name] = nc.dram_tensor(f"in_{name}_dram", a.shape, _mybir.dt.from_np(a.dtype), kind="ExternalInput").ap()
    io["out"] = nc.dram_tensor("out_dram", (N, D), F32, kind="ExternalOutput").ap()
    program(nc, io)
    r = _run(nc, [arrays], core_ids=[0])
    return r.results[0]["out_dram"]
```
